# Optimizing a Trainium2 kernel written in Bass

```python
import numpy as np
import jax
import jax.numpy as jnp

def _softmax(x, axis=-1):
    return jax.nn.softmax(x, axis=axis)
def _gelu(x):
    return jax.nn.gelu(x, approximate=True)
def _silu(x):
    return jax.nn.silu(x)
def _sigmoid(x):
    return jax.nn.sigmoid(x)
def _layernorm(x, axis=-1, eps=1e-5):
    m = jnp.mean(x, axis=axis, keepdims=True)
    v = jnp.var(x, axis=axis, keepdims=True)
    return (x - m) / jnp.sqrt(v + eps)
def _scatter_add(tgt, idx, src, axis=0):
    return tgt.at[idx].add(src)
def _segment_sum(src, seg, n):
    return jax.ops.segment_sum(src, seg, n)

kernel_name = 'mk_adj_resnorm_d2_adj_256_877917'

def setup_inputs(seed: int = 0):
    np.random.seed(seed)
    _w = jnp.asarray
    def _rec_inputs():
        import jax
        import jax.numpy as jnp
        _gk = jax.random.key(seed)
        x = -0.0005207 + 1.001 * jax.random.normal(jax.random.fold_in(_gk, 1), (8, 2048, 256), jnp.float32)
        _w = (1.0 + jnp.arange(2048, dtype=jnp.float32)) ** -0.5
        _w = _w / _w.mean()
        _pij = jnp.clip(0.015625 * _w[:, None] * _w[None, :], 0.0, 1.0)
        _a = jax.random.uniform(jax.random.fold_in(_gk, 2), (2048, 2048)) < _pij
        adj = _a.astype(jnp.int32)
        return x, adj
    x, adj = _rec_inputs()
    def _L0_gnn_setup():
        import jax, jax.numpy as jnp
        import numpy as np
        import math
        CHUNK = 256
        NUM_HEADS = 4
        EPS = 1e-05
        key = jax.random.key(seed)
        ks = jax.random.split(key, 12)
        B, N, F = (4, 2048, 256)
        x = jax.random.normal(ks[0], (B, N, F), dtype=jnp.float32)
        adj_matrix = jax.random.randint(ks[1], (N, N), 0, 2, dtype=jnp.int32)
        s = 1.0 / math.sqrt(F)
        Wq = jax.random.normal(ks[2], (F, F), dtype=jnp.float32) * s
        bq = jnp.zeros((F,), dtype=jnp.float32)
        Wk = jax.random.normal(ks[3], (F, F), dtype=jnp.float32) * s
        bk = jnp.zeros((F,), dtype=jnp.float32)
        Wv = jax.random.normal(ks[4], (F, F), dtype=jnp.float32) * s
        bv = jnp.zeros((F,), dtype=jnp.float32)
        Wo = jax.random.normal(ks[5], (F, F), dtype=jnp.float32) * s
        bo = jnp.zeros((F,), dtype=jnp.float32)
        gamma = jnp.ones((F,), dtype=jnp.float32)
        beta = jnp.zeros((F,), dtype=jnp.float32)
        return {'x': x, 'adj_matrix': adj_matrix, 'Wq': Wq, 'bq': bq, 'Wk': Wk, 'bk': bk, 'Wv': Wv, 'bv': bv, 'Wo': Wo, 'bo': bo, 'gamma': gamma, 'beta': beta}
    _L0_gnn_all = _L0_gnn_setup()
    _L0_gnn_in = {k: v for k, v in _L0_gnn_all.items() if k in ('Wq', 'bq', 'Wk', 'bk', 'Wv', 'bv', 'Wo', 'bo', 'gamma', 'beta', )}
    del _L0_gnn_all

    def _L1_gnn_setup():
        import jax, jax.numpy as jnp
        import numpy as np
        IN_DIM = 256
        OUT_DIM = 64
        NUM_HEADS = 4
        ALPHA = 0.2
        NEG_INF = -9000000000000000.0
        key = jax.random.key(seed)
        k1, k2, k3, k4 = jax.random.split(key, 4)
        B, N = (4, 2048)
        h = jax.random.normal(k1, (B, N, IN_DIM), dtype=jnp.float32)
        adj = jax.random.randint(k2, (N, N), 0, 2, dtype=jnp.int32)
        W = jax.random.normal(k3, (IN_DIM, NUM_HEADS * OUT_DIM), dtype=jnp.float32) * (1.0 / np.sqrt(IN_DIM))
        a = jax.random.normal(k4, (2 * OUT_DIM,), dtype=jnp.float32) * (1.0 / np.sqrt(2 * OUT_DIM))
        return {'h': h, 'adj': adj, 'W': W, 'a': a}
    _L1_gnn_all = _L1_gnn_setup()
    _L1_gnn_in = {k: v for k, v in _L1_gnn_all.items() if k in ('W', 'a', )}
    del _L1_gnn_all

    return {
        "x": x,
        "adj": adj,
        "L0_gnn_Wq": _L0_gnn_in["Wq"],
        "L0_gnn_bq": _L0_gnn_in["bq"],
        "L0_gnn_Wk": _L0_gnn_in["Wk"],
        "L0_gnn_bk": _L0_gnn_in["bk"],
        "L0_gnn_Wv": _L0_gnn_in["Wv"],
        "L0_gnn_bv": _L0_gnn_in["bv"],
        "L0_gnn_Wo": _L0_gnn_in["Wo"],
        "L0_gnn_bo": _L0_gnn_in["bo"],
        "L0_gnn_gamma": _L0_gnn_in["gamma"],
        "L0_gnn_beta": _L0_gnn_in["beta"],
        "L1_gnn_W": _L1_gnn_in["W"],
        "L1_gnn_a": _L1_gnn_in["a"],
    }

def reference(x, adj, L0_gnn_Wq, L0_gnn_bq, L0_gnn_Wk, L0_gnn_bk, L0_gnn_Wv, L0_gnn_bv, L0_gnn_Wo, L0_gnn_bo, L0_gnn_gamma, L0_gnn_beta, L1_gnn_W, L1_gnn_a):
    import jax
    import jax.numpy as jnp
    def _L0_gnn_ref(x, adj_matrix, Wq, bq, Wk, bk, Wv, bv, Wo, bo, gamma, beta):
        import jax, jax.numpy as jnp
        import numpy as np
        import math
        CHUNK = 256
        NUM_HEADS = 4
        EPS = 1e-05
        B, N, Fin = x.shape
        H = NUM_HEADS
        Dout = Wq.shape[0]
        Dh = Dout // H
        Nc = N // CHUNK
        q = (x @ Wq.T + bq).reshape(B, N, H, Dh).transpose(0, 2, 1, 3)
        k = (x @ Wk.T + bk).reshape(B, N, H, Dh).transpose(0, 2, 1, 3)
        v = (x @ Wv.T + bv).reshape(B, N, H, Dh).transpose(0, 2, 1, 3)
        kc = k.reshape(B, H, Nc, CHUNK, Dh)
        vc = v.reshape(B, H, Nc, CHUNK, Dh)
        scores = jnp.einsum('bhnd,bhjcd->bhnjc', q, kc) / jnp.sqrt(jnp.asarray(Dh, dtype=q.dtype))
        scores = jnp.clip(scores, -10.0, 10.0)
        mask = adj_matrix.reshape(N, Nc, CHUNK)[None, None]
        scores = jnp.where(mask == 0, jnp.asarray(-10.0, scores.dtype), scores)
        attn = jax.nn.softmax(scores, axis=-1)
        ctx = jnp.einsum('bhnjc,bhjcd->bhnd', attn, vc)
        ctx = ctx.transpose(0, 2, 1, 3).reshape(B, N, Dout)
        out = ctx @ Wo.T + bo
        out = out + x
        mu = jnp.mean(out, axis=-1, keepdims=True)
        var = jnp.mean(jnp.square(out - mu), axis=-1, keepdims=True)
        out = (out - mu) * jax.lax.rsqrt(var + EPS) * gamma + beta
        return out

    def _L1_gnn_ref(h, adj, W, a):
        import jax, jax.numpy as jnp
        import numpy as np
        IN_DIM = 256
        OUT_DIM = 64
        NUM_HEADS = 4
        ALPHA = 0.2
        NEG_INF = -9000000000000000.0
        B, N, _ = h.shape
        H, D = (NUM_HEADS, OUT_DIM)
        q = (h @ W).reshape(B, N, H, D)
        a_src, a_dst = (a[:D], a[D:])
        e_src = jnp.einsum('bnhd,d->bnh', q, a_src)
        e_dst = jnp.einsum('bnhd,d->bnh', q, a_dst)
        e = e_src[:, :, None, :] + e_dst[:, None, :, :]
        e = jnp.where(e >= 0, e, ALPHA * e)
        mask = (adj > 0)[None, :, :, None]
        e = jnp.where(mask, e, NEG_INF)
        attn = jax.nn.softmax(e, axis=2)
        h_prime = jnp.einsum('bijh,bjhd->bihd', attn, q)
        return jax.nn.elu(h_prime.reshape(B, N, H * D))

    x = _layernorm(x + _L0_gnn_ref(x, adj, L0_gnn_Wq, L0_gnn_bq, L0_gnn_Wk, L0_gnn_bk, L0_gnn_Wv, L0_gnn_bv, L0_gnn_Wo, L0_gnn_bo, L0_gnn_gamma, L0_gnn_beta), axis=-1)
    x = _layernorm(x + _L1_gnn_ref(x, adj, L1_gnn_W, L1_gnn_a), axis=-1)
    return x


_drawn_inputs = setup_inputs


def setup_inputs(seed=0):
    import zlib

    import numpy as np

    out = dict(_drawn_inputs(seed))
    spreads = {'L0_gnn_bq': (0.0, 0.313),
     'L0_gnn_bk': (0.0, 2.0),
     'L0_gnn_bv': (0.0, 0.1),
     'L0_gnn_bo': (0.0, 0.1),
     'L0_gnn_gamma': (1.0, 0.2),
     'L0_gnn_beta': (0.0, 0.1)}
    factors = {}
    for name, (base, spread) in spreads.items():
        noise = np.random.default_rng([zlib.crc32(name.encode()), seed]).standard_normal(out[name].shape)
        drawn = base * np.exp(spread * noise) if base else spread * noise
        out[name] = jnp.asarray(drawn.astype(out[name].dtype))
    for name, factor in factors.items():
        out[name] = (out[name] * factor).astype(out[name].dtype)
    return out
```

```python
from contextlib import ExitStack

import concourse.bass as bass
from concourse import mybir

ALU = mybir.AluOpType
ACT = mybir.ActivationFunctionType
AXIS_FREE = mybir.AxisListType.X
F32 = mybir.dt.float32
F16 = mybir.dt.float16
BF16 = mybir.dt.bfloat16
I32 = mybir.dt.int32
I8 = mybir.dt.int8
U8 = mybir.dt.uint8
REDUCE_MAX = bass.bass_isa.ReduceOp.max

P = 128
F = 256
FC = F // P
H = 4
DH = F // H
DV = DH + 1
PAIRS = H // 2
CHUNK = 256
KT = CHUNK // P
QG = 512
QT = QG // P
CLIP = 10.0
SCALE = float(DH) ** -0.5
RAW_CLIP = CLIP / SCALE
EPS = 1e-5
SLOPE = 0.2
MAX_EXPONENT = 80.0
DMA = 16


def allocators(nc, ctx, phase):
    def sb(name, shape, dt):
        return ctx.enter_context(nc.sbuf_tensor(f"{phase}_{name}", shape, dt))

    def ps(name, shape, dt):
        return ctx.enter_context(nc.psum_tensor(f"{phase}_{name}", shape, dt))

    def sem(name):
        return ctx.enter_context(nc.semaphore(f"{phase}_{name}"))

    return sb, ps, sem


def hold(engine, semaphore, value, held):
    engine.wait_ge(semaphore, value)
    engine.sem_inc(held, 1)


class Scratch:

    def __init__(self, nc, B, N):
        NT = N // P
        self.q = nc.dram_tensor("q_split", [B, PAIRS, 2, P, N], F16, kind="Internal")
        self.k = nc.dram_tensor("k_split", [B, PAIRS, 2, P, N], F16, kind="Internal")
        self.v = nc.dram_tensor("v_ones", [B, H, P, NT * DV], F32, kind="Internal")
        self.ctx = nc.dram_tensor("context", [B, N, F], F32, kind="Internal")
        self.x1 = nc.dram_tensor("x_layer1", [B, N, F], F32, kind="Internal")
        self.v1 = nc.dram_tensor("v1_ones", [B, H, P, NT * DV], F32, kind="Internal")
        self.e = nc.dram_tensor("edge_terms", [B, P, NT * 2 * H], F32, kind="Internal")
        self.ratio = nc.dram_tensor("ratio_rows", [B * H * NT, P], F32, kind="Internal")
        self.dst = nc.dram_tensor("dst_factors", [B, H, P, 3 * NT], F32, kind="Internal")


class Constants:

    def __init__(self, nc, ctx, N):
        NT = N // P

        sb, ps, sem = allocators(nc, ctx, "const")
        self.clip_mask = sb("clip_mask", [P, NT, N], I8)
        self.edge_mask = sb("edge_mask", [P, NT, N], U8)
        self.ident = sb("ident", [P, P], F32)
        self.ident16 = sb("ident16", [P, P], BF16)
        self.wqT = sb("wqT", [P, FC, F], F32)
        self.wkT = sb("wkT", [P, FC, F], F32)
        self.wvT = sb("wvT", [P, FC, F], F32)
        self.woT = sb("woT", [P, FC, F], F32)
        self.w1 = sb("w1", [P, FC, F + 2 * H], F32)
        self.bq = sb("bq", [P, PAIRS], F32)
        self.bk = sb("bk", [P, PAIRS], F32)
        self.bv = sb("bv", [P, F], F32)
        self.bo = sb("bo", [P, F], F32)
        self.gamma = sb("gamma", [P, F], F32)
        self.beta = sb("beta", [P, F], F32)
        self.minus_half = sb("minus_half", [P, 16], F32)
        self.eps = sb("eps", [P, 16], F32)


def prepare_weights(nc, c, w):
    with ExitStack() as ctx:
        sb, ps, sem = allocators(nc, ctx, "weights")
        raw = sb("raw_weights", [P, 4, FC, F], F32)
        a_rows = sb("a_rows", [P, 2, DH], F32)
        product = sb("product", [P, 2, FC * H, DH], F32)
        turned = [ps(f"turned{i}", [P, FC, F], F32) for i in range(4)]
        raw_loaded = sem("raw_loaded")
        w1_loaded = sem("w1_loaded")
        rows_loaded = sem("rows_loaded")
        cleared = sem("cleared")
        ident_ready = sem("ident_ready")
        turned_ready = sem("turned_ready")
        copied = sem("copied")
        product_ready = sem("product_ready")
        sp_held = sem("sp_held")
        block = ctx.enter_context(nc.Block())

        @block.sync
        def _(sp):
            for m, name in enumerate(("Wq", "Wk", "Wv", "Wo")):
                sp.dma_start(raw[:, m], w[name].rearrange("(c p) f -> p c f", p=P)).then_inc(raw_loaded, DMA)
            sp.dma_start(c.w1[:, :, 0:F], w["W"].rearrange("(c p) f -> p c f", p=P)).then_inc(w1_loaded, DMA)
            sp.dma_start(a_rows[:].rearrange("p s d -> p (s d)"), w["a"].partition_broadcast(P)).then_inc(w1_loaded, DMA)
            for dst, name in ((c.bv, "bv"), (c.bo, "bo"), (c.gamma, "gamma"), (c.beta, "beta")):
                sp.dma_start(dst[:], w[name].partition_broadcast(P)).then_inc(rows_loaded, DMA)
            with nc.allow_non_contiguous_dma(reason="two small bias columns"):
                for dst, name in ((c.bq, "bq"), (c.bk, "bk")):
                    sp.dma_start(dst[:], w[name].rearrange("(c p) -> p c", p=P)).then_inc(rows_loaded, DMA)
            hold(sp, rows_loaded, 6 * DMA, sp_held)

        @block.gpsimd
        def _(pool):
            nc.gpsimd.memset(c.minus_half[:], -0.5)
            nc.gpsimd.memset(c.eps[:], EPS)
            nc.gpsimd.memset(c.ident16[:], 0.0)
            nc.gpsimd.memset(c.ident[:], 0.0).then_inc(cleared, 1)
            pool.wait_ge(cleared, 1)
            nc.gpsimd.affine_select(out=c.ident16[:], in_=c.ident16[:], compare_op=ALU.not_equal, fill=1.0,
                                    base=0, pattern=[[-1, P]], channel_multiplier=1)
            nc.gpsimd.affine_select(out=c.ident[:], in_=c.ident[:], compare_op=ALU.not_equal, fill=1.0,
                                    base=0, pattern=[[-1, P]], channel_multiplier=1).then_inc(ident_ready, 1)

        @block.tensor
        def _(pe):
            pe.wait_ge(raw_loaded, 4 * DMA)
            pe.wait_ge(ident_ready, 1)
            for m in range(4):
                for oc in range(FC):
                    for fc in range(FC):
                        mm = nc.tensor.transpose(turned[m][:, fc, oc * P:(oc + 1) * P],
                                                 raw[:, m, oc, fc * P:(fc + 1) * P], c.ident[:])
                mm.then_inc(turned_ready, 1)

        @block.scalar
        def _(act):
            for m, dst in enumerate((c.wqT, c.wkT, c.wvT, c.woT)):
                act.wait_ge(turned_ready, m + 1)
                nc.scalar.copy(dst[:], turned[m][:]).then_inc(copied, 1)
            act.wait_ge(copied, 4)

        @block.vector
        def _(dve):
            dve.wait_ge(w1_loaded, 2 * DMA)
            heads = c.w1[:, :, 0:F].rearrange("p c (h d) -> p c h d", h=H)
            for s in range(2):
                for fc in range(FC):
                    last = nc.vector.tensor_tensor(
                        product[:, s, fc * H:(fc + 1) * H, :], heads[:, fc],
                        a_rows[:, s:s + 1, :].to_broadcast([P, H, DH]), ALU.mult)
            last.then_inc(product_ready, 1)
            dve.wait_ge(product_ready, 1)
            for s in range(2):
                for fc in range(FC):
                    nc.vector.tensor_reduce(c.w1[:, fc, F + s * H:F + (s + 1) * H],
                                            product[:, s, fc * H:(fc + 1) * H, :], AXIS_FREE,
                                            ALU.add).then_inc(product_ready, 1)
            dve.wait_ge(product_ready, 1 + 2 * FC)


def project_layer0(nc, c, s, x, adj, B, N):
    NT = N // P
    STEP = 512
    TT = STEP // P
    ITERATIONS = B * N // (2 * STEP)
    ROWS = NT // ITERATIONS
    assert ROWS * ITERATIONS == NT
    HALF = 8
    HALVES = NT // HALF
    x_steps = x.rearrange("b n f -> (b n) f").rearrange("(i t p) f -> i p t f", p=P, t=TT)
    adj_rows = adj.rearrange("(i p) j -> i p j", p=P)
    STEPS = N // STEP
    assert STEPS % 2 == 0
    with ExitStack() as ctx:
        sb, ps, sem = allocators(nc, ctx, "project")
        x_in = [sb(f"x_in{i}", [P, TT, F], F32) for i in range(2)]
        xT = [sb(f"xT{i}", [P, FC, STEP], F32) for i in range(2)]
        split = [[sb(f"split{i}_{m}", [P, 2, STEP], F16) for m in range(2 * PAIRS)] for i in range(2)]
        v_out = [sb(f"v_out{i}", [P, H, TT, DV], F32) for i in range(2)]
        adj_in = sb("adj_in", [P, N], I32)
        is_zero = sb("is_zero", [P, N], BF16)
        is_edge = sb("is_edge", [P, N], BF16)
        xT_ps = ps("xT_ps", [P, FC, STEP], F32)
        qk_ps = [ps(f"qk_ps{i}", [P, STEP], F32) for i in range(2)]
        v_ps = [ps(f"v_ps{i}", [P, 2, F], F32) for i in range(2)]
        mask_ps = [ps(f"mask_ps{i}", [P, HALF, P], BF16) for i in range(2)]

        x_loaded = [sem(f"x_loaded{i}") for i in range(2)]
        x_turned = sem("x_turned")
        xT_ready = sem("xT_ready")
        qk_ready = sem("qk_ready")
        high_ready = sem("high_ready")
        low_ready = sem("low_ready")
        v_ready = sem("v_ready")
        v_copied = sem("v_copied")
        ones_ready = sem("ones_ready")
        split_stored = [sem(f"split_stored{i}") for i in range(2)]
        v_stored = [sem(f"v_stored{i}") for i in range(2)]
        adj_loaded = sem("adj_loaded")
        adj_coded = sem("adj_coded")
        mask_turned = sem("mask_turned")
        mask_ready = sem("mask_ready")
        sp_held = sem("sp_held")
        block = ctx.enter_context(nc.Block())
        codes = (is_zero, is_edge)
        turns = {q * 4 // (ROWS * HALVES): (q // HALVES, q % HALVES) for q in range(ROWS * HALVES)}
        assert len(turns) == ROWS * HALVES

        @block.sync
        def _(sp):
            def load_x(b, st):
                i = st % 2
                hold(sp, x_turned, STEPS * b + st - 1, sp_held)
                at = x_steps[bass.ds(STEPS * b + st, 1)].rearrange("o p t f -> (o p) t f")
                sp.dma_start(x_in[i][:], at).then_inc(x_loaded[i], DMA)

            def batch(b, last):
                for st in range(STEPS):
                    i = st % 2
                    if not (last and st == STEPS - 1):
                        load_x(b, st + 1)
                    if i == 0:
                        for r in range(ROWS):
                            row = ROWS * (STEPS // 2 * b + st // 2) + r
                            hold(sp, adj_coded, row, sp_held)
                            sp.dma_start(adj_in[:], adj_rows[bass.ds(row, 1)].rearrange("o p j -> (o p) j")
                                         ).then_inc(adj_loaded, DMA)
                    for m in range(2 * PAIRS):
                        hold(sp, low_ready, 2 * PAIRS * (STEPS * b + st) + m + 1, sp_held)
                        dst = (s.q, s.k)[m // PAIRS][bass.ds(b, 1), m % PAIRS, :, :, st * STEP:(st + 1) * STEP]
                        sp.dma_start(dst.rearrange("o s p w -> p (o s) w"), split[i][m][:]
                                     ).then_inc(split_stored[i], DMA)
                    hold(sp, v_copied, 2 * (STEPS * b + st) + 2, sp_held)
                    dst = s.v[bass.ds(b, 1), :, :, st * TT * DV:(st + 1) * TT * DV]
                    sp.dma_start(dst.rearrange("o h p w -> p (o h) w"), v_out[i][:].rearrange("p h t d -> p h (t d)")
                                 ).then_inc(v_stored[i], DMA)

            first = x_steps[0:1].rearrange("o p t f -> (o p) t f")
            sp.dma_start(x_in[0][:], first).then_inc(x_loaded[0], DMA)
            if B > 1:
                with sp.Fori(0, B - 1) as b:
                    batch(b, last=False)
            batch(B - 1, last=True)
            for i in range(2):
                hold(sp, split_stored[i], ITERATIONS * 2 * PAIRS * DMA, sp_held)
                hold(sp, v_stored[i], ITERATIONS * DMA, sp_held)

        @block.gpsimd
        def _(pool):
            for i in range(2):
                last = nc.gpsimd.memset(v_out[i][:, :, :, DH:DV], 1.0)
            last.then_inc(ones_ready, 1)

        @block.tensor
        def _(pe):
            def turn_masks(n, r, half):
                pe.wait_ge(adj_coded, ROWS * n + r + 1)
                pe.wait_ge(mask_ready, 2 * (HALVES * (ROWS * n + r) + half))
                for m in range(2):
                    for j in range(HALF):
                        col = (half * HALF + j) * P
                        mm = nc.tensor.transpose(mask_ps[m][:, j, :], codes[m][:, col:col + P], c.ident16[:])
                mm.then_inc(mask_turned, 1)

            with pe.Fori(0, ITERATIONS) as n:
                for i in range(2):
                    pe.wait_ge(x_loaded[i], DMA * (n + 1))
                    pe.wait_ge(xT_ready, 2 * n + i)
                    for fc in range(FC):
                        for t in range(TT):
                            mm = nc.tensor.transpose(xT_ps[:, fc, t * P:(t + 1) * P],
                                                     x_in[i][:, t, fc * P:(fc + 1) * P], c.ident[:])
                    mm.then_inc(x_turned, 1)
                    pe.wait_ge(xT_ready, 2 * n + i + 1)
                    for m in range(2 * PAIRS):
                        w = (c.wqT, c.wkT)[m // PAIRS]
                        pair = m % PAIRS
                        item = 2 * PAIRS * i + m
                        if item >= 2:
                            pe.wait_ge(low_ready, 4 * PAIRS * n + item - 1)
                        else:
                            pe.wait_ge(low_ready, 4 * PAIRS * n)
                        for fc in range(FC):
                            mm = nc.tensor.matmul(qk_ps[m % 2][:], w[:, fc, pair * P:(pair + 1) * P], xT[i][:, fc, :],
                                                  start=fc == 0, stop=fc == FC - 1)
                        mm.then_inc(qk_ready, 1)
                        if m % 2 and 2 * i + m // 2 in turns:
                            turn_masks(n, *turns[2 * i + m // 2])
                    for t2 in range(2):
                        pe.wait_ge(v_copied, 4 * n + 2 * i)
                        for t in range(2):
                            tok = (2 * t2 + t) * P
                            for fc in range(FC):
                                mm = nc.tensor.matmul(v_ps[t2][:, t, :], xT[i][:, fc, tok:tok + P], c.wvT[:, fc, :],
                                                      start=fc == 0, stop=fc == FC - 1)
                        mm.then_inc(v_ready, 1)

        @block.scalar
        def _(act):
            with act.Fori(0, ITERATIONS) as n:
                for i in range(2):
                    act.wait_ge(x_turned, 2 * n + i + 1)
                    act.wait_ge(v_ready, 4 * n)
                    nc.scalar.copy(xT[i][:], xT_ps[:]).then_inc(xT_ready, 1)
                    for m in range(2 * PAIRS):
                        act.wait_ge(qk_ready, 4 * PAIRS * n + 2 * PAIRS * i + m + 1)
                        if m == 0:
                            act.wait_ge(split_stored[i], 2 * PAIRS * DMA * n)
                        nc.scalar.activation(split[i][m][:, 0, :], qk_ps[m % 2][:], ACT.Identity,
                                             bias=(c.bq, c.bk)[m // PAIRS][:, m % PAIRS:m % PAIRS + 1],
                                             ).then_inc(high_ready, 1)

        @block.vector
        def _(dve):
            def code_row(row):
                dve.wait_ge(adj_loaded, DMA * (row + 1))
                dve.wait_ge(mask_turned, HALVES * row)
                nc.vector.tensor_scalar(is_zero[:], adj_in[:], 0.0, -2 * RAW_CLIP, ALU.is_equal, ALU.mult)
                nc.vector.tensor_scalar(is_edge[:], adj_in[:], 0.0, None, ALU.is_gt).then_inc(adj_coded, 1)

            def keep_masks(row, half):
                dve.wait_ge(mask_turned, HALVES * row + half + 1)
                for m, value in ((0, RAW_CLIP), (1, 0.0)):
                    mask = (c.clip_mask, c.edge_mask)[m]
                    nc.vector.tensor_scalar(mask[:, half * HALF:(half + 1) * HALF, bass.ds(row * P, P)],
                                            mask_ps[m][:], value, None, ALU.add).then_inc(mask_ready, 1)

            dve.wait_ge(ones_ready, 1)
            with dve.Fori(0, ITERATIONS) as n:
                for i in range(2):
                    for m in range(2 * PAIRS):
                        turn = turns.get(2 * i + m // 2)
                        if m % 2 == 0 and turn and turn[1] == 0:
                            code_row(ROWS * n + turn[0])
                        dve.wait_ge(high_ready, 2 * PAIRS * (2 * n + i) + m + 1)
                        nc.vector.scalar_tensor_tensor(
                            out=split[i][m][:, 1, :], in0=qk_ps[m % 2][:],
                            scalar=(c.bq, c.bk)[m // PAIRS][:, m % PAIRS:m % PAIRS + 1],
                            in1=split[i][m][:, 0, :], op0=ALU.add, op1=ALU.subtract).then_inc(low_ready, 1)
                        if m % 2 and turn:
                            keep_masks(ROWS * n + turn[0], turn[1])
                    dve.wait_ge(v_stored[i], DMA * n)
                    for t2 in range(2):
                        dve.wait_ge(v_ready, 2 * (2 * n + i) + t2 + 1)
                        nc.vector.tensor_tensor(
                            v_out[i][:, :, 2 * t2:2 * t2 + 2, 0:DH].rearrange("p h t d -> p t h d"),
                            v_ps[t2][:].rearrange("p t (h d) -> p t h d", h=H),
                            c.bv[:].rearrange("p (o h d) -> p o h d", o=1, h=H).to_broadcast([P, 2, H, DH]),
                            ALU.add).then_inc(v_copied, 1)


def attend_layer0(nc, c, s, B, N):
    NQ, NCH = N // QG, N // CHUNK
    HEAD_UNITS = NQ * NCH
    BODY_UNITS = 2 * HEAD_UNITS
    PAIR_COUNT = B * PAIRS
    UNITS = BODY_UNITS * PAIR_COUNT
    GROUPS = 2 * NQ
    NT = N // P
    S_RING, P_RING, O_RING = 2, 8, 4
    AHEAD = 3
    assert BODY_UNITS % P_RING == 0 and NCH % O_RING == 0 and AHEAD < P_RING
    with ExitStack() as ctx:
        sb, ps, sem = allocators(nc, ctx, "attend0")
        k_split = [sb(f"k_split{i}", [P, N], F16) for i in range(2)]
        q_high = [sb(f"q_high{i}", [P, N], F16) for i in range(2)]
        q_low = [sb(f"q_low{i}", [P, N], F16) for i in range(2)]
        values = [sb(f"values{i}", [P, NT, DV], F32) for i in range(2)]
        probs = [sb(f"probs{i}", [P, KT, QG], F32) for i in range(P_RING)]
        sums = [sb(f"sums{i}", [P, NCH * QT, DV], F32) for i in range(2)]
        inverse = [sb(f"inverse{i}", [P, NCH * QT], F32) for i in range(2)]
        scaled = sb("scaled", [P, NCH * QT, DH], F32)
        context = [sb(f"context{i}", [P, QT, DH], F32) for i in range(2)]
        s_ps = [ps(f"s_ps{i}", [P, KT, QG], F32) for i in range(S_RING)]
        o_ps = [ps(f"o_ps{i}", [P, QT, P], F32) for i in range(O_RING)]

        qk_loaded = [sem(f"qk_loaded{i}") for i in range(2)]
        v_loaded = [sem(f"v_loaded{i}") for i in range(2)]
        scores_ready = sem("scores_ready")
        masked = sem("masked")
        probs_ready = sem("probs_ready")
        probs_free = sem("probs_free")
        summed = sem("summed")
        sums_free = sem("sums_free")
        inverse_ready = sem("inverse_ready")
        group_free = sem("group_free")
        pool_step = sem("pool_step")
        context_ready = sem("context_ready")
        context_stored = [sem(f"context_stored{i}") for i in range(2)]
        sp_held = sem("sp_held")
        block = ctx.enter_context(nc.Block())
        LEVELS = NCH.bit_length() - 1
        assert NCH == 1 << LEVELS and LEVELS >= 1

        def unit(u):
            return u // HEAD_UNITS, u % HEAD_UNITS // NCH, u % NCH

        @block.sync
        def _(sp):
            def load_head(b, h):
                i = h % 2
                head = H * b + h
                bb, hh = (b, h) if h < H else (b + 1, h - H)
                rows = slice(hh % 2 * DH, hh % 2 * DH + DH)
                if not (isinstance(head, int) and head < 2):
                    hold(sp, scores_ready, HEAD_UNITS * (head - 1), sp_held)
                at = [[t[bass.ds(bb, 1), hh // 2, half, rows, :].rearrange("o d n -> (o d) n") for half in range(2)]
                      for t in (s.q, s.k)]
                for half in range(2):
                    place = slice(half * DH, half * DH + DH)
                    sp.dma_start(k_split[i][place, :], at[1][half]).then_inc(qk_loaded[i], DMA)
                    sp.dma_start(q_high[i][place, :], at[0][0]).then_inc(qk_loaded[i], DMA)
                    sp.dma_start(q_low[i][place, :], at[0][1]).then_inc(qk_loaded[i], DMA)
                if not (isinstance(head, int) and head < 2):
                    hold(sp, probs_free, P_RING + HEAD_UNITS * (head - 1), sp_held)
                v_at = s.v[bass.ds(bb, 1), hh, :, :].rearrange("o p w -> (o p) w")
                sp.dma_start(values[i][:].rearrange("p t d -> p (t d)"), v_at).then_inc(v_loaded[i], DMA)

            def store_group(b, h, g):
                hold(sp, context_ready, NQ * (H * b + h) + g + 1, sp_held)
                dst = s.ctx[bass.ds(b, 1), g * QG:(g + 1) * QG, h * DH:(h + 1) * DH]
                sp.dma_start(dst.rearrange("o (t p) d -> p (o t) d", p=P), context[g % 2][:]
                             ).then_inc(context_stored[g % 2], DMA)

            def batch(b, last):
                for h in range(H):
                    for g in range(NQ):
                        if g == 0 and not (last and h == H - 1):
                            load_head(b, h + 1)
                        store_group(b, h, g)

            load_head(0, 0)
            if B > 1:
                with sp.Fori(0, B - 1) as b:
                    batch(b, last=False)
            batch(B - 1, last=True)
            for i in range(2):
                hold(sp, context_stored[i], B * H * NQ // 2 * DMA, sp_held)

        @block.tensor
        def _(pe):
            def scores(it, u):
                if u >= BODY_UNITS:
                    it, u = it + 1, u - BODY_UNITS
                hh, g, j = unit(u)
                if u % HEAD_UNITS == 0:
                    pe.wait_ge(qk_loaded[hh], 6 * DMA * (it + 1))
                if not (isinstance(it, int) and it == 0 and u < S_RING):
                    pe.wait_ge(masked, BODY_UNITS * it + u - S_RING + 1)
                for kt in range(KT):
                    key = (KT * j + kt) * P
                    for half, q in enumerate((q_high, q_low)):
                        mm = nc.tensor.matmul(s_ps[u % S_RING][:, kt, :], k_split[hh][:, key:key + P],
                                              q[hh][:, g * QG:(g + 1) * QG], start=half == 0, stop=half == 1)
                mm.then_inc(scores_ready, 1)

            def products(it, u):
                hh, g, j = unit(u)
                if u % HEAD_UNITS == 0:
                    pe.wait_ge(v_loaded[hh], DMA * (it + 1))
                pe.wait_ge(probs_ready, BODY_UNITS * it + u + 1)
                pe.wait_ge(sums_free, BODY_UNITS * it + u + 1)
                for t in range(QT):
                    for kt in range(KT):
                        mm = nc.tensor.matmul(o_ps[u % O_RING][:, t, 0:DV],
                                              probs[u % P_RING][:, kt, t * P:(t + 1) * P],
                                              values[hh][:, KT * j + kt, :], start=kt == 0, stop=kt == KT - 1)
                mm.then_inc(probs_free, 1)

            pe.sem_inc(probs_free, P_RING)
            for u in range(AHEAD):
                scores(0, u)
            with pe.Fori(0, PAIR_COUNT - 1) as it:
                for u in range(BODY_UNITS):
                    scores(it, u + AHEAD)
                    products(it, u)
            for u in range(BODY_UNITS):
                if u + AHEAD < BODY_UNITS:
                    scores(PAIR_COUNT - 1, u + AHEAD)
                products(PAIR_COUNT - 1, u)

        @block.scalar
        def _(act):
            def exponentials(it, u):
                if u >= BODY_UNITS:
                    it, u = it + 1, u - BODY_UNITS
                act.wait_ge(masked, BODY_UNITS * it + u + 1)
                nc.scalar.activation(probs[u % P_RING][:], probs[u % P_RING][:], ACT.Exp, scale=SCALE
                                     ).then_inc(probs_ready, 1)

            def copy_sums(it, u):
                g = u // NCH
                if u % NCH == 0:
                    act.wait_ge(group_free, GROUPS * it + g + 1)
                act.wait_ge(probs_free, P_RING + BODY_UNITS * it + u + 1)
                nc.scalar.copy(sums[g % 2][:, u % NCH * QT:(u % NCH + 1) * QT, :], o_ps[u % O_RING][:, :, 0:DV]
                               ).then_inc(sums_free, 1)

            act.sem_inc(sums_free, O_RING)
            for u in range(AHEAD):
                exponentials(0, u)
            with act.Fori(0, PAIR_COUNT - 1) as it:
                for u in range(BODY_UNITS):
                    exponentials(it, u + AHEAD)
                    copy_sums(it, u)
            for u in range(BODY_UNITS):
                if u + AHEAD < BODY_UNITS:
                    exponentials(PAIR_COUNT - 1, u + AHEAD)
                copy_sums(PAIR_COUNT - 1, u)

        @block.vector
        def _(dve):
            LATE = NCH + AHEAD + 2

            def mask(it, u):
                if u >= BODY_UNITS:
                    it, u = it + 1, u - BODY_UNITS
                hh, g, j = unit(u)
                dve.wait_ge(scores_ready, BODY_UNITS * it + u + 1)
                dve.wait_ge(probs_free, BODY_UNITS * it + u + 1)
                nc.vector.scalar_tensor_tensor(
                    out=probs[u % P_RING][:], in0=s_ps[u % S_RING][:], scalar=-RAW_CLIP,
                    in1=c.clip_mask[:, KT * j:KT * (j + 1), g * QG:(g + 1) * QG],
                    op0=ALU.max, op1=ALU.min).then_inc(masked, 1)

            def invert(it, g):
                dve.wait_ge(sums_free, O_RING + BODY_UNITS * it + NCH * (g + 1))
                nc.vector.reciprocal(inverse[g % 2][:], sums[g % 2][:, :, DH]).then_inc(inverse_ready, 1)

            for u in range(LATE):
                mask(0, u)
            with dve.Fori(0, PAIR_COUNT - 1) as it:
                for g in range(GROUPS):
                    invert(it, g)
                    for u in range(NCH):
                        mask(it, NCH * g + LATE + u)
            for g in range(GROUPS):
                invert(PAIR_COUNT - 1, g)
                for u in range(NCH):
                    if NCH * g + LATE + u < BODY_UNITS:
                        mask(PAIR_COUNT - 1, NCH * g + LATE + u)

        @block.gpsimd
        def _(pool):
            pool.sem_inc(group_free, 2)
            with pool.Fori(0, PAIR_COUNT) as it:
                for g in range(GROUPS):
                    count = GROUPS * it + g
                    i = g % 2
                    pool.wait_ge(inverse_ready, count + 1)
                    pool.wait_ge(context_ready, count)
                    nc.gpsimd.tensor_tensor(scaled[:], sums[i][:, :, 0:DH],
                                            inverse[i][:].unsqueeze(2).to_broadcast([P, NCH * QT, DH]), ALU.mult
                                            ).then_inc(group_free, 1)
                    pool.wait_ge(group_free, 2 + count + 1)
                    width = NCH * QT
                    for level in range(LEVELS - 1):
                        width //= 2
                        nc.gpsimd.tensor_tensor(scaled[:, 0:width, :], scaled[:, 0:width, :],
                                                scaled[:, width:2 * width, :], ALU.add).then_inc(pool_step, 1)
                        pool.wait_ge(pool_step, (LEVELS - 1) * count + level + 1)
                    pool.wait_ge(context_stored[i], DMA * (NQ * it + g // 2))
                    nc.gpsimd.tensor_tensor(context[i][:], scaled[:, 0:QT, :], scaled[:, QT:2 * QT, :], ALU.add
                                            ).then_inc(context_ready, 1)


def finish_layer0(nc, c, s, x, B, N):
    NT = N // P
    TILES = NT // 2
    CHUNKS = TILES // 2
    V1 = F + 2 * H
    with ExitStack() as ctx:
        sb, ps, sem = allocators(nc, ctx, "finish0")
        context = [sb(f"context_in{i}", [P, TILES, F], F32) for i in range(2)]
        x_in = [sb(f"x_res{i}", [P, TILES, F], F32) for i in range(2)]
        x_out = [sb(f"x_out{i}", [P, TILES, F], F32) for i in range(2)]
        contextT = [sb(f"contextT{i}", [P, FC, 2, P], F32) for i in range(2)]
        outT = [sb(f"outT{i}", [P, CHUNKS, FC, 2, P], F32) for i in range(2)]
        v1 = [sb(f"v1_{i}", [P, H, TILES, DV], F32) for i in range(2)]
        edge = [sb(f"edge{i}", [P, TILES, 2 * H], F32) for i in range(2)]
        stats = sb("stats", [P, TILES, 6], F32)
        moments = sb("moments", [P, 2, TILES, 2], F32)
        var_eps = sb("var_eps", [P, 2, TILES], F32)
        rstd = sb("rstd", [P, 2, TILES], F32)
        turn_ps = [ps(f"turn_ps{i}", [P, FC, 2, P], F32) for i in range(2)]
        o_ps = [ps(f"proj_ps{i}", [P, 2, F], F32) for i in range(2)]
        out_turn_ps = [ps(f"out_turn_ps{i}", [P, FC, 2, P], F32) for i in range(2)]
        v1_ps = [ps(f"v1_ps{i}", [P, 512], F32) for i in range(2)]

        loaded = [sem(f"loaded{i}") for i in range(2)]
        turned = sem("turned")
        turned_copied = sem("turned_copied")
        projected = sem("projected")
        biased = sem("biased")
        added = sem("added")
        dve_step = sem("dve_step")
        moments_ready = sem("moments_ready")
        pool_step = sem("pool_step")
        held = sem("held")
        rstd_ready = sem("rstd_ready")
        out_ready = sem("out_ready")
        out_turned = sem("out_turned")
        out_copied = sem("out_copied")
        v1_projected = sem("v1_projected")
        v1_ready = sem("v1_ready")
        ones_ready = sem("ones_ready")
        stored = [sem(f"stored{i}") for i in range(2)]
        sp_held = sem("sp_held")
        block = ctx.enter_context(nc.Block())
        STORES = 3

        @block.sync
        def _(sp):
            def load(b, i):
                if i == 2:
                    b, i = b + 1, 0
                if not (isinstance(b, int) and b == 0):
                    hold(sp, stored[i], STORES * DMA * b, sp_held)
                    hold(sp, turned, CHUNKS * (2 * b + i - 1), sp_held)
                rows = slice(i * TILES * P, (i + 1) * TILES * P)
                for dst, src in ((context[i], s.ctx), (x_in[i], x)):
                    at = src[bass.ds(b, 1), rows, :].rearrange("o (t p) f -> p (o t) f", p=P)
                    sp.dma_start(dst[:], at).then_inc(loaded[i], DMA)

            def store(b, i):
                half = 2 * b + i
                rows = slice(i * TILES * P, (i + 1) * TILES * P)
                hold(sp, out_ready, half + 1, sp_held)
                at = s.x1[bass.ds(b, 1), rows, :].rearrange("o (t p) f -> p (o t) f", p=P)
                sp.dma_start(at, x_out[i][:]).then_inc(stored[i], DMA)
                hold(sp, v1_ready, TILES * (half + 1), sp_held)
                at = s.v1[bass.ds(b, 1), :, :, i * TILES * DV:(i + 1) * TILES * DV]
                sp.dma_start(at.rearrange("o h p w -> p (o h) w"), v1[i][:].rearrange("p h t d -> p h (t d)")
                             ).then_inc(stored[i], DMA)
                at = s.e[bass.ds(b, 1), :, i * TILES * 2 * H:(i + 1) * TILES * 2 * H]
                sp.dma_start(at.rearrange("o p w -> (o p) w"), edge[i][:].rearrange("p t e -> p (t e)")
                             ).then_inc(stored[i], DMA)

            load(0, 0)
            load(0, 1)
            if B > 1:
                with sp.Fori(0, B - 1) as b:
                    for i in range(2):
                        store(b, i)
                        load(b + 1, i)
            for i in range(2):
                store(B - 1, i)
            for i in range(2):
                hold(sp, stored[i], STORES * DMA * B, sp_held)

        @block.gpsimd
        def _(pool):
            last = None
            for i in range(2):
                last = nc.gpsimd.memset(v1[i][:, :, :, DH:DV], 1.0)
            last.then_inc(ones_ready, 1)
            with pool.Fori(0, B) as b:
                for i in range(2):
                    half = 2 * b + i
                    pool.wait_ge(loaded[i], 2 * DMA * (b + 1))
                    nc.gpsimd.tensor_tensor(x_out[i][:], x_in[i][:],
                                            c.beta[:].unsqueeze(1).to_broadcast([P, TILES, F]), ALU.add
                                            ).then_inc(pool_step, 1)
                    pool.wait_ge(pool_step, 3 * half + 1)
                    nc.gpsimd.tensor_tensor(x_in[i][:], x_in[i][:],
                                            c.bo[:].unsqueeze(1).to_broadcast([P, TILES, F]), ALU.add
                                            ).then_inc(biased, 1)
                    for norm in range(2):
                        pool.wait_ge(moments_ready, 2 * half + norm + 1)
                        nc.gpsimd.tensor_tensor(var_eps[:, norm], moments[:, norm, :, 1], c.eps[:, 0:TILES], ALU.add
                                                ).then_inc(pool_step, 1)
                        pool.wait_ge(pool_step, 3 * half + norm + 2)
                        nc.gpsimd.tensor_tensor(rstd[:, norm], var_eps[:, norm], c.minus_half[:, 0:TILES], ALU.pow
                                                ).then_inc(rstd_ready, 1)

        @block.tensor
        def _(pe):
            def front(b, i):
                half = 2 * b + i
                pe.wait_ge(loaded[i], 2 * DMA * (b + 1))

                def turn(k):
                    if k >= 2:
                        pe.wait_ge(turned_copied, CHUNKS * half + k - 1)
                    for fc in range(FC):
                        for t in range(2):
                            mm = nc.tensor.transpose(turn_ps[k % 2][:, fc, t, :],
                                                     context[i][:, 2 * k + t, fc * P:(fc + 1) * P], c.ident[:])
                    mm.then_inc(turned, 1)

                def project(k):
                    pe.wait_ge(turned_copied, CHUNKS * half + k + 1)
                    pe.wait_ge(added, CHUNKS * half + (k - 1 if k >= 2 else 0))
                    for t in range(2):
                        for fc in range(FC):
                            mm = nc.tensor.matmul(o_ps[k % 2][:, t, :], contextT[k % 2][:, fc, t, :],
                                                  c.woT[:, fc, :], start=fc == 0, stop=fc == FC - 1)
                    mm.then_inc(projected, 1)

                turn(0)
                for k in range(CHUNKS):
                    if k + 1 < CHUNKS:
                        turn(k + 1)
                    project(k)

            def back(b, i):
                half = 2 * b + i
                pe.wait_ge(out_ready, half + 1)
                for k in range(CHUNKS):
                    if k >= 2:
                        pe.wait_ge(out_copied, CHUNKS * half + k - 1)
                    for fc in range(FC):
                        for t in range(2):
                            mm = nc.tensor.transpose(out_turn_ps[k % 2][:, fc, t, :],
                                                     x_out[i][:, 2 * k + t, fc * P:(fc + 1) * P], c.ident[:])
                    mm.then_inc(out_turned, 1)
                for t in range(TILES):
                    pe.wait_ge(out_copied, CHUNKS * half + t // 2 + 1)
                    pe.wait_ge(v1_ready, TILES * half + (t - 1 if t >= 2 else 0))
                    for fc in range(FC):
                        mm = nc.tensor.matmul(v1_ps[t % 2][:, 0:V1], outT[i][:, t // 2, fc, t % 2, :],
                                              c.w1[:, fc, :], start=fc == 0, stop=fc == FC - 1)
                    mm.then_inc(v1_projected, 1)

            front(0, 0)
            if B > 1:
                with pe.Fori(0, B - 1) as b:
                    front(b, 1)
                    back(b, 0)
                    front(b + 1, 0)
                    back(b, 1)
            front(B - 1, 1)
            back(B - 1, 0)
            back(B - 1, 1)

        @block.scalar
        def _(act):
            def front(b, i):
                half = 2 * b + i
                for k in range(CHUNKS):
                    count = CHUNKS * half + k
                    act.wait_ge(turned, count + 1)
                    if not (isinstance(count, int) and count < 2):
                        act.wait_ge(projected, count - 1)
                    nc.scalar.copy(contextT[k % 2][:], turn_ps[k % 2][:]).then_inc(turned_copied, 1)

            def back(b, i):
                half = 2 * b + i
                for k in range(CHUNKS):
                    act.wait_ge(out_turned, CHUNKS * half + k + 1)
                    nc.scalar.copy(outT[i][:, k], out_turn_ps[k % 2][:]).then_inc(out_copied, 1)
                if not (isinstance(b, int) and b == 0):
                    act.wait_ge(stored[i], STORES * DMA * b)
                for t in range(TILES):
                    act.wait_ge(v1_projected, TILES * half + t + 1)
                    nc.scalar.copy(edge[i][:, t, :], v1_ps[t % 2][:, F:V1])
                    nc.scalar.copy(v1[i][:, :, t, 0:DH], v1_ps[t % 2][:, 0:F].rearrange("p (h d) -> p h d", h=H)
                                   ).then_inc(v1_ready, 1)

            act.wait_ge(ones_ready, 1)
            front(0, 0)
            if B > 1:
                with act.Fori(0, B - 1) as b:
                    front(b, 1)
                    back(b, 0)
                    front(b + 1, 0)
                    back(b, 1)
            front(B - 1, 1)
            back(B - 1, 0)
            back(B - 1, 1)

        @block.vector
        def _(dve):
            with dve.Fori(0, B) as b:
                for i in range(2):
                    half = 2 * b + i
                    X, G = x_in[i], x_out[i]
                    dve.wait_ge(biased, half + 1)
                    for k in range(CHUNKS):
                        dve.wait_ge(projected, CHUNKS * half + k + 1)
                        nc.vector.tensor_tensor(X[:, 2 * k:2 * k + 2, :], o_ps[k % 2][:], X[:, 2 * k:2 * k + 2, :],
                                                ALU.add).then_inc(added, 1)
                    dve.wait_ge(added, CHUNKS * (half + 1))
                    for norm in range(2):
                        source = (X, G)[norm]
                        for t in range(TILES):
                            last = nc.vector.bn_stats(stats[:, t, :], source[:, t, :])
                        last.then_inc(dve_step, 1)
                        hold(dve, dve_step, 4 * half + 1 + 3 * norm, held)
                        for t in range(TILES):
                            last = nc.vector.bn_aggr(moments[:, norm, t, :], stats[:, t, :])
                        last.then_inc(moments_ready, 1)
                        dve.wait_ge(moments_ready, 2 * half + norm + 1)
                        if norm == 0:
                            for t in range(TILES):
                                last = nc.vector.scalar_tensor_tensor(
                                    out=X[:, t, :], in0=X[:, t, :], scalar=moments[:, 0, t, 0:1], in1=c.gamma[:],
                                    op0=ALU.subtract, op1=ALU.mult)
                            last.then_inc(dve_step, 1)
                            dve.wait_ge(dve_step, 4 * half + 2)
                            dve.wait_ge(rstd_ready, 2 * half + 1)
                            for t in range(TILES):
                                last = nc.vector.scalar_tensor_tensor(
                                    out=G[:, t, :], in0=X[:, t, :], scalar=rstd[:, 0, t:t + 1], in1=G[:, t, :],
                                    op0=ALU.mult, op1=ALU.add)
                            last.then_inc(dve_step, 1)
                            dve.wait_ge(dve_step, 4 * half + 3)
                        else:
                            dve.wait_ge(rstd_ready, 2 * half + 2)
                            for t in range(TILES):
                                last = nc.vector.tensor_scalar(G[:, t, :], G[:, t, :], moments[:, 1, t, 0:1],
                                                               rstd[:, 1, t:t + 1], ALU.subtract, ALU.mult)
                            last.then_inc(out_ready, 1)


def prepare_layer1(nc, c, s, B, N, no_edge):
    NT = N // P
    COLS = B * H * NT
    BLOCKS = COLS // P
    MM = 512
    with ExitStack() as ctx:
        sb, ps, sem = allocators(nc, ctx, "prepare1")
        edge = sb("edge_all", [P, B, NT, 2 * H], F32)
        highest = sb("highest", [P, B, H], F32)
        top = sb("top", [P, B, H], F32)
        shifted = sb("shifted", [P, B, H, NT], F32)
        exponent = sb("exponent", [P, B, H, NT], F32)
        ratio = sb("ratio", [P, COLS], F32)
        factors = sb("factors", [P, B, H, 3, NT], F32)
        rows = sb("ratio_rows_sb", [P, BLOCKS, P], F32)
        ones = sb("ones16", [P, P], BF16)
        mask16 = [sb(f"mask16_{i}", [P, N], BF16) for i in range(2)]
        rows_ps = ps("rows_ps", [P, BLOCKS, P], F32)
        degree = ps("degree", [P, N], F32)
        loaded = sem("edge_loaded")
        dve_step = sem("dve_step")
        top_ready = sem("top_ready")
        shifted_ready = sem("shifted_ready")
        exp_ready = sem("exp_ready")
        ones_ready = sem("ones_ready")
        mask_ready = sem("mask_ready")
        mask_used = sem("mask_used")
        rows_ready = sem("rows_ready")
        rows_copied = sem("rows_copied")
        negated = sem("negated")
        stored = sem("stored")
        sp_held = sem("sp_held")
        block = ctx.enter_context(nc.Block())

        @block.sync
        def _(sp):
            sp.dma_start(edge[:].rearrange("p b t e -> p b (t e)"), s.e[:, :, :].rearrange("b p w -> p b w")
                         ).then_inc(loaded, DMA)
            hold(sp, negated, 1, sp_held)
            hold(sp, exp_ready, 3, sp_held)
            for b in range(B):
                sp.dma_start(s.dst[b].rearrange("h p w -> p h w"), factors[:, b].rearrange("p h k t -> p h (k t)")
                             ).then_inc(stored, DMA)
            hold(sp, rows_copied, 1, sp_held)
            sp.dma_start(s.ratio[:, :].rearrange("(k p) w -> p k w", p=P), rows[:]).then_inc(stored, DMA)
            hold(sp, stored, (B + 1) * DMA, sp_held)

        @block.gpsimd
        def _(pool):
            nc.gpsimd.memset(ones[:], 1.0).then_inc(ones_ready, 1)
            pool.wait_ge(dve_step, 1)
            nc.gpsimd.partition_all_reduce(top[:].rearrange("p b h -> p (b h)"),
                                           highest[:].rearrange("p b h -> p (b h)"), P, REDUCE_MAX
                                           ).then_inc(top_ready, 1)

        @block.tensor
        def _(pe):
            pe.wait_ge(ones_ready, 1)
            for j in range(NT):
                pe.wait_ge(mask_ready, j + 1)
                for q in range(N // MM):
                    mm = nc.tensor.matmul(degree[:, q * MM:(q + 1) * MM], ones[:],
                                          mask16[j % 2][:, q * MM:(q + 1) * MM], start=j == 0, stop=j == NT - 1)
                mm.then_inc(mask_used, 1)
            pe.wait_ge(exp_ready, 3)
            for k in range(BLOCKS):
                mm = nc.tensor.transpose(rows_ps[:, k, :], ratio[:, k * P:(k + 1) * P], c.ident[:])
            mm.then_inc(rows_ready, 1)

        @block.scalar
        def _(act):
            for j in range(NT):
                if j >= 2:
                    act.wait_ge(mask_used, j - 1)
                nc.scalar.copy(mask16[j % 2][:], c.edge_mask[:, j, :]).then_inc(mask_ready, 1)
            act.wait_ge(shifted_ready, 2)
            for k, scale in ((0, 1.0), (1, SLOPE)):
                nc.scalar.activation(factors[:, :, :, k, :].rearrange("p b h t -> p (b h) t"),
                                     shifted[:].rearrange("p b h t -> p (b h) t"), ACT.Exp, scale=scale
                                     ).then_inc(exp_ready, 1)
            nc.scalar.activation(ratio[:], exponent[:].rearrange("p b h t -> p (b h t)"), ACT.Exp
                                 ).then_inc(exp_ready, 1)
            act.wait_ge(rows_ready, 1)
            nc.scalar.copy(rows[:], rows_ps[:]).then_inc(rows_copied, 1)

        @block.vector
        def _(dve):
            dve.wait_ge(loaded, DMA)
            src = edge[:, :, :, 0:H].rearrange("p b t h -> p b h t")
            dst = edge[:, :, :, H:2 * H].rearrange("p b t h -> p b h t")
            for b in range(B):
                last = nc.vector.tensor_reduce(highest[:, b], dst[:, b], AXIS_FREE, ALU.max)
            last.then_inc(dve_step, 1)
            dve.wait_ge(top_ready, 1)
            for b in range(B):
                at = top[:, b].unsqueeze(2).to_broadcast([P, H, NT])
                nc.vector.tensor_tensor(shifted[:, b], dst[:, b], at, ALU.subtract)
                last = nc.vector.tensor_tensor(exponent[:, b], src[:, b], at, ALU.add)
            last.then_inc(shifted_ready, 1)
            dve.wait_ge(shifted_ready, 1)
            nc.vector.tensor_scalar(exponent[:], exponent[:], SLOPE - 1.0, MAX_EXPONENT, ALU.mult, ALU.min
                                    ).then_inc(shifted_ready, 1)
            dve.wait_ge(exp_ready, 1)
            for b in range(B):
                last = nc.vector.tensor_scalar(factors[:, b, :, 2, :], factors[:, b, :, 0, :], -1.0, None, ALU.mult)
            last.then_inc(negated, 1)
            dve.wait_ge(mask_used, NT)
            nc.vector.tensor_scalar(no_edge[:], degree[:], 0.0, None, ALU.is_equal).then_inc(negated, 1)
            dve.wait_ge(negated, 2)


def attend_layer1(nc, c, s, out, B, N, no_edge):
    NT = N // P
    HEAD_UNITS = NT
    BODY_UNITS = H * NT
    RING = 4
    LATE = 4
    BANK_T = 4
    BANKS = NT // BANK_T
    assert BODY_UNITS % RING == 0 and LATE < NT
    with ExitStack() as ctx:
        sb, ps, sem = allocators(nc, ctx, "attend1")
        ratio = [sb(f"ratio{i}", [P, N], F32) for i in range(2)]
        factors = [sb(f"factors{i}", [P, 3, NT], F32) for i in range(2)]
        values = [sb(f"values1_{i}", [P, NT, DV], F32) for i in range(2)]
        total = [sb(f"total{i}", [P, NT // 2, DV], F32) for i in range(2)]
        weights = [sb(f"weights{i}", [P, N], F32) for i in range(RING)]
        inverse = sb("inverse1", [P, NT], F32)
        hidden = sb("hidden", [P, NT, F], F32)
        x1 = sb("x1_in", [P, NT, F], F32)
        low = sb("low", [P, NT, F], F32)
        stats = sb("stats1", [P, NT, 6], F32)
        moments = sb("moments1", [P, NT, 2], F32)
        var_eps = sb("var_eps1", [P, NT], F32)
        rstd = sb("rstd1", [P, NT], F32)
        shift = sb("shift1", [P, NT], F32)
        acc = [[ps(f"acc{i}_{k}", [P, BANK_T, P], F32) for k in range(BANKS)]
               for i in range(2)]

        loaded = [sem(f"head_loaded{i}") for i in range(2)]
        x1_loaded = sem("x1_loaded")
        total_ready = sem("total_ready")
        pool_step = sem("pool_step")
        excess = sem("excess")
        weights_ready = sem("weights_ready")
        weights_free = sem("weights_free")
        head_summed = sem("head_summed")
        inverse_ready = sem("inverse_ready")
        head_ready = sem("head_ready")
        low_ready = sem("low_ready")
        low_exp = sem("low_exp")
        dve_step = sem("dve_step")
        moments_ready = sem("moments_ready")
        held = sem("held")
        rstd_ready = sem("rstd_ready")
        shift_ready = sem("shift_ready")
        normed = sem("normed")
        stored = sem("out_stored")
        sp_held = sem("sp_held")
        block = ctx.enter_context(nc.Block())

        @block.sync
        def _(sp):
            def load_head(b, h):
                i = h % 2
                head = H * b + h
                bb, hh = (b, h) if h < H else (b + 1, h - H)
                if not (isinstance(head, int) and head < 2):
                    hold(sp, excess, HEAD_UNITS * (head - 1), sp_held)
                    hold(sp, weights_ready, HEAD_UNITS * (head - 1), sp_held)
                    hold(sp, head_summed, head - 1, sp_held)
                    hold(sp, total_ready, head - 1, sp_held)
                at = s.ratio[bass.ds(head * NT, NT), :].rearrange("t p -> (t p)").partition_broadcast(P)
                sp.dma_start(ratio[i][:], at).then_inc(loaded[i], DMA)
                at = s.dst[bass.ds(bb, 1), hh].rearrange("o p w -> (o p) w")
                sp.dma_start(factors[i][:].rearrange("p k t -> p (k t)"), at).then_inc(loaded[i], DMA)
                at = s.v1[bass.ds(bb, 1), hh].rearrange("o p w -> (o p) w")
                sp.dma_start(values[i][:].rearrange("p t d -> p (t d)"), at).then_inc(loaded[i], DMA)

            def batch(b, last):
                for h in range(H):
                    if h == 1:
                        hold(sp, stored, DMA * b, sp_held)
                        at = s.x1[bass.ds(b, 1)].rearrange("o (t p) f -> p (o t) f", p=P)
                        hold(sp, moments_ready, b, sp_held)
                        sp.dma_start(x1[:], at).then_inc(x1_loaded, DMA)
                    if not (last and h == H - 1):
                        load_head(b, h + 1)

            def store(b):
                hold(sp, normed, b + 1, sp_held)
                at = out[bass.ds(b, 1)].rearrange("o (t p) f -> p (o t) f", p=P)
                sp.dma_start(at, low[:]).then_inc(stored, DMA)

            load_head(0, 0)
            batch(0, last=B == 1)
            if B > 2:
                with sp.Fori(1, B - 1) as b:
                    load_next(sp, b, load_head, store, batch)
            if B > 1:
                load_next(sp, B - 1, load_head, store, lambda b, last: batch(b, True))
            store(B - 1)
            hold(sp, stored, DMA * B, sp_held)

        @block.gpsimd
        def _(pool):
            def head_total(b, h):
                i = h % 2
                head = H * b + h
                pool.wait_ge(loaded[i], 3 * DMA * (H // 2 * b + h // 2 + 1))
                if not (isinstance(head, int) and head < 2):
                    pool.wait_ge(head_summed, head - 1)
                width = NT // 2
                steps = width.bit_length()
                nc.gpsimd.tensor_tensor(total[i][:], values[i][:, 0:width, :], values[i][:, width:2 * width, :],
                                        ALU.add).then_inc(pool_step, 1)
                for level in range(1, steps):
                    width //= 2
                    pool.wait_ge(pool_step, steps * head + level)
                    nc.gpsimd.tensor_tensor(total[i][:, 0:width, :], total[i][:, 0:width, :],
                                            total[i][:, width:2 * width, :], ALU.add).then_inc(pool_step, 1)
                pool.wait_ge(pool_step, steps * (head + 1))
                pool.sem_inc(total_ready, 1)

            def tail(b):
                pool.wait_ge(head_ready, 2 + H * (b + 1))
                hold(pool, stored, DMA * b, held)
                nc.gpsimd.tensor_scalar(low[:], hidden[:], 0.0, None, ALU.min).then_inc(low_ready, 1)
                pool.wait_ge(moments_ready, b + 1)
                nc.gpsimd.tensor_tensor(var_eps[:], moments[:, :, 1], c.eps[:, 0:NT], ALU.add).then_inc(low_ready, 1)
                pool.wait_ge(low_ready, 2 * (b + 1))
                nc.gpsimd.tensor_tensor(rstd[:], var_eps[:], c.minus_half[:, 0:NT], ALU.pow).then_inc(rstd_ready, 1)

            head_total(0, 0)
            if B > 1:
                with pool.Fori(0, B - 1) as b:
                    for h in range(H):
                        head_total(b, h + 1)
                    tail(b)
            for h in range(H - 1):
                head_total(B - 1, h + 1)
            tail(B - 1)

        @block.tensor
        def _(pe):
            with pe.Fori(0, B) as b:
                for h in range(H):
                    i = h % 2
                    head = H * b + h
                    pe.wait_ge(loaded[i], 3 * DMA * (H // 2 * b + h // 2 + 1))
                    pe.wait_ge(head_ready, head + 1)
                    for j in range(NT):
                        pe.wait_ge(weights_ready, HEAD_UNITS * head + j + 1)
                        for t in range(NT):
                            mm = nc.tensor.matmul(acc[i][t // BANK_T][:, t % BANK_T, 0:DV],
                                                  weights[j % RING][:, t * P:(t + 1) * P], values[i][:, j, :],
                                                  start=j == 0 and t % BANK_T == 0, stop=False,
                                                  skip_group_check=True)
                        mm.then_inc(weights_free, 1)
                    pe.wait_ge(total_ready, head + 1)
                    for t in range(NT):
                        mm = nc.tensor.matmul(acc[i][t // BANK_T][:, t % BANK_T, 0:DV],
                                              no_edge[:, t * P:(t + 1) * P], total[i][:, 0, :],
                                              start=False, stop=t % BANK_T == BANK_T - 1, skip_group_check=True)
                    mm.then_inc(head_summed, 1)

        @block.scalar
        def _(act):
            act.sem_inc(weights_free, RING)

            def unit(b, u):
                if u >= BODY_UNITS:
                    b, u = b + 1, u - BODY_UNITS
                h, j = u // NT, u % NT
                if j == 0:
                    act.wait_ge(loaded[h % 2], 3 * DMA * (H // 2 * b + h // 2 + 1))
                act.wait_ge(weights_free, BODY_UNITS * b + u + 1)
                nc.scalar.activation(weights[u % RING][:], ratio[h % 2][:], ACT.Relu,
                                     bias=factors[h % 2][:, 2, j:j + 1], scale=factors[h % 2][:, 1, j:j + 1]
                                     ).then_inc(excess, 1)

            def tail(b):
                act.wait_ge(low_ready, 2 * b + 1)
                nc.scalar.activation(low[:], low[:], ACT.Exp).then_inc(low_exp, 1)

            def norm(b):
                act.wait_ge(shift_ready, b + 1)
                for t in range(NT):
                    last = nc.scalar.activation(low[:, t, :], hidden[:, t, :], ACT.Identity,
                                                bias=shift[:, t:t + 1], scale=rstd[:, t:t + 1])
                last.then_inc(normed, 1)

            for u in range(LATE + 4):
                unit(0, u)
            if B > 1:
                with act.Fori(0, B - 1) as b:
                    for u in range(LATE + 4, BODY_UNITS + LATE + 4):
                        unit(b, u)
                        if u == BODY_UNITS + LATE + 1:
                            tail(b)
                    norm(b)
            for u in range(LATE + 4, BODY_UNITS):
                unit(B - 1, u)
            tail(B - 1)
            norm(B - 1)

        @block.vector
        def _(dve):
            dve.sem_inc(head_ready, 2)

            def unit(b, u):
                if u >= BODY_UNITS:
                    b, u = b + 1, u - BODY_UNITS
                h, j = u // NT, u % NT
                dve.wait_ge(excess, BODY_UNITS * b + u + 1)
                nc.vector.scalar_tensor_tensor(
                    out=weights[u % RING][:], in0=weights[u % RING][:], scalar=factors[h % 2][:, 0, j:j + 1],
                    in1=c.edge_mask[:, j, :], op0=ALU.add, op1=ALU.mult).then_inc(weights_ready, 1)

            def take_head(b, h):
                i = h % 2
                head = H * b + h
                dve.wait_ge(head_summed, head + 1)
                for k in range(BANKS):
                    last = nc.vector.reciprocal(inverse[:, k * BANK_T:(k + 1) * BANK_T], acc[i][k][:, :, DH])
                last.then_inc(inverse_ready, 1)
                dve.wait_ge(inverse_ready, head + 1)
                if h == 0:
                    dve.wait_ge(normed, b)
                for k in range(BANKS):
                    tiles = slice(k * BANK_T, (k + 1) * BANK_T)
                    last = nc.vector.tensor_tensor(
                        hidden[:, tiles, h * DH:(h + 1) * DH], acc[i][k][:, :, 0:DH],
                        inverse[:, tiles].unsqueeze(2).to_broadcast([P, BANK_T, DH]), ALU.mult)
                last.then_inc(head_ready, 1)

            def tail(b):
                dve.wait_ge(low_exp, b + 1)
                nc.vector.scalar_tensor_tensor(out=hidden[:], in0=hidden[:], scalar=0.0, in1=low[:], op0=ALU.max,
                                               op1=ALU.add).then_inc(dve_step, 1)
                dve.wait_ge(dve_step, 3 * b + 1)
                dve.wait_ge(x1_loaded, DMA * (b + 1))
                nc.vector.scalar_tensor_tensor(out=hidden[:], in0=hidden[:], scalar=-1.0, in1=x1[:], op0=ALU.add,
                                               op1=ALU.add).then_inc(dve_step, 1)
                dve.wait_ge(dve_step, 3 * b + 2)
                for t in range(NT):
                    last = nc.vector.bn_stats(stats[:, t, :], hidden[:, t, :])
                last.then_inc(dve_step, 1)
                hold(dve, dve_step, 3 * b + 3, held)
                for t in range(NT):
                    last = nc.vector.bn_aggr(moments[:, t, :], stats[:, t, :])
                last.then_inc(moments_ready, 1)
                dve.wait_ge(rstd_ready, b + 1)
                nc.vector.scalar_tensor_tensor(out=shift[:], in0=moments[:, :, 0], scalar=-1.0, in1=rstd[:],
                                               op0=ALU.mult, op1=ALU.mult).then_inc(shift_ready, 1)

            for u in range(LATE):
                unit(0, u)
            if B > 1:
                with dve.Fori(0, B - 1) as b:
                    for h in range(H):
                        for u in range(NT):
                            unit(b, h * NT + LATE + u)
                        take_head(b, h)
                    tail(b)
            for h in range(H):
                for u in range(NT):
                    if h * NT + LATE + u < BODY_UNITS:
                        unit(B - 1, h * NT + LATE + u)
                take_head(B - 1, h)
            tail(B - 1)


def load_next(sp, b, load_head, store, batch):
    store(b - 1)
    batch(b, last=False)


def program(nc, x, adj, weights, out):
    B, N, _ = x.shape
    s = Scratch(nc, B, N)
    with ExitStack() as ctx:
        c = Constants(nc, ctx, N)
        prepare_weights(nc, c, weights)
        project_layer0(nc, c, s, x, adj, B, N)
        attend_layer0(nc, c, s, B, N)
        finish_layer0(nc, c, s, x, B, N)
        no_edge = ctx.enter_context(nc.sbuf_tensor("no_edge", [P, N], F32))
        prepare_layer1(nc, c, s, B, N, no_edge)
        attend_layer1(nc, c, s, out, B, N, no_edge)


_WEIGHTS = {"Wq": "L0_gnn_Wq", "bq": "L0_gnn_bq", "Wk": "L0_gnn_Wk", "bk": "L0_gnn_bk", "Wv": "L0_gnn_Wv",
            "bv": "L0_gnn_bv", "Wo": "L0_gnn_Wo", "bo": "L0_gnn_bo", "gamma": "L0_gnn_gamma",
            "beta": "L0_gnn_beta", "W": "L1_gnn_W", "a": "L1_gnn_a"}


def kernel(**inputs):
    import numpy as np
    from concourse import bacc
    from concourse.bass_utils import run_bass_kernel_spmd

    nc = bacc.Bacc("TRN2", target_bir_lowering=False, num_devices=1)
    arrays, aps = {}, {}
    for name in ("x", "adj", *_WEIGHTS.values()):
        a = np.ascontiguousarray(inputs[name])
        arrays[f"in_{name}"] = a
        aps[name] = nc.dram_tensor(f"in_{name}", a.shape, mybir.dt.from_np(a.dtype), kind="ExternalInput").ap()
    out = nc.dram_tensor("out", aps["x"].shape, F32, kind="ExternalOutput").ap()
    program(nc, aps["x"], aps["adj"], {short: aps[name] for short, name in _WEIGHTS.items()}, out)
    r = run_bass_kernel_spmd(nc, [arrays], core_ids=[0])
    return r.results[0]["out"]
```

```python
import math
from contextlib import ExitStack

import concourse.bass as bass
from concourse import mybir

ALU = mybir.AluOpType
ACT = mybir.ActivationFunctionType
AXIS_FREE = mybir.AxisListType.X
F32 = mybir.dt.float32
F16 = mybir.dt.float16
BF16 = mybir.dt.bfloat16
I32 = mybir.dt.int32
I8 = mybir.dt.int8
REDUCE_MAX = bass.bass_isa.ReduceOp.max

P = 128
F = 256
FC = F // P
H = 4
DH = F // H
DV = DH + 1
PAIRS = H // 2
CHUNK = 256
KT = CHUNK // P
QG = 512
QT = QG // P
CLIP = 10.0
SCALE = float(DH) ** -0.5
RAW_CLIP = CLIP / SCALE
EXP_BIAS = CLIP - 6 * math.log(2.0)
SOURCE_BIAS = 12 * math.log(2.0)
EPS = 1e-5
SLOPE = 0.2
STEEP = 2.0 ** 100
FACTORS = 5
DMA = 16


def allocators(nc, ctx, phase):
    def sb(name, shape, dt):
        return ctx.enter_context(nc.sbuf_tensor(f"{phase}_{name}", shape, dt))

    def ps(name, shape, dt):
        return ctx.enter_context(nc.psum_tensor(f"{phase}_{name}", shape, dt))

    def sem(name):
        return ctx.enter_context(nc.semaphore(f"{phase}_{name}"))

    return sb, ps, sem


def hold(engine, semaphore, value, held):
    engine.wait_ge(semaphore, value)
    engine.sem_inc(held, 1)


class Scratch:

    def __init__(self, nc, B, N):
        NT = N // P
        self.q = nc.dram_tensor("q_split", [B, PAIRS, 2, P, N], F16, kind="Internal")
        self.k = nc.dram_tensor("k_split", [B, PAIRS, 2, P, N], F16, kind="Internal")
        self.v = nc.dram_tensor("v_split", [B, H, P, NT * 2 * DV], F16, kind="Internal")
        self.edge_mask = nc.dram_tensor("edge_mask_16", [P, NT, N], BF16, kind="Internal")
        self.ctx = nc.dram_tensor("context", [B, N, F], F32, kind="Internal")
        self.x1 = nc.dram_tensor("x_layer1", [B, N, F], F32, kind="Internal")
        self.v1 = nc.dram_tensor("v1_ones", [B, H, P, NT * DV], F32, kind="Internal")
        self.e = nc.dram_tensor("edge_terms", [B, P, NT * 2 * H], F32, kind="Internal")
        self.src = nc.dram_tensor("src_rows", [B * H * NT, P], F32, kind="Internal")
        self.factors = nc.dram_tensor("factors", [B, H, P, FACTORS * NT], F32, kind="Internal")


class Constants:

    def __init__(self, nc, ctx):
        sb, ps, sem = allocators(nc, ctx, "const")
        self.ident = sb("ident", [P, P], F32)
        self.ident16 = sb("ident16", [P, P], BF16)
        self.woT = sb("woT", [P, FC, F], F32)
        self.w1 = sb("w1", [P, FC, F + 2 * H], F32)
        self.bo = sb("bo", [P, F], F32)
        self.gamma = sb("gamma", [P, F], F32)
        self.beta = sb("beta", [P, F], F32)
        self.minus_half = sb("minus_half", [P, 16], F32)
        self.eps = sb("eps", [P, 16], F32)
        self.exp_bias = sb("exp_bias", [P, 1], F32)
        self.source_bias = sb("source_bias", [P, 1], F32)

    def for_layer0(self, nc, ctx, N):
        sb, ps, sem = allocators(nc, ctx, "layer0")
        self.clip_mask = sb("clip_mask", [P, N // P, N], I8)
        self.wqT = sb("wqT", [P, FC, F], F32)
        self.wkT = sb("wkT", [P, FC, F], F32)
        self.wvT = sb("wvT", [P, FC, F], F32)
        self.bq = sb("bq", [P, PAIRS], F32)
        self.bk = sb("bk", [P, PAIRS], F32)
        self.bv = sb("bv", [P, F], F32)

    def for_layer1(self, nc, ctx, N):
        sb, ps, sem = allocators(nc, ctx, "layer1")
        self.edge_mask = sb("edge_mask", [P, N // P, N], BF16)
        self.no_edge = sb("no_edge", [P, N], BF16)


def prepare_weights(nc, c, w):
    with ExitStack() as ctx:
        sb, ps, sem = allocators(nc, ctx, "weights")
        raw = sb("raw_weights", [P, 4, FC, F], F32)
        a_rows = sb("a_rows", [P, 2, DH], F32)
        product = sb("product", [P, 2, FC * H, DH], F32)
        turned = [ps(f"turned{i}", [P, FC, F], F32) for i in range(4)]
        raw_loaded = sem("raw_loaded")
        w1_loaded = sem("w1_loaded")
        rows_loaded = sem("rows_loaded")
        cleared = sem("cleared")
        ident_ready = sem("ident_ready")
        turned_ready = sem("turned_ready")
        copied = sem("copied")
        product_ready = sem("product_ready")
        sp_held = sem("sp_held")
        block = ctx.enter_context(nc.Block())

        @block.sync
        def _(sp):
            for m, name in enumerate(("Wq", "Wk", "Wv", "Wo")):
                sp.dma_start(raw[:, m], w[name].rearrange("(c p) f -> p c f", p=P)).then_inc(raw_loaded, DMA)
            sp.dma_start(c.w1[:, :, 0:F], w["W"].rearrange("(c p) f -> p c f", p=P)).then_inc(w1_loaded, DMA)
            sp.dma_start(a_rows[:].rearrange("p s d -> p (s d)"), w["a"].partition_broadcast(P)).then_inc(w1_loaded, DMA)
            for dst, name in ((c.bv, "bv"), (c.bo, "bo"), (c.gamma, "gamma"), (c.beta, "beta")):
                sp.dma_start(dst[:], w[name].partition_broadcast(P)).then_inc(rows_loaded, DMA)
            with nc.allow_non_contiguous_dma(reason="two small bias columns"):
                for dst, name in ((c.bq, "bq"), (c.bk, "bk")):
                    sp.dma_start(dst[:], w[name].rearrange("(c p) -> p c", p=P)).then_inc(rows_loaded, DMA)
            hold(sp, rows_loaded, 6 * DMA, sp_held)

        @block.gpsimd
        def _(pool):
            nc.gpsimd.memset(c.minus_half[:], -0.5)
            nc.gpsimd.memset(c.eps[:], EPS)
            nc.gpsimd.memset(c.exp_bias[:], EXP_BIAS)
            nc.gpsimd.memset(c.source_bias[:], SOURCE_BIAS)
            nc.gpsimd.memset(c.ident16[:], 0.0)
            nc.gpsimd.memset(c.ident[:], 0.0).then_inc(cleared, 1)
            pool.wait_ge(cleared, 1)
            nc.gpsimd.affine_select(out=c.ident16[:], in_=c.ident16[:], compare_op=ALU.not_equal, fill=1.0,
                                    base=0, pattern=[[-1, P]], channel_multiplier=1)
            nc.gpsimd.affine_select(out=c.ident[:], in_=c.ident[:], compare_op=ALU.not_equal, fill=1.0,
                                    base=0, pattern=[[-1, P]], channel_multiplier=1).then_inc(ident_ready, 1)

        @block.tensor
        def _(pe):
            pe.wait_ge(raw_loaded, 4 * DMA)
            pe.wait_ge(ident_ready, 1)
            for m in range(4):
                for oc in range(FC):
                    for fc in range(FC):
                        mm = nc.tensor.transpose(turned[m][:, fc, oc * P:(oc + 1) * P],
                                                 raw[:, m, oc, fc * P:(fc + 1) * P], c.ident[:])
                mm.then_inc(turned_ready, 1)

        @block.scalar
        def _(act):
            for m, dst in enumerate((c.wqT, c.wkT, c.wvT, c.woT)):
                act.wait_ge(turned_ready, m + 1)
                nc.scalar.copy(dst[:], turned[m][:]).then_inc(copied, 1)
            act.wait_ge(copied, 4)

        @block.vector
        def _(dve):
            dve.wait_ge(w1_loaded, 2 * DMA)
            heads = c.w1[:, :, 0:F].rearrange("p c (h d) -> p c h d", h=H)
            for s in range(2):
                for fc in range(FC):
                    last = nc.vector.tensor_tensor(
                        product[:, s, fc * H:(fc + 1) * H, :], heads[:, fc],
                        a_rows[:, s:s + 1, :].to_broadcast([P, H, DH]), ALU.mult)
            last.then_inc(product_ready, 1)
            dve.wait_ge(product_ready, 1)
            for s in range(2):
                for fc in range(FC):
                    nc.vector.tensor_reduce(c.w1[:, fc, F + s * H:F + (s + 1) * H],
                                            product[:, s, fc * H:(fc + 1) * H, :], AXIS_FREE,
                                            ALU.add).then_inc(product_ready, 1)
            dve.wait_ge(product_ready, 1 + 2 * FC)


def project_layer0(nc, c, s, x, adj, B, N):
    NT = N // P
    STEP = 512
    TT = STEP // P
    ITERATIONS = B * N // (2 * STEP)
    ROWS = NT // ITERATIONS
    assert ROWS * ITERATIONS == NT
    HALF = 8
    HALVES = NT // HALF
    x_steps = x.rearrange("b n f -> (b n) f").rearrange("(i t p) f -> i p t f", p=P, t=TT)
    adj_rows = adj.rearrange("(i p) j -> i p j", p=P)
    STEPS = N // STEP
    assert STEPS % 2 == 0
    with ExitStack() as ctx:
        sb, ps, sem = allocators(nc, ctx, "project")
        x_in = [sb(f"x_in{i}", [P, TT, F], F32) for i in range(2)]
        xT = [sb(f"xT{i}", [P, FC, STEP], F32) for i in range(2)]
        split = [[sb(f"split{i}_{m}", [P, 2, STEP], F16) for m in range(2 * PAIRS)] for i in range(2)]
        v_sum = [sb(f"v_sum{i}", [P, H, TT, DH], F32) for i in range(2)]
        v_out = [sb(f"v_out{i}", [P, H * TT, 2, DV], F16) for i in range(2)]
        edge_tiles = sb("edge_tiles", [P, HALVES, HALF, P], BF16)
        adj_in = sb("adj_in", [P, N], I32)
        is_zero = sb("is_zero", [P, N], BF16)
        is_edge = sb("is_edge", [P, N], BF16)
        xT_ps = ps("xT_ps", [P, FC, STEP], F32)
        qk_ps = [ps(f"qk_ps{i}", [P, STEP], F32) for i in range(2)]
        v_ps = [ps(f"v_ps{i}", [P, 2, F], F32) for i in range(2)]
        mask_ps = [ps(f"mask_ps{i}", [P, HALF, P], BF16) for i in range(2)]

        x_loaded = [sem(f"x_loaded{i}") for i in range(2)]
        x_turned = sem("x_turned")
        xT_ready = sem("xT_ready")
        qk_ready = sem("qk_ready")
        high_ready = sem("high_ready")
        low_ready = sem("low_ready")
        v_ready = sem("v_ready")
        v_copied = sem("v_copied")
        v_high = sem("v_high")
        v_split = sem("v_split")
        edges_stored = sem("edges_stored")
        ones_ready = sem("ones_ready")
        split_stored = [sem(f"split_stored{i}") for i in range(2)]
        v_stored = [sem(f"v_stored{i}") for i in range(2)]
        adj_loaded = sem("adj_loaded")
        adj_coded = sem("adj_coded")
        mask_turned = sem("mask_turned")
        mask_ready = sem("mask_ready")
        sp_held = sem("sp_held")
        block = ctx.enter_context(nc.Block())
        codes = (is_zero, is_edge)
        turns = {q * 4 // (ROWS * HALVES): (q // HALVES, q % HALVES) for q in range(ROWS * HALVES)}
        assert len(turns) == ROWS * HALVES

        @block.sync
        def _(sp):
            def load_x(b, st):
                i = st % 2
                hold(sp, x_turned, STEPS * b + st - 1, sp_held)
                at = x_steps[bass.ds(STEPS * b + st, 1)].rearrange("o p t f -> (o p) t f")
                sp.dma_start(x_in[i][:], at).then_inc(x_loaded[i], DMA)

            def batch(b, last):
                for st in range(STEPS):
                    i = st % 2
                    if not (last and st == STEPS - 1):
                        load_x(b, st + 1)
                    if i == 0:
                        for r in range(ROWS):
                            row = ROWS * (STEPS // 2 * b + st // 2) + r
                            if not (isinstance(b, int) and b == 0 and st == 0 and r == 0):
                                hold(sp, adj_coded, row, sp_held)
                            sp.dma_start(adj_in[:], adj_rows[bass.ds(row, 1)].rearrange("o p j -> (o p) j")
                                         ).then_inc(adj_loaded, DMA)
                    for m in range(2 * PAIRS):
                        hold(sp, low_ready, 2 * PAIRS * (STEPS * b + st) + m + 1, sp_held)
                        dst = (s.q, s.k)[m // PAIRS][bass.ds(b, 1), m % PAIRS, :, :, st * STEP:(st + 1) * STEP]
                        sp.dma_start(dst.rearrange("o s p w -> p (o s) w"), split[i][m][:]
                                     ).then_inc(split_stored[i], DMA)
                    hold(sp, v_split, STEPS * b + st + 1, sp_held)
                    wide = TT * 2 * DV
                    dst = s.v[bass.ds(b, 1), :, :, st * wide:(st + 1) * wide]
                    sp.dma_start(dst.rearrange("o h p w -> p (o h) w"),
                                 v_out[i][:].rearrange("p (h t) s d -> p h (t s d)", h=H)).then_inc(v_stored[i], DMA)
                    for q, (r, half) in turns.items():
                        if q // 2 == i and half == HALVES - 1:
                            row = ROWS * (STEPS // 2 * b + st // 2) + r
                            hold(sp, mask_ready, 2 * HALVES * (row + 1), sp_held)
                            sp.dma_start(s.edge_mask[:, :, bass.ds(row * P, P)],
                                         edge_tiles[:].rearrange("p a j w -> p (a j) w")).then_inc(edges_stored, DMA)

            first = x_steps[0:1].rearrange("o p t f -> (o p) t f")
            sp.dma_start(x_in[0][:], first).then_inc(x_loaded[0], DMA)
            if B > 1:
                with sp.Fori(0, B - 1) as b:
                    batch(b, last=False)
            batch(B - 1, last=True)
            for i in range(2):
                hold(sp, split_stored[i], ITERATIONS * 2 * PAIRS * DMA, sp_held)
                hold(sp, v_stored[i], ITERATIONS * DMA, sp_held)
            hold(sp, edges_stored, NT * DMA, sp_held)

        @block.gpsimd
        def _(pool):
            for i in range(2):
                nc.gpsimd.memset(v_out[i][:, :, 0, DH:DV], 1.0)
                last = nc.gpsimd.memset(v_out[i][:, :, 1, DH:DV], 0.0)
            last.then_inc(ones_ready, 1)
            with pool.Fori(0, ITERATIONS) as n:
                for i in range(2):
                    pool.wait_ge(v_high, 2 * n + i + 1)
                    nc.gpsimd.tensor_tensor(v_out[i][:, :, 1, 0:DH], v_sum[i][:].rearrange("p h t d -> p (h t) d"),
                                            v_out[i][:, :, 0, 0:DH], ALU.subtract).then_inc(v_split, 1)

        @block.tensor
        def _(pe):
            def turn_masks(n, r, half):
                pe.wait_ge(adj_coded, ROWS * n + r + 1)
                pe.wait_ge(mask_ready, 2 * (HALVES * (ROWS * n + r) + half))
                for m in range(2):
                    for j in range(HALF):
                        col = (half * HALF + j) * P
                        mm = nc.tensor.transpose(mask_ps[m][:, j, :], codes[m][:, col:col + P], c.ident16[:])
                mm.then_inc(mask_turned, 1)

            with pe.Fori(0, ITERATIONS) as n:
                for i in range(2):
                    pe.wait_ge(x_loaded[i], DMA * (n + 1))
                    pe.wait_ge(xT_ready, 2 * n + i)
                    for fc in range(FC):
                        for t in range(TT):
                            mm = nc.tensor.transpose(xT_ps[:, fc, t * P:(t + 1) * P],
                                                     x_in[i][:, t, fc * P:(fc + 1) * P], c.ident[:])
                    mm.then_inc(x_turned, 1)
                    pe.wait_ge(xT_ready, 2 * n + i + 1)
                    for m in range(2 * PAIRS):
                        w = (c.wqT, c.wkT)[m // PAIRS]
                        pair = m % PAIRS
                        item = 2 * PAIRS * i + m
                        if item >= 2:
                            pe.wait_ge(low_ready, 4 * PAIRS * n + item - 1)
                        else:
                            pe.wait_ge(low_ready, 4 * PAIRS * n)
                        for fc in range(FC):
                            mm = nc.tensor.matmul(qk_ps[m % 2][:], w[:, fc, pair * P:(pair + 1) * P], xT[i][:, fc, :],
                                                  start=fc == 0, stop=fc == FC - 1)
                        mm.then_inc(qk_ready, 1)
                        if m % 2 and 2 * i + m // 2 in turns:
                            turn_masks(n, *turns[2 * i + m // 2])
                    for t2 in range(2):
                        pe.wait_ge(v_copied, 4 * n + 2 * i)
                        for t in range(2):
                            tok = (2 * t2 + t) * P
                            for fc in range(FC):
                                mm = nc.tensor.matmul(v_ps[t2][:, t, :], xT[i][:, fc, tok:tok + P], c.wvT[:, fc, :],
                                                      start=fc == 0, stop=fc == FC - 1)
                        mm.then_inc(v_ready, 1)

        @block.scalar
        def _(act):
            act.wait_ge(ones_ready, 1)
            with act.Fori(0, ITERATIONS) as n:
                for i in range(2):
                    act.wait_ge(x_turned, 2 * n + i + 1)
                    act.wait_ge(v_ready, 4 * n)
                    nc.scalar.copy(xT[i][:], xT_ps[:]).then_inc(xT_ready, 1)
                    for m in range(2 * PAIRS):
                        act.wait_ge(qk_ready, 4 * PAIRS * n + 2 * PAIRS * i + m + 1)
                        if m == 0:
                            act.wait_ge(split_stored[i], 2 * PAIRS * DMA * n)
                        nc.scalar.activation(split[i][m][:, 0, :], qk_ps[m % 2][:], ACT.Identity,
                                             bias=(c.bq, c.bk)[m // PAIRS][:, m % PAIRS:m % PAIRS + 1],
                                             ).then_inc(high_ready, 1)
                    act.wait_ge(v_stored[i], DMA * n)
                    act.wait_ge(v_copied, 2 * (2 * n + i) + 2)
                    nc.scalar.copy(v_out[i][:, :, 0, 0:DH], v_sum[i][:].rearrange("p h t d -> p (h t) d")
                                   ).then_inc(v_high, 1)

        @block.vector
        def _(dve):
            def code_row(row):
                dve.wait_ge(adj_loaded, DMA * (row + 1))
                dve.wait_ge(mask_turned, HALVES * row)
                nc.vector.tensor_scalar(is_zero[:], adj_in[:], 0.0, -2 * RAW_CLIP, ALU.is_equal, ALU.mult)
                nc.vector.tensor_scalar(is_edge[:], adj_in[:], 0.0, None, ALU.is_gt).then_inc(adj_coded, 1)

            def keep_masks(row, half):
                dve.wait_ge(mask_turned, HALVES * row + half + 1)
                nc.vector.tensor_scalar(c.clip_mask[:, half * HALF:(half + 1) * HALF, bass.ds(row * P, P)],
                                        mask_ps[0][:], RAW_CLIP, None, ALU.add).then_inc(mask_ready, 1)
                if half == 0:
                    dve.wait_ge(edges_stored, DMA * row)
                nc.vector.tensor_copy(edge_tiles[:, half], mask_ps[1][:]).then_inc(mask_ready, 1)

            with dve.Fori(0, ITERATIONS) as n:
                for i in range(2):
                    for m in range(2 * PAIRS):
                        turn = turns.get(2 * i + m // 2)
                        if m % 2 == 0 and turn and turn[1] == 0:
                            code_row(ROWS * n + turn[0])
                        dve.wait_ge(high_ready, 2 * PAIRS * (2 * n + i) + m + 1)
                        nc.vector.scalar_tensor_tensor(
                            out=split[i][m][:, 1, :], in0=qk_ps[m % 2][:],
                            scalar=(c.bq, c.bk)[m // PAIRS][:, m % PAIRS:m % PAIRS + 1],
                            in1=split[i][m][:, 0, :], op0=ALU.add, op1=ALU.subtract).then_inc(low_ready, 1)
                        if m % 2 and turn:
                            keep_masks(ROWS * n + turn[0], turn[1])
                    dve.wait_ge(v_split, 2 * n)
                    for t2 in range(2):
                        dve.wait_ge(v_ready, 2 * (2 * n + i) + t2 + 1)
                        nc.vector.tensor_tensor(
                            v_sum[i][:, :, 2 * t2:2 * t2 + 2, :].rearrange("p h t d -> p t h d"),
                            v_ps[t2][:].rearrange("p t (h d) -> p t h d", h=H),
                            c.bv[:].rearrange("p (o h d) -> p o h d", o=1, h=H).to_broadcast([P, 2, H, DH]),
                            ALU.add).then_inc(v_copied, 1)


def attend_layer0(nc, c, s, B, N):
    NQ, NCH = N // QG, N // CHUNK
    HEAD_UNITS = NQ * NCH
    BODY_UNITS = 2 * HEAD_UNITS
    PAIR_COUNT = B * PAIRS
    UNITS = BODY_UNITS * PAIR_COUNT
    GROUPS = 2 * NQ
    NT = N // P
    S_RING, P_RING, O_RING = 2, 8, 4
    AHEAD = 5
    EXP_AHEAD = 4
    MASK_AHEAD = 2
    assert BODY_UNITS % P_RING == 0 and NCH % O_RING == 0 and AHEAD < P_RING and PAIR_COUNT > 2
    with ExitStack() as ctx:
        sb, ps, sem = allocators(nc, ctx, "attend0")
        k_split = [sb(f"k_split{i}", [P, N], F16) for i in range(2)]
        q_high = [sb(f"q_high{i}", [P, N], F16) for i in range(2)]
        q_low = [sb(f"q_low{i}", [P, N], F16) for i in range(2)]
        values = [sb(f"values{i}", [P, NT, 2, DV], F16) for i in range(2)]
        probs = [sb(f"probs{i}", [P, KT, QG], F32) for i in range(P_RING)]
        rest = [sb(f"rest{i}", [P, KT, QG], F16) for i in range(P_RING)]
        sums = [sb(f"sums{i}", [P, NCH * QT, DV], F32) for i in range(2)]
        inverse = [sb(f"inverse{i}", [P, NCH * QT], F32) for i in range(2)]
        scaled = sb("scaled", [P, NCH * QT, DH], F32)
        context = [sb(f"context{i}", [P, QT, DH], F32) for i in range(2)]
        s_ps = [ps(f"s_ps{i}", [P, KT, QG], F32) for i in range(S_RING)]
        o_ps = [ps(f"o_ps{i}", [P, QT, P], F32) for i in range(O_RING)]

        qk_loaded = [sem(f"qk_loaded{i}") for i in range(2)]
        v_loaded = [sem(f"v_loaded{i}") for i in range(2)]
        scores_ready = sem("scores_ready")
        masked = sem("masked")
        probs_ready = sem("probs_ready")
        rest_dve = sem("rest_dve")
        rest_pool = sem("rest_pool")
        probs_free = sem("probs_free")
        summed = sem("summed")
        sums_free = sem("sums_free")
        inverse_ready = sem("inverse_ready")
        group_free = sem("group_free")
        pool_step = sem("pool_step")
        context_ready = sem("context_ready")
        context_stored = [sem(f"context_stored{i}") for i in range(2)]
        sp_held = sem("sp_held")
        block = ctx.enter_context(nc.Block())
        LEVELS = NCH.bit_length() - 1
        assert NCH == 1 << LEVELS and LEVELS >= 1

        def unit(u):
            return u // HEAD_UNITS, u % HEAD_UNITS // NCH, u % NCH

        POOL_UNITS = [u % 2 == 1 for u in range(BODY_UNITS)]

        def rest_count(it, u):
            mine = [x == POOL_UNITS[u] for x in POOL_UNITS]
            return (rest_pool if POOL_UNITS[u] else rest_dve), sum(mine) * it + sum(mine[:u + 1])

        @block.sync
        def _(sp):
            def load_head(b, h):
                i = h % 2
                head = H * b + h
                bb, hh = (b, h) if h < H else (b + 1, h - H)
                rows = slice(hh % 2 * DH, hh % 2 * DH + DH)
                if not (isinstance(head, int) and head < 2):
                    hold(sp, scores_ready, HEAD_UNITS * (head - 1), sp_held)
                at = [[t[bass.ds(bb, 1), hh // 2, half, rows, :].rearrange("o d n -> (o d) n") for half in range(2)]
                      for t in (s.q, s.k)]
                for half in range(2):
                    place = slice(half * DH, half * DH + DH)
                    sp.dma_start(k_split[i][place, :], at[1][half]).then_inc(qk_loaded[i], DMA)
                    sp.dma_start(q_high[i][place, :], at[0][0]).then_inc(qk_loaded[i], DMA)
                    sp.dma_start(q_low[i][place, :], at[0][1]).then_inc(qk_loaded[i], DMA)
                if not (isinstance(head, int) and head < 2):
                    hold(sp, probs_free, P_RING + HEAD_UNITS * (head - 1), sp_held)
                v_at = s.v[bass.ds(bb, 1), hh, :, :].rearrange("o p w -> (o p) w")
                sp.dma_start(values[i][:].rearrange("p t s d -> p (t s d)"), v_at).then_inc(v_loaded[i], DMA)

            def store_group(b, h, g):
                hold(sp, context_ready, NQ * (H * b + h) + g + 1, sp_held)
                dst = s.ctx[bass.ds(b, 1), g * QG:(g + 1) * QG, h * DH:(h + 1) * DH]
                sp.dma_start(dst.rearrange("o (t p) d -> p (o t) d", p=P), context[g % 2][:]
                             ).then_inc(context_stored[g % 2], DMA)

            def batch(b, last):
                for h in range(H):
                    for g in range(NQ):
                        if g == 0 and not (last and h == H - 1):
                            load_head(b, h + 1)
                        store_group(b, h, g)

            load_head(0, 0)
            if B > 1:
                with sp.Fori(0, B - 1) as b:
                    batch(b, last=False)
            batch(B - 1, last=True)
            for i in range(2):
                hold(sp, context_stored[i], B * H * NQ // 2 * DMA, sp_held)

        @block.tensor
        def _(pe):
            def scores(it, u):
                if u >= BODY_UNITS:
                    it, u = it + 1, u - BODY_UNITS
                hh, g, j = unit(u)
                if u % HEAD_UNITS == 0:
                    pe.wait_ge(qk_loaded[hh], 6 * DMA * (it + 1))
                if not (isinstance(it, int) and it == 0 and u < S_RING):
                    pe.wait_ge(masked, BODY_UNITS * it + u - S_RING + 1)
                for kt in range(KT):
                    key = (KT * j + kt) * P
                    for half, q in enumerate((q_high, q_low)):
                        mm = nc.tensor.matmul(s_ps[u % S_RING][:, kt, :], k_split[hh][:, key:key + P],
                                              q[hh][:, g * QG:(g + 1) * QG], start=half == 0, stop=half == 1)
                mm.then_inc(scores_ready, 1)

            def products(it, u):
                hh, g, j = unit(u)
                if u % HEAD_UNITS == 0:
                    pe.wait_ge(v_loaded[hh], DMA * (it + 1))
                rest_ready, count = rest_count(it, u)
                pe.wait_ge(rest_ready, count)
                pe.wait_ge(sums_free, BODY_UNITS * it + u + 1)
                upper = probs[u % P_RING][:].bitcast(BF16)
                for t in range(QT):
                    to = o_ps[u % O_RING][:, t, :]
                    for kt in range(KT):
                        w_high = upper[:, kt, 2 * t * P + 1:2 * (t + 1) * P:2]
                        w_rest = rest[u % P_RING][:, kt, t * P:(t + 1) * P]
                        v = values[hh][:, KT * j + kt]
                        last = kt == KT - 1
                        nc.tensor.matmul(to[:, 0:DV], w_high, v[:, 0, :], start=kt == 0, stop=False)
                        nc.tensor.matmul(to[:, 0:DH], w_high, v[:, 1, 0:DH], start=False, stop=False,
                                         skip_group_check=True)
                        mm = nc.tensor.matmul(to[:, 0:DV], w_rest, v[:, 0, :], start=False, stop=last)
                mm.then_inc(probs_free, 1)

            pe.sem_inc(probs_free, P_RING)
            for u in range(AHEAD):
                scores(0, u)
            with pe.Fori(0, PAIR_COUNT - 1) as it:
                for u in range(BODY_UNITS):
                    scores(it, u + AHEAD)
                    products(it, u)
            for u in range(BODY_UNITS):
                if u + AHEAD < BODY_UNITS:
                    scores(PAIR_COUNT - 1, u + AHEAD)
                products(PAIR_COUNT - 1, u)

        @block.scalar
        def _(act):
            def exponentials(it, u):
                if u >= BODY_UNITS:
                    it, u = it + 1, u - BODY_UNITS
                act.wait_ge(masked, BODY_UNITS * it + u + 1)
                nc.scalar.activation(probs[u % P_RING][:], probs[u % P_RING][:], ACT.Exp, bias=c.exp_bias[:],
                                     scale=SCALE).then_inc(probs_ready, 1)

            def copy_sums(it, u):
                g = u // NCH
                if u % NCH == 0:
                    act.wait_ge(group_free, GROUPS * it + g + 1)
                act.wait_ge(probs_free, P_RING + BODY_UNITS * it + u + 1)
                nc.scalar.copy(sums[g % 2][:, u % NCH * QT:(u % NCH + 1) * QT, :], o_ps[u % O_RING][:, :, 0:DV]
                               ).then_inc(sums_free, 1)

            act.sem_inc(sums_free, O_RING)
            for u in range(EXP_AHEAD):
                exponentials(0, u)
            with act.Fori(0, PAIR_COUNT - 1) as it:
                for u in range(BODY_UNITS):
                    exponentials(it, u + EXP_AHEAD)
                    copy_sums(it, u)
            for u in range(BODY_UNITS):
                if u + EXP_AHEAD < BODY_UNITS:
                    exponentials(PAIR_COUNT - 1, u + EXP_AHEAD)
                copy_sums(PAIR_COUNT - 1, u)

        @block.vector
        def _(dve):
            LATE = 2

            def mask(it, u):
                if u >= BODY_UNITS:
                    it, u = it + 1, u - BODY_UNITS
                hh, g, j = unit(u)
                dve.wait_ge(scores_ready, BODY_UNITS * it + u + 1)
                dve.wait_ge(probs_free, BODY_UNITS * it + u + 1)
                nc.vector.scalar_tensor_tensor(
                    out=probs[u % P_RING][:], in0=s_ps[u % S_RING][:], scalar=-RAW_CLIP,
                    in1=c.clip_mask[:, KT * j:KT * (j + 1), g * QG:(g + 1) * QG],
                    op0=ALU.max, op1=ALU.min).then_inc(masked, 1)

            def take_rest(it, u):
                if POOL_UNITS[u]:
                    return
                dve.wait_ge(probs_ready, BODY_UNITS * it + u + 1)
                p = probs[u % P_RING]
                nc.vector.tensor_tensor(rest[u % P_RING][:], p[:], p[:].bitcast(BF16)[:, :, 1::2], ALU.subtract
                                        ).then_inc(rest_dve, 1)

            def invert(it, g):
                dve.wait_ge(sums_free, O_RING + BODY_UNITS * it + NCH * (g + 1))
                nc.vector.reciprocal(inverse[g % 2][:], sums[g % 2][:, :, DH]).then_inc(inverse_ready, 1)

            def iteration(it, last):
                for u in range(BODY_UNITS):
                    if not (last and u + MASK_AHEAD >= BODY_UNITS):
                        mask(it, u + MASK_AHEAD)
                    take_rest(it, u)
                    g = u // NCH - 1
                    if u % NCH == LATE and g >= 0:
                        invert(it, g)
                    elif u % NCH == LATE and not (isinstance(it, int) and it == 0):
                        invert(it - 1, GROUPS - 1)
                if last:
                    invert(it, GROUPS - 1)

            for u in range(MASK_AHEAD):
                mask(0, u)
            iteration(0, last=False)
            with dve.Fori(1, PAIR_COUNT - 1) as it:
                iteration(it, last=False)
            iteration(PAIR_COUNT - 1, last=True)

        @block.gpsimd
        def _(pool):
            def take_rest(it, u):
                if not POOL_UNITS[u]:
                    return
                pool.wait_ge(probs_ready, BODY_UNITS * it + u + 1)
                p = probs[u % P_RING]
                nc.gpsimd.tensor_tensor(rest[u % P_RING][:], p[:], p[:].bitcast(BF16)[:, :, 1::2], ALU.subtract
                                        ).then_inc(rest_pool, 1)

            def group_steps(it, g):
                count = GROUPS * it + g
                i = g % 2

                def scale():
                    pool.wait_ge(inverse_ready, count + 1)
                    if not (isinstance(count, int) and count == 0):
                        pool.wait_ge(context_ready, count)
                    nc.gpsimd.tensor_tensor(scaled[:], sums[i][:, :, 0:DH],
                                            inverse[i][:].unsqueeze(2).to_broadcast([P, NCH * QT, DH]), ALU.mult
                                            ).then_inc(group_free, 1)

                def halve(level):
                    width = NCH * QT >> level + 1
                    if level == 0:
                        pool.wait_ge(group_free, 2 + count + 1)
                    else:
                        pool.wait_ge(pool_step, (LEVELS - 1) * count + level)
                    if level < LEVELS - 1:
                        nc.gpsimd.tensor_tensor(scaled[:, 0:width, :], scaled[:, 0:width, :],
                                                scaled[:, width:2 * width, :], ALU.add).then_inc(pool_step, 1)
                        return
                    if not (isinstance(it, int) and it == 0 and g < 2):
                        pool.wait_ge(context_stored[i], DMA * (NQ * it + g // 2))
                    nc.gpsimd.tensor_tensor(context[i][:], scaled[:, 0:QT, :], scaled[:, QT:2 * QT, :], ALU.add
                                            ).then_inc(context_ready, 1)

                return [scale] + [lambda level=level: halve(level) for level in range(LEVELS)]

            def iteration(it, last):
                for u in range(BODY_UNITS):
                    take_rest(it, u)
                    g, place = u // NCH - 1, u % NCH - FIRST_STEP
                    if place < 0 or place > LEVELS or (g < 0 and isinstance(it, int) and it == 0):
                        continue
                    (group_steps(it, g) if g >= 0 else group_steps(it - 1, GROUPS - 1))[place]()
                if last:
                    for step in group_steps(it, GROUPS - 1):
                        step()

            FIRST_STEP = NCH - LEVELS - 1
            pool.sem_inc(group_free, 2)
            iteration(0, last=False)
            with pool.Fori(1, PAIR_COUNT - 1) as it:
                iteration(it, last=False)
            iteration(PAIR_COUNT - 1, last=True)


def finish_layer0(nc, c, s, x, B, N):
    NT = N // P
    TILES = NT // 2
    CHUNKS = TILES // 2
    V1 = F + 2 * H
    with ExitStack() as ctx:
        sb, ps, sem = allocators(nc, ctx, "finish0")
        context = [sb(f"context_in{i}", [P, TILES, F], F32) for i in range(2)]
        x_in = [sb(f"x_res{i}", [P, TILES, F], F32) for i in range(2)]
        x_out = [sb(f"x_out{i}", [P, TILES, F], F32) for i in range(2)]
        contextT = [sb(f"contextT{i}", [P, FC, 2, P], F32) for i in range(2)]
        outT = [sb(f"outT{i}", [P, CHUNKS, FC, 2, P], F32) for i in range(2)]
        v1 = [sb(f"v1_{i}", [P, H, TILES, DV], F32) for i in range(2)]
        edge = [sb(f"edge{i}", [P, TILES, 2 * H], F32) for i in range(2)]
        stats = sb("stats", [P, TILES, 6], F32)
        moments = sb("moments", [P, 2, TILES, 2], F32)
        var_eps = sb("var_eps", [P, 2, TILES], F32)
        rstd = sb("rstd", [P, 2, TILES], F32)
        turn_ps = [ps(f"turn_ps{i}", [P, FC, 2, P], F32) for i in range(2)]
        o_ps = [ps(f"proj_ps{i}", [P, 2, F], F32) for i in range(2)]
        out_turn_ps = [ps(f"out_turn_ps{i}", [P, FC, 2, P], F32) for i in range(2)]
        v1_ps = [ps(f"v1_ps{i}", [P, 512], F32) for i in range(2)]

        loaded = [sem(f"loaded{i}") for i in range(2)]
        edges_loaded = sem("edges_loaded")
        turned = sem("turned")
        turned_copied = sem("turned_copied")
        projected = sem("projected")
        biased = sem("biased")
        added = sem("added")
        dve_step = sem("dve_step")
        moments_ready = sem("moments_ready")
        pool_step = sem("pool_step")
        held = sem("held")
        rstd_ready = sem("rstd_ready")
        out_ready = sem("out_ready")
        out_turned = sem("out_turned")
        out_copied = sem("out_copied")
        v1_projected = sem("v1_projected")
        v1_ready = sem("v1_ready")
        ones_ready = sem("ones_ready")
        stored = [sem(f"stored{i}") for i in range(2)]
        sp_held = sem("sp_held")
        block = ctx.enter_context(nc.Block())
        STORES = 3

        @block.sync
        def _(sp):
            def load(b, i):
                if i == 2:
                    b, i = b + 1, 0
                if not (isinstance(b, int) and b == 0):
                    hold(sp, stored[i], STORES * DMA * b, sp_held)
                    hold(sp, turned, CHUNKS * (2 * b + i - 1), sp_held)
                rows = slice(i * TILES * P, (i + 1) * TILES * P)
                for dst, src in ((context[i], s.ctx), (x_in[i], x)):
                    at = src[bass.ds(b, 1), rows, :].rearrange("o (t p) f -> p (o t) f", p=P)
                    sp.dma_start(dst[:], at).then_inc(loaded[i], DMA)

            def store(b, i):
                half = 2 * b + i
                rows = slice(i * TILES * P, (i + 1) * TILES * P)
                hold(sp, out_ready, half + 1, sp_held)
                at = s.x1[bass.ds(b, 1), rows, :].rearrange("o (t p) f -> p (o t) f", p=P)
                sp.dma_start(at, x_out[i][:]).then_inc(stored[i], DMA)
                hold(sp, v1_ready, TILES * (half + 1), sp_held)
                at = s.v1[bass.ds(b, 1), :, :, i * TILES * DV:(i + 1) * TILES * DV]
                sp.dma_start(at.rearrange("o h p w -> p (o h) w"), v1[i][:].rearrange("p h t d -> p h (t d)")
                             ).then_inc(stored[i], DMA)
                at = s.e[bass.ds(b, 1), :, i * TILES * 2 * H:(i + 1) * TILES * 2 * H]
                sp.dma_start(at.rearrange("o p w -> (o p) w"), edge[i][:].rearrange("p t e -> p (t e)")
                             ).then_inc(stored[i], DMA)

            load(0, 0)
            load(0, 1)
            for t in range(0, NT, 4):
                sp.dma_start(c.edge_mask[:, t:t + 4, :], s.edge_mask[:, t:t + 4, :]).then_inc(edges_loaded, DMA)
            if B > 1:
                with sp.Fori(0, B - 1) as b:
                    for i in range(2):
                        store(b, i)
                        load(b + 1, i)
            for i in range(2):
                store(B - 1, i)
            for i in range(2):
                hold(sp, stored[i], STORES * DMA * B, sp_held)
            hold(sp, edges_loaded, NT // 4 * DMA, sp_held)

        @block.gpsimd
        def _(pool):
            last = None
            for i in range(2):
                last = nc.gpsimd.memset(v1[i][:, :, :, DH:DV], 1.0)
            last.then_inc(ones_ready, 1)
            with pool.Fori(0, B) as b:
                for i in range(2):
                    half = 2 * b + i
                    pool.wait_ge(loaded[i], 2 * DMA * (b + 1))
                    nc.gpsimd.tensor_tensor(x_out[i][:], x_in[i][:],
                                            c.beta[:].unsqueeze(1).to_broadcast([P, TILES, F]), ALU.add
                                            ).then_inc(pool_step, 1)
                    pool.wait_ge(pool_step, 3 * half + 1)
                    nc.gpsimd.tensor_tensor(x_in[i][:], x_in[i][:],
                                            c.bo[:].unsqueeze(1).to_broadcast([P, TILES, F]), ALU.add
                                            ).then_inc(biased, 1)
                    for norm in range(2):
                        pool.wait_ge(moments_ready, 2 * half + norm + 1)
                        nc.gpsimd.tensor_tensor(var_eps[:, norm], moments[:, norm, :, 1], c.eps[:, 0:TILES], ALU.add
                                                ).then_inc(pool_step, 1)
                        pool.wait_ge(pool_step, 3 * half + norm + 2)
                        nc.gpsimd.tensor_tensor(rstd[:, norm], var_eps[:, norm], c.minus_half[:, 0:TILES], ALU.pow
                                                ).then_inc(rstd_ready, 1)

        @block.tensor
        def _(pe):
            def front(b, i):
                half = 2 * b + i
                pe.wait_ge(loaded[i], 2 * DMA * (b + 1))

                def turn(k):
                    if k >= 2:
                        pe.wait_ge(turned_copied, CHUNKS * half + k - 1)
                    for fc in range(FC):
                        for t in range(2):
                            mm = nc.tensor.transpose(turn_ps[k % 2][:, fc, t, :],
                                                     context[i][:, 2 * k + t, fc * P:(fc + 1) * P], c.ident[:])
                    mm.then_inc(turned, 1)

                def project(k):
                    pe.wait_ge(turned_copied, CHUNKS * half + k + 1)
                    pe.wait_ge(added, CHUNKS * half + (k - 1 if k >= 2 else 0))
                    for t in range(2):
                        for fc in range(FC):
                            mm = nc.tensor.matmul(o_ps[k % 2][:, t, :], contextT[k % 2][:, fc, t, :],
                                                  c.woT[:, fc, :], start=fc == 0, stop=fc == FC - 1)
                    mm.then_inc(projected, 1)

                turn(0)
                for k in range(CHUNKS):
                    if k + 1 < CHUNKS:
                        turn(k + 1)
                    project(k)

            def back(b, i):
                half = 2 * b + i
                pe.wait_ge(out_ready, half + 1)
                for k in range(CHUNKS):
                    if k >= 2:
                        pe.wait_ge(out_copied, CHUNKS * half + k - 1)
                    for fc in range(FC):
                        for t in range(2):
                            mm = nc.tensor.transpose(out_turn_ps[k % 2][:, fc, t, :],
                                                     x_out[i][:, 2 * k + t, fc * P:(fc + 1) * P], c.ident[:])
                    mm.then_inc(out_turned, 1)
                for t in range(TILES):
                    pe.wait_ge(out_copied, CHUNKS * half + t // 2 + 1)
                    pe.wait_ge(v1_ready, TILES * half + (t - 1 if t >= 2 else 0))
                    for fc in range(FC):
                        mm = nc.tensor.matmul(v1_ps[t % 2][:, 0:V1], outT[i][:, t // 2, fc, t % 2, :],
                                              c.w1[:, fc, :], start=fc == 0, stop=fc == FC - 1)
                    mm.then_inc(v1_projected, 1)

            front(0, 0)
            if B > 1:
                with pe.Fori(0, B - 1) as b:
                    front(b, 1)
                    back(b, 0)
                    front(b + 1, 0)
                    back(b, 1)
            front(B - 1, 1)
            back(B - 1, 0)
            back(B - 1, 1)

        @block.scalar
        def _(act):
            def front(b, i):
                half = 2 * b + i
                for k in range(CHUNKS):
                    count = CHUNKS * half + k
                    act.wait_ge(turned, count + 1)
                    if not (isinstance(count, int) and count < 2):
                        act.wait_ge(projected, count - 1)
                    nc.scalar.copy(contextT[k % 2][:], turn_ps[k % 2][:]).then_inc(turned_copied, 1)

            def back(b, i):
                half = 2 * b + i
                for k in range(CHUNKS):
                    act.wait_ge(out_turned, CHUNKS * half + k + 1)
                    nc.scalar.copy(outT[i][:, k], out_turn_ps[k % 2][:]).then_inc(out_copied, 1)
                if not (isinstance(b, int) and b == 0):
                    act.wait_ge(stored[i], STORES * DMA * b)
                for t in range(TILES):
                    act.wait_ge(v1_projected, TILES * half + t + 1)
                    nc.scalar.copy(edge[i][:, t, :], v1_ps[t % 2][:, F:V1])
                    nc.scalar.copy(v1[i][:, :, t, 0:DH], v1_ps[t % 2][:, 0:F].rearrange("p (h d) -> p h d", h=H)
                                   ).then_inc(v1_ready, 1)

            act.wait_ge(ones_ready, 1)
            front(0, 0)
            if B > 1:
                with act.Fori(0, B - 1) as b:
                    front(b, 1)
                    back(b, 0)
                    front(b + 1, 0)
                    back(b, 1)
            front(B - 1, 1)
            back(B - 1, 0)
            back(B - 1, 1)

        @block.vector
        def _(dve):
            with dve.Fori(0, B) as b:
                for i in range(2):
                    half = 2 * b + i
                    X, G = x_in[i], x_out[i]
                    dve.wait_ge(biased, half + 1)
                    for k in range(CHUNKS):
                        dve.wait_ge(projected, CHUNKS * half + k + 1)
                        nc.vector.tensor_tensor(X[:, 2 * k:2 * k + 2, :], o_ps[k % 2][:], X[:, 2 * k:2 * k + 2, :],
                                                ALU.add).then_inc(added, 1)
                    dve.wait_ge(added, CHUNKS * (half + 1))
                    for norm in range(2):
                        source = (X, G)[norm]
                        for t in range(TILES):
                            last = nc.vector.bn_stats(stats[:, t, :], source[:, t, :])
                        last.then_inc(dve_step, 1)
                        hold(dve, dve_step, 4 * half + 1 + 3 * norm, held)
                        for t in range(TILES):
                            last = nc.vector.bn_aggr(moments[:, norm, t, :], stats[:, t, :])
                        last.then_inc(moments_ready, 1)
                        dve.wait_ge(moments_ready, 2 * half + norm + 1)
                        if norm == 0:
                            for t in range(TILES):
                                last = nc.vector.scalar_tensor_tensor(
                                    out=X[:, t, :], in0=X[:, t, :], scalar=moments[:, 0, t, 0:1], in1=c.gamma[:],
                                    op0=ALU.subtract, op1=ALU.mult)
                            last.then_inc(dve_step, 1)
                            dve.wait_ge(dve_step, 4 * half + 2)
                            dve.wait_ge(rstd_ready, 2 * half + 1)
                            for t in range(TILES):
                                last = nc.vector.scalar_tensor_tensor(
                                    out=G[:, t, :], in0=X[:, t, :], scalar=rstd[:, 0, t:t + 1], in1=G[:, t, :],
                                    op0=ALU.mult, op1=ALU.add)
                            last.then_inc(dve_step, 1)
                            dve.wait_ge(dve_step, 4 * half + 3)
                        else:
                            dve.wait_ge(rstd_ready, 2 * half + 2)
                            for t in range(TILES):
                                last = nc.vector.tensor_scalar(G[:, t, :], G[:, t, :], moments[:, 1, t, 0:1],
                                                               rstd[:, 1, t:t + 1], ALU.subtract, ALU.mult)
                            last.then_inc(out_ready, 1)


def prepare_layer1(nc, c, s, B, N):
    NT = N // P
    COLS = B * H * NT
    BLOCKS = COLS // P
    MM = 512
    with ExitStack() as ctx:
        sb, ps, sem = allocators(nc, ctx, "prepare1")
        edge = sb("edge_all", [P, B, NT, 2 * H], F32)
        highest = sb("highest", [P, B, H], F32)
        top = sb("top", [P, B, H], F32)
        src = sb("src", [P, B, H, NT], F32)
        d = sb("d", [P, B, H, NT], F32)
        total = sb("s_plus", [P, B, H, NT], F32)
        small = sb("s_small", [P, B, H, NT], F32)
        largest = sb("m", [P, B, H, NT], F32)
        exponents = sb("exponents", [P, 2, B, H, NT], F32)
        factors = sb("factors", [P, B, H, FACTORS, NT], F32)
        rows = sb("src_rows_sb", [P, BLOCKS, P], F32)
        ones = sb("ones16", [P, P], BF16)
        rows_ps = ps("rows_ps", [P, BLOCKS, P], F32)
        degree = ps("degree", [P, N], F32)
        loaded = sem("edge_loaded")
        highest_ready = sem("highest_ready")
        top_ready = sem("top_ready")
        src_ready = sem("src_ready")
        dve_step = sem("dve_step")
        exponents_ready = sem("exponents_ready")
        exp_ready = sem("exp_ready")
        ones_ready = sem("ones_ready")
        degree_ready = sem("degree_ready")
        rows_ready = sem("rows_ready")
        rows_copied = sem("rows_copied")
        no_edge_ready = sem("no_edge_ready")
        stored = sem("stored")
        sp_held = sem("sp_held")
        block = ctx.enter_context(nc.Block())

        @block.sync
        def _(sp):
            sp.dma_start(edge[:].rearrange("p b t e -> p b (t e)"), s.e[:, :, :].rearrange("b p w -> p b w")
                         ).then_inc(loaded, DMA)
            hold(sp, rows_copied, 1, sp_held)
            width = min(P, COLS)
            sp.dma_start(s.src[:, :].rearrange("(k p) w -> p k w", p=width), rows[0:width]).then_inc(stored, DMA)
            hold(sp, exp_ready, 4, sp_held)
            for b in range(B):
                sp.dma_start(s.factors[b].rearrange("h p w -> p h w"),
                             factors[:, b].rearrange("p h k t -> p h (k t)")).then_inc(stored, DMA)
            hold(sp, stored, (B + 1) * DMA, sp_held)

        @block.gpsimd
        def _(pool):
            nc.gpsimd.memset(ones[:], 1.0).then_inc(ones_ready, 1)
            pool.wait_ge(highest_ready, 1)
            nc.gpsimd.partition_all_reduce(top[:].rearrange("p b h -> p (b h)"),
                                           highest[:].rearrange("p b h -> p (b h)"), P, REDUCE_MAX
                                           ).then_inc(top_ready, 1)

        @block.tensor
        def _(pe):
            pe.wait_ge(ones_ready, 1)
            for j in range(NT):
                for q in range(N // MM):
                    mm = nc.tensor.matmul(degree[:, q * MM:(q + 1) * MM], ones[:],
                                          c.edge_mask[:, j, q * MM:(q + 1) * MM], start=j == 0, stop=j == NT - 1)
            mm.then_inc(degree_ready, 1)
            pe.wait_ge(src_ready, 1)
            for k in range(BLOCKS):
                mm = nc.tensor.transpose(rows_ps[:, k, :],
                                         src[:].rearrange("p b h t -> p (b h t)")[:, k * P:(k + 1) * P], c.ident[:])
            mm.then_inc(rows_ready, 1)

        @block.scalar
        def _(act):
            act.wait_ge(rows_ready, 1)
            nc.scalar.copy(rows[:], rows_ps[:]).then_inc(rows_copied, 1)
            act.wait_ge(exponents_ready, 1)
            for k, source, scale, bias in ((0, d[:], 1.0, c.source_bias[:]), (1, d[:], SLOPE, c.source_bias[:]),
                                           (3, exponents[:, 0], 1.0, 0.0), (4, exponents[:, 1], 1.0, 0.0)):
                nc.scalar.activation(factors[:, :, :, k, :].rearrange("p b h t -> p (b h) t"),
                                     source.rearrange("p b h t -> p (b h) t"), ACT.Exp, bias=bias, scale=scale
                                     ).then_inc(exp_ready, 1)

        @block.vector
        def _(dve):
            dve.wait_ge(loaded, DMA)
            dst = edge[:, :, :, H:2 * H].rearrange("p b t h -> p b h t")
            for b in range(B):
                last = nc.vector.tensor_reduce(highest[:, b], dst[:, b], AXIS_FREE, ALU.max)
            last.then_inc(highest_ready, 1)
            for b in range(B):
                last = nc.vector.tensor_copy(src[:, b], edge[:, b, :, 0:H].rearrange("p t h -> p h t"))
            last.then_inc(src_ready, 1)
            for b in range(B):
                last = nc.vector.tensor_scalar(factors[:, b, :, 2, :], dst[:, b], STEEP, None, ALU.mult)
            dve.wait_ge(top_ready, 1)
            dve.wait_ge(src_ready, 1)
            for b in range(B):
                at = top[:, b].unsqueeze(2).to_broadcast([P, H, NT])
                nc.vector.tensor_tensor(d[:, b], dst[:, b], at, ALU.subtract)
                last = nc.vector.tensor_tensor(total[:, b], src[:, b], at, ALU.add)
            last.then_inc(dve_step, 1)
            dve.wait_ge(dve_step, 1)
            nc.vector.tensor_scalar(small[:], total[:], SLOPE, None, ALU.mult).then_inc(dve_step, 1)
            dve.wait_ge(dve_step, 2)
            nc.vector.tensor_tensor(largest[:], total[:], small[:], ALU.max).then_inc(dve_step, 1)
            dve.wait_ge(dve_step, 3)
            nc.vector.tensor_tensor(exponents[:, 0], total[:], largest[:], ALU.subtract)
            nc.vector.tensor_tensor(exponents[:, 1], small[:], largest[:], ALU.subtract).then_inc(exponents_ready, 1)
            dve.wait_ge(degree_ready, 1)
            nc.vector.tensor_scalar(c.no_edge[:], degree[:], 0.0, None, ALU.is_equal).then_inc(no_edge_ready, 1)
            dve.wait_ge(no_edge_ready, 1)


def attend_layer1(nc, c, s, out, B, N):
    NT = N // P
    TH = NT // 2
    W = N // 2
    GROUPS = 2 * H
    BODY_UNITS = GROUPS * NT
    R_RING, G_RING = 4, 8
    R_AHEAD = 2
    NEG_LAG = 4
    LATE = NEG_LAG + 4
    BANK_T = 4
    BANKS = max(TH // BANK_T, 1)
    assert BODY_UNITS % G_RING == 0 and LATE <= NT and TH == BANKS * BANK_T and B > 2
    with ExitStack() as ctx:
        sb, ps, sem = allocators(nc, ctx, "attend1")
        src_row = [sb(f"src_row{i}", [P, N], F32) for i in range(2)]
        factors = [sb(f"factors{i}", [P, FACTORS, NT], F32) for i in range(2)]
        values = [sb(f"values{i}", [P, NT, DV], F32) for i in range(2)]
        product = sb("product", [P, NT, DV], F32)
        high = [sb(f"high{i}", [P, 2, NT, DV], BF16) for i in range(2)]
        low_half = [sb(f"low_half{i}", [P, 2, NT, DV], F16) for i in range(2)]
        total = sb("total", [P, NT // 2, DV], F32)
        total_high = [sb(f"total_high{i}", [P, DV], BF16) for i in range(2)]
        total_low = [sb(f"total_low{i}", [P, DV], F16) for i in range(2)]
        steep = [sb(f"steep{i}", [P, W], BF16) for i in range(R_RING)]
        positive = [sb(f"positive{i}", [P, W], BF16) for i in range(G_RING)]
        negative = [sb(f"negative{i}", [P, W], BF16) for i in range(G_RING)]
        scaled = [sb(f"scaled{i}", [P, 2, TH, DV], F32) for i in range(2)]
        inverse = sb("inverse", [P, TH], F32)
        hidden = sb("hidden", [P, NT, F], F32)
        x1 = sb("x1", [P, TH, F], F32)
        low = sb("low", [P, TH, F], F32)
        stats = sb("stats", [P, TH, 6], F32)
        moments = sb("moments", [P, TH, 2], F32)
        var_eps = sb("var_eps", [P, TH], F32)
        rstd = sb("rstd", [P, TH], F32)
        shift = sb("shift", [P, TH], F32)
        acc = [[[ps(f"acc{i}_{sign}_{k}", [P, BANK_T, P], F32) for k in range(BANKS)] for sign in range(2)]
               for i in range(2)]

        loaded = [sem(f"head_loaded{i}") for i in range(2)]
        x1_loaded = sem("x1_loaded")
        pool_step = sem("pool_step")
        split_part = sem("split_part")
        total_part = sem("total_part")
        split_ready = sem("split_ready")
        steep_ready = sem("steep_ready")
        positive_ready = sem("positive_ready")
        negative_dve = sem("negative_dve")
        negative_pool = sem("negative_pool")
        matrices_free = sem("matrices_free")
        group_summed = sem("group_summed")
        sums_scaled = sem("sums_scaled")
        group_added = sem("group_added")
        inverse_ready = sem("inverse_ready")
        group_ready = sem("group_ready")
        low_ready = sem("low_ready")
        low_exp = sem("low_exp")
        dve_step = sem("dve_step")
        moments_ready = sem("moments_ready")
        variance_ready = sem("variance_ready")
        held = sem("held")
        rstd_ready = sem("rstd_ready")
        shift_ready = sem("shift_ready")
        normed = sem("normed")
        stored = sem("out_stored")
        sp_held = sem("sp_held")
        block = ctx.enter_context(nc.Block())

        def wrapped(b, u):
            return (b + 1, u - BODY_UNITS) if u >= BODY_UNITS else (b, u)

        def place(u):
            return u // (2 * NT), u // NT % 2, u % NT

        POOL_UNITS = [u % NT % 4 == 1 for u in range(BODY_UNITS)]

        def negative_count(b, u):
            mine = [x == POOL_UNITS[u] for x in POOL_UNITS]
            return (negative_pool if POOL_UNITS[u] else negative_dve), sum(mine) * b + sum(mine[:u + 1])

        @block.sync
        def _(sp):
            def load_head(b, h):
                i = h % 2
                head = H * b + h
                bb, hh = (b, h) if h < H else (b + 1, h - H)
                if not (isinstance(head, int) and head < 2):
                    hold(sp, steep_ready, 2 * NT * (head - 1), sp_held)
                    hold(sp, split_ready, head - 1, sp_held)
                    hold(sp, sums_scaled, 2 + 2 * (head - 1), sp_held)
                at = s.src[bass.ds(head * NT, NT), :].rearrange("t p -> (t p)").partition_broadcast(P)
                sp.dma_start(src_row[i][:], at).then_inc(loaded[i], DMA)
                at = s.factors[bass.ds(bb, 1), hh].rearrange("o p w -> (o p) w")
                sp.dma_start(factors[i][:].rearrange("p k t -> p (k t)"), at).then_inc(loaded[i], DMA)
                at = s.v1[bass.ds(bb, 1), hh].rearrange("o p w -> (o p) w")
                sp.dma_start(values[i][:].rearrange("p t d -> p (t d)"), at).then_inc(loaded[i], DMA)

            def half_of(t, b, k):
                return t[bass.ds(b, 1), k * TH * P:(k + 1) * TH * P, :].rearrange("o (t p) f -> p (o t) f", p=P)

            def load_x1(b, k):
                sp.dma_start(x1[:], half_of(s.x1, b, k)).then_inc(x1_loaded, DMA)

            def finish_batch(b, last):
                for k in range(2):
                    hold(sp, moments_ready, 2 * b + k + 1, sp_held)
                    if k == 0:
                        load_x1(b, 1)
                    elif not last:
                        load_x1(b + 1, 0)
                    hold(sp, normed, 2 * b + k + 1, sp_held)
                    sp.dma_start(half_of(out, b, k), low[:]).then_inc(stored, DMA)

            load_head(0, 0)
            load_x1(0, 0)
            for h in range(H):
                load_head(0, h + 1)
            with sp.Fori(1, B - 1) as b:
                load_head(b, 1)
                finish_batch(b - 1, last=False)
                for h in range(1, H):
                    load_head(b, h + 1)
            load_head(B - 1, 1)
            finish_batch(B - 2, last=False)
            for h in range(1, H - 1):
                load_head(B - 1, h + 1)
            finish_batch(B - 1, last=True)
            hold(sp, stored, 2 * DMA * B, sp_held)

        @block.gpsimd
        def _(pool):
            LEVELS = (NT // 2).bit_length()
            STEPS = 4 + LEVELS
            STRIDE = NT // 8

            def head_steps(b, h):
                i = h % 2
                head = H * b + h
                v = values[i]

                def multiply(k):
                    if k == 0:
                        pool.wait_ge(loaded[i], 3 * DMA * (H // 2 * b + h // 2 + 1))
                        if not (isinstance(head, int) and head < 2):
                            pool.wait_ge(sums_scaled, 2 + 2 * (head - 1))
                    if k == 0 and not (isinstance(head, int) and head == 0):
                        pool.wait_ge(pool_step, STEPS * head)
                    elif k == 1:
                        pool.wait_ge(pool_step, STEPS * head + 2)
                    nc.gpsimd.tensor_tensor(product[:], v[:], factors[i][:, k, :].unsqueeze(2).to_broadcast(
                        [P, NT, DV]), ALU.mult).then_inc(split_part, 1)
                    hold(pool, split_part, 2 * head + k + 1, held)

                def take_high(k):
                    nc.gpsimd.tensor_copy(high[i][:, k], product[:]).then_inc(pool_step, 1)

                def rest(k):
                    pool.wait_ge(pool_step, STEPS * head + 2 * k + 1)
                    nc.gpsimd.tensor_tensor(low_half[i][:, k], product[:], high[i][:, k], ALU.subtract
                                            ).then_inc(pool_step, 1)

                def add_all():
                    width = NT // 2
                    nc.gpsimd.tensor_tensor(total[:, 0:width], v[:, 0:width, :], v[:, width:2 * width, :],
                                            ALU.add).then_inc(pool_step, 1)
                    for level in range(1, LEVELS):
                        width //= 2
                        pool.wait_ge(pool_step, STEPS * head + 4 + level)
                        nc.gpsimd.tensor_tensor(total[:, 0:width], total[:, 0:width], total[:, width:2 * width],
                                                ALU.add).then_inc(pool_step, 1)
                    hold(pool, pool_step, STEPS * (head + 1), held)
                    nc.gpsimd.tensor_copy(total_high[i][:], total[:, 0]).then_inc(total_part, 1)
                    pool.wait_ge(total_part, head + 1)
                    nc.gpsimd.tensor_tensor(total_low[i][:], total[:, 0], total_high[i][:], ALU.subtract
                                            ).then_inc(split_ready, 1)

                return [lambda: (multiply(0), take_high(0)), lambda: rest(0), lambda: (multiply(1), take_high(1)),
                        lambda: rest(1), add_all]

            def take_negative(b, u):
                h, half, j = place(u)
                pool.wait_ge(positive_ready, BODY_UNITS * b + u + 1)
                pool.wait_ge(matrices_free, BODY_UNITS * b + u + 1)
                nc.gpsimd.tensor_tensor(negative[u % G_RING][:], c.edge_mask[:, j, half * W:(half + 1) * W],
                                        positive[u % G_RING][:], ALU.subtract).then_inc(negative_pool, 1)

            def take_group(b, g):
                h, i = g // 2, g % 2
                count = GROUPS * b + g
                pool.wait_ge(sums_scaled, 2 + count + 1)
                nc.gpsimd.tensor_tensor(scaled[i][:, 0], scaled[i][:, 0], scaled[i][:, 1], ALU.add
                                        ).then_inc(group_added, 1)
                if g == 0 and not (isinstance(b, int) and b == 0):
                    pool.wait_ge(normed, 2 * b)
                pool.wait_ge(inverse_ready, count + 1)
                nc.gpsimd.tensor_tensor(hidden[:, i * TH:(i + 1) * TH, h * DH:(h + 1) * DH], scaled[i][:, 0, :, 0:DH],
                                        inverse[:].unsqueeze(2).to_broadcast([P, TH, DH]), ALU.mult
                                        ).then_inc(group_ready, 1)

            def take_low(b, k):
                if k == 0:
                    hold(pool, group_ready, GROUPS * (b + 1), held)
                if not (isinstance(b, int) and b == 0 and k == 0):
                    hold(pool, stored, DMA * (2 * b + k), held)
                nc.gpsimd.tensor_scalar(low[:], hidden[:, k * TH:(k + 1) * TH], 0.0, None, ALU.min
                                        ).then_inc(low_ready, 1)

            def take_rstd(b, k):
                pool.wait_ge(moments_ready, 2 * b + k + 1)
                nc.gpsimd.tensor_tensor(var_eps[:], moments[:, :, 1], c.eps[:, 0:TH], ALU.add
                                        ).then_inc(variance_ready, 1)
                pool.wait_ge(variance_ready, 2 * b + k + 1)
                nc.gpsimd.tensor_tensor(rstd[:], var_eps[:], c.minus_half[:, 0:TH], ALU.pow).then_inc(rstd_ready, 1)

            def batch(b, first=False, last=False):
                for u in range(BODY_UNITS):
                    h, half, j = place(u)
                    if POOL_UNITS[u]:
                        take_negative(b, u)
                    if half == 1 and j % STRIDE == 0 and j // STRIDE < 5 and not (last and h == H - 1):
                        (head_steps(b, h + 1) if h + 1 < H else head_steps(b + 1, 0))[j // STRIDE]()
                    g = u // NT - 1
                    if j == LATE - 1 and g >= 0:
                        take_group(b, g)
                    elif j == LATE - 1 and not first:
                        take_group(b - 1, GROUPS - 1)
                        tail(b - 1)
                if last:
                    take_group(b, GROUPS - 1)
                    tail(b)

            def tail(b):
                for k in range(2):
                    take_low(b, k)
                    take_rstd(b, k)

            for step in head_steps(0, 0):
                step()
            batch(0, first=True)
            with pool.Fori(1, B - 1) as b:
                batch(b)
            batch(B - 1, last=True)

        @block.tensor
        def _(pe):
            def matrix(b, u, sign):
                h, half, j = place(u)
                if j == 0 and sign == 0:
                    if half == 0:
                        pe.wait_ge(split_ready, H * b + h + 1)
                    pe.wait_ge(sums_scaled, GROUPS * b + 2 * h + half + 1)
                if sign == 0:
                    pe.wait_ge(positive_ready, BODY_UNITS * b + u + 1)
                else:
                    ready, count = negative_count(b, u)
                    pe.wait_ge(ready, count)
                w = (positive, negative)[sign][u % G_RING]
                for t in range(TH):
                    to = acc[half][sign][t // BANK_T][:, t % BANK_T, 0:DV]
                    for part in range(2):
                        mm = nc.tensor.matmul(to, w[:, t * P:(t + 1) * P], (high, low_half)[part][h % 2][:, sign, j, :],
                                              start=j == 0 and part == 0 and t % BANK_T == 0, stop=False,
                                              skip_group_check=True)
                if sign == 1:
                    mm.then_inc(matrices_free, 1)
                if j == NT - 1:
                    for t in range(TH):
                        to = acc[half][sign][t // BANK_T][:, t % BANK_T, 0:DV]
                        tile = (half * TH + t) * P
                        for part in range(2):
                            mm = nc.tensor.matmul(to, c.no_edge[:, tile:tile + P], (total_high, total_low)[part][h % 2][:],
                                                  start=False, stop=part == 1 and t % BANK_T == BANK_T - 1,
                                                  skip_group_check=True)
                    if sign == 1:
                        mm.then_inc(group_summed, 1)

            pe.sem_inc(matrices_free, G_RING)
            for u in range(NEG_LAG):
                matrix(0, u, 0)
            with pe.Fori(0, B - 1) as b:
                for u in range(BODY_UNITS):
                    matrix(*wrapped(b, u + NEG_LAG), 0)
                    matrix(b, u, 1)
            for u in range(BODY_UNITS):
                if u + NEG_LAG < BODY_UNITS:
                    matrix(B - 1, u + NEG_LAG, 0)
                matrix(B - 1, u, 1)

        @block.scalar
        def _(act):
            def unit(b, u):
                h, half, j = place(u)
                if half == 0 and j == 0:
                    act.wait_ge(loaded[h % 2], 3 * DMA * (H // 2 * b + h // 2 + 1))
                if not (isinstance(b, int) and b == 0 and u < R_RING):
                    act.wait_ge(positive_ready, BODY_UNITS * b + u - R_RING + 1)
                nc.scalar.activation(steep[u % R_RING][:], src_row[h % 2][:, half * W:(half + 1) * W], ACT.Relu,
                                     bias=factors[h % 2][:, 2, j:j + 1], scale=STEEP).then_inc(steep_ready, 1)

            def exponential(b, k):
                act.wait_ge(low_ready, 2 * b + k + 1)
                nc.scalar.activation(low[:], low[:], ACT.Exp).then_inc(low_exp, 1)

            def norm(b, k):
                act.wait_ge(shift_ready, 2 * b + k + 1)
                for t in range(TH):
                    last = nc.scalar.activation(low[:, t, :], hidden[:, k * TH + t, :], ACT.Identity,
                                                bias=shift[:, t:t + 1], scale=rstd[:, t:t + 1])
                last.then_inc(normed, 1)

            TAIL = {LATE + 4: lambda b: exponential(b, 0), LATE + 7: lambda b: (norm(b, 0), exponential(b, 1)),
                    LATE + 10: lambda b: norm(b, 1)}

            def batch(b, first=False):
                for u in range(BODY_UNITS):
                    unit(b, u)
                    if u in TAIL and not first:
                        TAIL[u](b - 1)

            batch(0, first=True)
            with act.Fori(1, B) as b:
                batch(b)
            for part in TAIL.values():
                part(B - 1)

        @block.vector
        def _(dve):
            def unit(b, u):
                h, half, j = place(u)
                dve.wait_ge(steep_ready, BODY_UNITS * b + u + 1)
                dve.wait_ge(matrices_free, BODY_UNITS * b + u + 1)
                edges = c.edge_mask[:, j, half * W:(half + 1) * W]
                nc.vector.tensor_tensor(positive[u % G_RING][:], steep[u % R_RING][:], edges, ALU.min
                                        ).then_inc(positive_ready, 1)

            def take_negative(b, u):
                if POOL_UNITS[u]:
                    return
                h, half, j = place(u)
                edges = c.edge_mask[:, j, half * W:(half + 1) * W]
                dve.wait_ge(positive_ready, BODY_UNITS * b + u + 1)
                nc.vector.tensor_tensor(negative[u % G_RING][:], edges, positive[u % G_RING][:], ALU.subtract
                                        ).then_inc(negative_dve, 1)

            def scale_sums(b, g):
                h, i = g // 2, g % 2
                count = GROUPS * b + g
                dve.wait_ge(group_summed, count + 1)
                if not (isinstance(count, int) and count < 2):
                    dve.wait_ge(group_ready, count - 1)
                for sign in range(2):
                    factor = factors[h % 2][:, 3 + sign, i * TH:(i + 1) * TH].unsqueeze(2)
                    for k in range(BANKS):
                        tiles = slice(k * BANK_T, (k + 1) * BANK_T)
                        last = nc.vector.tensor_tensor(
                            scaled[i][:, sign, tiles, :], acc[i][sign][k][:, :, 0:DV],
                            factor[:, tiles].to_broadcast([P, BANK_T, DV]), ALU.mult)
                last.then_inc(sums_scaled, 1)

            def invert(b, g):
                count = GROUPS * b + g
                dve.wait_ge(group_added, count + 1)
                if not (isinstance(count, int) and count == 0):
                    dve.wait_ge(group_ready, count)
                nc.vector.reciprocal(inverse[:], scaled[g % 2][:, 0, :, DH]).then_inc(inverse_ready, 1)

            def residual(b, k):
                step = 3 * (2 * b + k)
                part = hidden[:, k * TH:(k + 1) * TH]
                dve.wait_ge(low_exp, 2 * b + k + 1)
                nc.vector.scalar_tensor_tensor(out=part, in0=part, scalar=0.0, in1=low[:], op0=ALU.max, op1=ALU.add
                                               ).then_inc(dve_step, 1)
                dve.wait_ge(dve_step, step + 1)
                dve.wait_ge(x1_loaded, DMA * (2 * b + k + 1))
                nc.vector.scalar_tensor_tensor(out=part, in0=part, scalar=-1.0, in1=x1[:], op0=ALU.add, op1=ALU.add
                                               ).then_inc(dve_step, 1)
                dve.wait_ge(dve_step, step + 2)
                for t in range(TH):
                    last = nc.vector.bn_stats(stats[:, t, :], hidden[:, k * TH + t, :])
                last.then_inc(dve_step, 1)
                hold(dve, dve_step, step + 3, held)
                for t in range(TH):
                    last = nc.vector.bn_aggr(moments[:, t, :], stats[:, t, :])
                last.then_inc(moments_ready, 1)

            def take_shift(b, k):
                dve.wait_ge(rstd_ready, 2 * b + k + 1)
                nc.vector.scalar_tensor_tensor(out=shift[:], in0=moments[:, :, 0], scalar=-1.0, in1=rstd[:],
                                               op0=ALU.mult, op1=ALU.mult).then_inc(shift_ready, 1)

            TAIL = {LATE + 2: lambda b: residual(b, 0), LATE + 3: lambda b: take_shift(b, 0),
                    LATE + 5: lambda b: residual(b, 1), LATE + 6: lambda b: take_shift(b, 1)}

            def batch(b, first=False, last=False):
                for u in range(BODY_UNITS):
                    if not (last and u + R_AHEAD >= BODY_UNITS):
                        unit(*wrapped(b, u + R_AHEAD))
                    take_negative(b, u)
                    j = u % NT
                    g = u // NT - 1
                    if g >= 0 or not first:
                        at = (b, g) if g >= 0 else (b - 1, GROUPS - 1)
                        if j == LATE - 2:
                            scale_sums(*at)
                        if j == LATE - 1:
                            invert(*at)
                    if u in TAIL and not first:
                        TAIL[u](b - 1)

            dve.sem_inc(sums_scaled, 2)
            for u in range(R_AHEAD):
                unit(0, u)
            batch(0, first=True)
            with dve.Fori(1, B - 1) as b:
                batch(b)
            batch(B - 1, last=True)
            scale_sums(B - 1, GROUPS - 1)
            invert(B - 1, GROUPS - 1)
            for part in TAIL.values():
                part(B - 1)


def program(nc, x, adj, weights, out):
    B, N, _ = x.shape
    s = Scratch(nc, B, N)
    with ExitStack() as ctx:
        c = Constants(nc, ctx)
        with ExitStack() as layer0:
            c.for_layer0(nc, layer0, N)
            prepare_weights(nc, c, weights)
            project_layer0(nc, c, s, x, adj, B, N)
            attend_layer0(nc, c, s, B, N)
        c.for_layer1(nc, ctx, N)
        finish_layer0(nc, c, s, x, B, N)
        prepare_layer1(nc, c, s, B, N)
        attend_layer1(nc, c, s, out, B, N)


_WEIGHTS = {"Wq": "L0_gnn_Wq", "bq": "L0_gnn_bq", "Wk": "L0_gnn_Wk", "bk": "L0_gnn_bk", "Wv": "L0_gnn_Wv",
            "bv": "L0_gnn_bv", "Wo": "L0_gnn_Wo", "bo": "L0_gnn_bo", "gamma": "L0_gnn_gamma",
            "beta": "L0_gnn_beta", "W": "L1_gnn_W", "a": "L1_gnn_a"}


def kernel(**inputs):
    import numpy as np
    from concourse import bacc
    from concourse.bass_utils import run_bass_kernel_spmd

    nc = bacc.Bacc("TRN2", target_bir_lowering=False, num_devices=1)
    arrays, aps = {}, {}
    for name in ("x", "adj", *_WEIGHTS.values()):
        a = np.ascontiguousarray(inputs[name])
        arrays[f"in_{name}"] = a
        aps[name] = nc.dram_tensor(f"in_{name}", a.shape, mybir.dt.from_np(a.dtype), kind="ExternalInput").ap()
    out = nc.dram_tensor("out", aps["x"].shape, F32, kind="ExternalOutput").ap()
    program(nc, aps["x"], aps["adj"], {short: aps[name] for short, name in _WEIGHTS.items()}, out)
    r = run_bass_kernel_spmd(nc, [arrays], core_ids=[0])
    return r.results[0]["out"]
```

```python
import math
from contextlib import ExitStack

import concourse.bass as bass
from concourse import mybir

ALU = mybir.AluOpType
ACT = mybir.ActivationFunctionType
AXIS_FREE = mybir.AxisListType.X
F32 = mybir.dt.float32
F16 = mybir.dt.float16
BF16 = mybir.dt.bfloat16
I32 = mybir.dt.int32
I8 = mybir.dt.int8
REDUCE_MAX = bass.bass_isa.ReduceOp.max

P = 128
F = 256
FC = F // P
H = 4
DH = F // H
DV = DH + 1
PAIRS = H // 2
CHUNK = 256
KT = CHUNK // P
QG = 512
QT = QG // P
CLIP = 10.0
SCALE = float(DH) ** -0.5
RAW_CLIP = CLIP / SCALE
EXP_BIAS = CLIP - 6 * math.log(2.0)
SOURCE_BIAS = 12 * math.log(2.0)
EPS = 1e-5
SLOPE = 0.2
STEEP = 2.0 ** 100
FACTORS = 6
STEEP_DST = 3
TARGET = 4
DMA = 16


def allocators(nc, ctx, phase):
    def sb(name, shape, dt):
        return ctx.enter_context(nc.sbuf_tensor(f"{phase}_{name}", shape, dt))

    def ps(name, shape, dt):
        return ctx.enter_context(nc.psum_tensor(f"{phase}_{name}", shape, dt))

    def sem(name):
        return ctx.enter_context(nc.semaphore(f"{phase}_{name}"))

    return sb, ps, sem


def hold(engine, semaphore, value, held):
    engine.wait_ge(semaphore, value)
    engine.sem_inc(held, 1)


class Scratch:

    def __init__(self, nc, B, N):
        NT = N // P
        self.q = nc.dram_tensor("q_split", [B, PAIRS, 2, P, N], F16, kind="Internal")
        self.k = nc.dram_tensor("k_split", [B, PAIRS, 2, P, N], F16, kind="Internal")
        self.v = nc.dram_tensor("v_split", [B, H, P, NT * 2 * DV], F16, kind="Internal")
        self.v32 = nc.dram_tensor("v_whole", [B, H, P, NT * DV], F32, kind="Internal")
        self.edge_mask = nc.dram_tensor("edge_mask_16", [P, NT, N], BF16, kind="Internal")
        self.ctx = nc.dram_tensor("context", [B, N, F], F32, kind="Internal")
        self.x1 = nc.dram_tensor("x_layer1", [B, N, F], F32, kind="Internal")
        self.v1 = nc.dram_tensor("v1_ones", [B, H, P, NT * DV], F32, kind="Internal")
        self.e = nc.dram_tensor("edge_terms", [B, P, NT * 2 * H], F32, kind="Internal")
        self.src = nc.dram_tensor("src_rows", [B * H * NT, P], F32, kind="Internal")
        self.factors = nc.dram_tensor("factors", [B, H, P, FACTORS * NT], F32, kind="Internal")


class Constants:

    def __init__(self, nc, ctx):
        sb, ps, sem = allocators(nc, ctx, "const")
        self.ident = sb("ident", [P, P], F32)
        self.ident16 = sb("ident16", [P, P], BF16)
        self.woT = sb("woT", [P, FC, F], F32)
        self.w1 = sb("w1", [P, FC, F + 2 * H], F32)
        self.bo = sb("bo", [P, F], F32)
        self.gamma = sb("gamma", [P, F], F32)
        self.beta = sb("beta", [P, F], F32)
        self.minus_half = sb("minus_half", [P, 16], F32)
        self.eps = sb("eps", [P, 16], F32)
        self.exp_bias = sb("exp_bias", [P, 1], F32)
        self.minus_one = sb("minus_one", [P, 1], F32)
        self.source_bias = sb("source_bias", [P, 1], F32)

    def for_layer0(self, nc, ctx, N):
        sb, ps, sem = allocators(nc, ctx, "layer0")
        self.clip_mask = sb("clip_mask", [P, N // P, N], I8)
        self.wqT = sb("wqT", [P, FC, F], F32)
        self.wkT = sb("wkT", [P, FC, F], F32)
        self.wvT = sb("wvT", [P, FC, F], F32)
        self.bq = sb("bq", [P, PAIRS], F32)
        self.bk = sb("bk", [P, PAIRS], F32)
        self.bv = sb("bv", [P, F], F32)

    def for_layer1(self, nc, ctx, N):
        sb, ps, sem = allocators(nc, ctx, "layer1")
        self.edge_mask = sb("edge_mask", [P, N // P, N], BF16)
        self.no_edge = sb("no_edge", [P, N], BF16)


def prepare_weights(nc, c, w):
    with ExitStack() as ctx:
        sb, ps, sem = allocators(nc, ctx, "weights")
        raw = sb("raw_weights", [P, 4, FC, F], F32)
        a_rows = sb("a_rows", [P, 2, DH], F32)
        product = sb("product", [P, 2, FC * H, DH], F32)
        turned = [ps(f"turned{i}", [P, FC, F], F32) for i in range(4)]
        raw_loaded = sem("raw_loaded")
        w1_loaded = sem("w1_loaded")
        rows_loaded = sem("rows_loaded")
        cleared = sem("cleared")
        ident_ready = sem("ident_ready")
        turned_ready = sem("turned_ready")
        copied = sem("copied")
        product_ready = sem("product_ready")
        sp_held = sem("sp_held")
        block = ctx.enter_context(nc.Block())

        @block.sync
        def _(sp):
            for m, name in enumerate(("Wq", "Wk", "Wv", "Wo")):
                sp.dma_start(raw[:, m], w[name].rearrange("(c p) f -> p c f", p=P)).then_inc(raw_loaded, DMA)
            sp.dma_start(c.w1[:, :, 0:F], w["W"].rearrange("(c p) f -> p c f", p=P)).then_inc(w1_loaded, DMA)
            sp.dma_start(a_rows[:].rearrange("p s d -> p (s d)"), w["a"].partition_broadcast(P)).then_inc(w1_loaded, DMA)
            for dst, name in ((c.bv, "bv"), (c.bo, "bo"), (c.gamma, "gamma"), (c.beta, "beta")):
                sp.dma_start(dst[:], w[name].partition_broadcast(P)).then_inc(rows_loaded, DMA)
            with nc.allow_non_contiguous_dma(reason="two small bias columns"):
                for dst, name in ((c.bq, "bq"), (c.bk, "bk")):
                    sp.dma_start(dst[:], w[name].rearrange("(c p) -> p c", p=P)).then_inc(rows_loaded, DMA)
            hold(sp, rows_loaded, 6 * DMA, sp_held)

        @block.gpsimd
        def _(pool):
            nc.gpsimd.memset(c.minus_half[:], -0.5)
            nc.gpsimd.memset(c.eps[:], EPS)
            nc.gpsimd.memset(c.exp_bias[:], EXP_BIAS)
            nc.gpsimd.memset(c.minus_one[:], -1.0)
            nc.gpsimd.memset(c.source_bias[:], SOURCE_BIAS)
            nc.gpsimd.memset(c.ident16[:], 0.0)
            nc.gpsimd.memset(c.ident[:], 0.0).then_inc(cleared, 1)
            pool.wait_ge(cleared, 1)
            nc.gpsimd.affine_select(out=c.ident16[:], in_=c.ident16[:], compare_op=ALU.not_equal, fill=1.0,
                                    base=0, pattern=[[-1, P]], channel_multiplier=1)
            nc.gpsimd.affine_select(out=c.ident[:], in_=c.ident[:], compare_op=ALU.not_equal, fill=1.0,
                                    base=0, pattern=[[-1, P]], channel_multiplier=1).then_inc(ident_ready, 1)

        @block.tensor
        def _(pe):
            pe.wait_ge(raw_loaded, 4 * DMA)
            pe.wait_ge(ident_ready, 1)
            for m in range(4):
                for oc in range(FC):
                    for fc in range(FC):
                        mm = nc.tensor.transpose(turned[m][:, fc, oc * P:(oc + 1) * P],
                                                 raw[:, m, oc, fc * P:(fc + 1) * P], c.ident[:])
                mm.then_inc(turned_ready, 1)

        @block.scalar
        def _(act):
            for m, dst in enumerate((c.wqT, c.wkT, c.wvT, c.woT)):
                act.wait_ge(turned_ready, m + 1)
                nc.scalar.copy(dst[:], turned[m][:]).then_inc(copied, 1)
            act.wait_ge(copied, 4)

        @block.vector
        def _(dve):
            dve.wait_ge(w1_loaded, 2 * DMA)
            heads = c.w1[:, :, 0:F].rearrange("p c (h d) -> p c h d", h=H)
            for s in range(2):
                for fc in range(FC):
                    last = nc.vector.tensor_tensor(
                        product[:, s, fc * H:(fc + 1) * H, :], heads[:, fc],
                        a_rows[:, s:s + 1, :].to_broadcast([P, H, DH]), ALU.mult)
            last.then_inc(product_ready, 1)
            dve.wait_ge(product_ready, 1)
            for s in range(2):
                for fc in range(FC):
                    nc.vector.tensor_reduce(c.w1[:, fc, F + s * H:F + (s + 1) * H],
                                            product[:, s, fc * H:(fc + 1) * H, :], AXIS_FREE,
                                            ALU.add).then_inc(product_ready, 1)
            dve.wait_ge(product_ready, 1 + 2 * FC)


def project_layer0(nc, c, s, x, adj, B, N):
    NT = N // P
    STEP = 512
    TT = STEP // P
    ITERATIONS = B * N // (2 * STEP)
    ROWS = NT // ITERATIONS
    assert ROWS * ITERATIONS == NT
    HALF = 8
    HALVES = NT // HALF
    x_steps = x.rearrange("b n f -> (b n) f").rearrange("(i t p) f -> i p t f", p=P, t=TT)
    adj_rows = adj.rearrange("(i p) j -> i p j", p=P)
    STEPS = N // STEP
    assert STEPS % 2 == 0
    with ExitStack() as ctx:
        sb, ps, sem = allocators(nc, ctx, "project")
        x_in = [sb(f"x_in{i}", [P, TT, F], F32) for i in range(2)]
        xT = [sb(f"xT{i}", [P, FC, STEP], F32) for i in range(2)]
        split = [[sb(f"split{i}_{m}", [P, 2, STEP], F16) for m in range(2 * PAIRS)] for i in range(2)]
        v_sum = [sb(f"v_sum{i}", [P, H * TT, DV], F32) for i in range(2)]
        v_out = [sb(f"v_out{i}", [P, H * TT, 2, DV], F16) for i in range(2)]
        edge_tiles = sb("edge_tiles", [P, HALVES, HALF, P], BF16)
        adj_in = sb("adj_in", [P, N], I32)
        is_zero = sb("is_zero", [P, N], BF16)
        is_edge = sb("is_edge", [P, N], BF16)
        xT_ps = ps("xT_ps", [P, FC, STEP], F32)
        qk_ps = [ps(f"qk_ps{i}", [P, STEP], F32) for i in range(2)]
        v_ps = [ps(f"v_ps{i}", [P, 2, F], F32) for i in range(2)]
        mask_ps = [ps(f"mask_ps{i}", [P, HALF, P], BF16) for i in range(2)]

        x_loaded = [sem(f"x_loaded{i}") for i in range(2)]
        x_turned = sem("x_turned")
        xT_ready = sem("xT_ready")
        qk_ready = sem("qk_ready")
        high_ready = sem("high_ready")
        low_ready = sem("low_ready")
        v_ready = sem("v_ready")
        v_copied = sem("v_copied")
        v_high = sem("v_high")
        v_split = sem("v_split")
        edges_stored = sem("edges_stored")
        ones_ready = sem("ones_ready")
        split_stored = [sem(f"split_stored{i}") for i in range(2)]
        v_stored = [sem(f"v_stored{i}") for i in range(2)]
        adj_loaded = sem("adj_loaded")
        adj_coded = sem("adj_coded")
        mask_turned = sem("mask_turned")
        mask_ready = sem("mask_ready")
        sp_held = sem("sp_held")
        block = ctx.enter_context(nc.Block())
        codes = (is_zero, is_edge)
        turns = {q * 4 // (ROWS * HALVES): (q // HALVES, q % HALVES) for q in range(ROWS * HALVES)}
        assert len(turns) == ROWS * HALVES

        @block.sync
        def _(sp):
            def load_x(b, st):
                i = st % 2
                hold(sp, x_turned, STEPS * b + st, sp_held)
                at = x_steps[bass.ds(STEPS * b + st, 1)].rearrange("o p t f -> (o p) t f")
                sp.dma_start(x_in[i][:], at).then_inc(x_loaded[i], DMA)

            def load_adj(row):
                sp.dma_start(adj_in[:], adj_rows[bass.ds(row, 1)].rearrange("o p j -> (o p) j")
                             ).then_inc(adj_loaded, DMA)

            def batch(b, last):
                for st in range(STEPS):
                    i = st % 2
                    if not (last and st + 2 >= STEPS):
                        load_x(b, st + 2)
                    for q, (r, half) in turns.items():
                        row = ROWS * (STEPS // 2 * b + st // 2) + r
                        if q // 2 == i and half == 0 and not (isinstance(row, int) and row == NT - 1):
                            hold(sp, adj_coded, row + 2, sp_held)
                            load_adj(row + 1)
                    for m in range(2 * PAIRS):
                        hold(sp, low_ready, 2 + 2 * PAIRS * (STEPS * b + st) + m + 1, sp_held)
                        dst = (s.q, s.k)[m // PAIRS][bass.ds(b, 1), m % PAIRS, :, :, st * STEP:(st + 1) * STEP]
                        sp.dma_start(dst.rearrange("o s p w -> p (o s) w"), split[i][m][:]
                                     ).then_inc(split_stored[i], DMA)
                    hold(sp, v_split, STEPS * b + st + 1, sp_held)
                    wide = TT * 2 * DV
                    dst = s.v[bass.ds(b, 1), :, :, st * wide:(st + 1) * wide]
                    sp.dma_start(dst.rearrange("o h p w -> p (o h) w"),
                                 v_out[i][:].rearrange("p (h t) s d -> p h (t s d)", h=H)).then_inc(v_stored[i], DMA)
                    wide = TT * DV
                    dst = s.v32[bass.ds(b, 1), :, :, st * wide:(st + 1) * wide]
                    sp.dma_start(dst.rearrange("o h p w -> p (o h) w"),
                                 v_sum[i][:].rearrange("p (h t) d -> p h (t d)", h=H)).then_inc(v_stored[i], DMA)
                    for q, (r, half) in turns.items():
                        if q // 2 == i and half == HALVES - 1:
                            row = ROWS * (STEPS // 2 * b + st // 2) + r
                            hold(sp, mask_ready, 2 + 2 * HALVES * (row + 1), sp_held)
                            sp.dma_start(s.edge_mask[:, :, bass.ds(row * P, P)],
                                         edge_tiles[:].rearrange("p a j w -> p (a j) w")).then_inc(edges_stored, DMA)

            for i in range(2):
                sp.sem_inc(split_stored[i], 2 * PAIRS * DMA)
                sp.sem_inc(v_stored[i], 2 * DMA)
            sp.sem_inc(edges_stored, DMA)
            for st in range(2):
                first = x_steps[st:st + 1].rearrange("o p t f -> (o p) t f")
                sp.dma_start(x_in[st][:], first).then_inc(x_loaded[st], DMA)
            load_adj(0)
            if B > 1:
                with sp.Fori(0, B - 1) as b:
                    batch(b, last=False)
            batch(B - 1, last=True)
            for i in range(2):
                hold(sp, split_stored[i], (1 + ITERATIONS) * 2 * PAIRS * DMA, sp_held)
                hold(sp, v_stored[i], (1 + ITERATIONS) * 2 * DMA, sp_held)
            hold(sp, edges_stored, (1 + NT) * DMA, sp_held)

        @block.gpsimd
        def _(pool):
            for i in range(2):
                nc.gpsimd.memset(v_sum[i][:, :, DH:DV], 1.0)
                nc.gpsimd.memset(v_out[i][:, :, 0, DH:DV], 1.0)
                last = nc.gpsimd.memset(v_out[i][:, :, 1, DH:DV], 0.0)
            last.then_inc(ones_ready, 1)
            with pool.Fori(0, ITERATIONS) as n:
                for i in range(2):
                    pool.wait_ge(v_high, 2 * n + i + 1)
                    nc.gpsimd.tensor_tensor(v_out[i][:, :, 1, 0:DH], v_sum[i][:, :, 0:DH],
                                            v_out[i][:, :, 0, 0:DH], ALU.subtract).then_inc(v_split, 1)

        @block.tensor
        def _(pe):
            def turn_x(n, i):
                n, i = n + i // 2, i % 2
                pe.wait_ge(x_loaded[i], DMA * (n + 1))
                if not (isinstance(n, int) and n == 0 and i == 0):
                    pe.wait_ge(xT_ready, 2 * n + i)
                for fc in range(FC):
                    for t in range(TT):
                        mm = nc.tensor.transpose(xT_ps[:, fc, t * P:(t + 1) * P],
                                                 x_in[i][:, t, fc * P:(fc + 1) * P], c.ident[:])
                mm.then_inc(x_turned, 1)

            def turn_masks(n, r, half):
                count = HALVES * (ROWS * n + r) + half
                pe.wait_ge(adj_coded, 1 + ROWS * n + r + 1)
                pe.wait_ge(mask_ready, 2 + 2 * count)
                for m in range(2):
                    for j in range(HALF):
                        col = (half * HALF + j) * P
                        mm = nc.tensor.transpose(mask_ps[m][:, j, :], codes[m][:, col:col + P], c.ident16[:])
                mm.then_inc(mask_turned, 1)

            def iteration(n, last):
                for i in range(2):
                    pe.wait_ge(xT_ready, 2 * n + i + 1)
                    for m in range(2 * PAIRS):
                        w = (c.wqT, c.wkT)[m // PAIRS]
                        pair = m % PAIRS
                        pe.wait_ge(low_ready, 4 * PAIRS * n + 2 * PAIRS * i + m + 1)
                        for fc in range(FC):
                            mm = nc.tensor.matmul(qk_ps[m % 2][:], w[:, fc, pair * P:(pair + 1) * P], xT[i][:, fc, :],
                                                  start=fc == 0, stop=fc == FC - 1)
                        mm.then_inc(qk_ready, 1)
                        if m % 2 and 2 * i + m // 2 in turns:
                            turn_masks(n, *turns[2 * i + m // 2])
                    if not (last and i == 1):
                        turn_x(n, i + 1)
                    for t2 in range(2):
                        pe.wait_ge(v_copied, 2 * (2 * n + i) + t2 + 1)
                        for t in range(2):
                            tok = (2 * t2 + t) * P
                            for fc in range(FC):
                                mm = nc.tensor.matmul(v_ps[t2][:, t, :], xT[i][:, fc, tok:tok + P], c.wvT[:, fc, :],
                                                      start=fc == 0, stop=fc == FC - 1)
                        mm.then_inc(v_ready, 1)

            pe.sem_inc(x_turned, 1)
            pe.sem_inc(mask_turned, HALVES)
            turn_x(0, 0)
            with pe.Fori(0, ITERATIONS - 1) as n:
                iteration(n, last=False)
            iteration(ITERATIONS - 1, last=True)

        @block.scalar
        def _(act):
            def copy_x(n, i):
                n, i = n + i // 2, i % 2
                act.wait_ge(x_turned, 1 + 2 * n + i + 1)
                nc.scalar.copy(xT[i][:], xT_ps[:]).then_inc(xT_ready, 1)

            def iteration(n, last):
                for i in range(2):
                    for m in range(2 * PAIRS):
                        act.wait_ge(qk_ready, 4 * PAIRS * n + 2 * PAIRS * i + m + 1)
                        if m == 0:
                            act.wait_ge(split_stored[i], 2 * PAIRS * DMA * (n + 1))
                        nc.scalar.activation(split[i][m][:, 0, :], qk_ps[m % 2][:], ACT.Identity,
                                             bias=(c.bq, c.bk)[m // PAIRS][:, m % PAIRS:m % PAIRS + 1],
                                             ).then_inc(high_ready, 1)
                    if not (last and i == 1):
                        copy_x(n, i + 1)
                    act.wait_ge(v_stored[i], 2 * DMA * (n + 1))
                    act.wait_ge(v_copied, 2 + 2 * (2 * n + i) + 2)
                    nc.scalar.copy(v_out[i][:, :, 0, 0:DH], v_sum[i][:, :, 0:DH]
                                   ).then_inc(v_high, 1)

            act.wait_ge(ones_ready, 1)
            copy_x(0, 0)
            with act.Fori(0, ITERATIONS - 1) as n:
                iteration(n, last=False)
            iteration(ITERATIONS - 1, last=True)

        @block.vector
        def _(dve):
            def code_row(row):
                dve.wait_ge(adj_loaded, DMA * (row + 1))
                dve.wait_ge(mask_turned, HALVES * (row + 1))
                nc.vector.tensor_scalar(is_zero[:], adj_in[:], 0.0, -2 * RAW_CLIP, ALU.is_equal, ALU.mult)
                nc.vector.tensor_scalar(is_edge[:], adj_in[:], 0.0, None, ALU.is_gt).then_inc(adj_coded, 1)

            def keep_masks(row, half):
                dve.wait_ge(mask_turned, HALVES * (row + 1) + half + 1)
                nc.vector.tensor_scalar(c.clip_mask[:, half * HALF:(half + 1) * HALF, bass.ds(row * P, P)],
                                        mask_ps[0][:], RAW_CLIP, None, ALU.add).then_inc(mask_ready, 1)
                if half == 0:
                    dve.wait_ge(edges_stored, DMA * (row + 1))
                nc.vector.tensor_copy(edge_tiles[:, half], mask_ps[1][:]).then_inc(mask_ready, 1)

            for semaphore, free in ((low_ready, 2), (v_copied, 2), (adj_coded, 1), (mask_ready, 2)):
                dve.sem_inc(semaphore, free)
            with dve.Fori(0, ITERATIONS) as n:
                for i in range(2):
                    for m in range(2 * PAIRS):
                        turn = turns.get(2 * i + m // 2)
                        if m % 2 == 0 and turn and turn[1] == 0:
                            code_row(ROWS * n + turn[0])
                        dve.wait_ge(high_ready, 2 * PAIRS * (2 * n + i) + m + 1)
                        nc.vector.scalar_tensor_tensor(
                            out=split[i][m][:, 1, :], in0=qk_ps[m % 2][:],
                            scalar=(c.bq, c.bk)[m // PAIRS][:, m % PAIRS:m % PAIRS + 1],
                            in1=split[i][m][:, 0, :], op0=ALU.add, op1=ALU.subtract).then_inc(low_ready, 1)
                        if m % 2 and turn:
                            keep_masks(ROWS * n + turn[0], turn[1])
                    dve.wait_ge(v_stored[i], 2 * DMA * (n + 1))
                    sums = v_sum[i][:].rearrange("p (h t) d -> p t h d", h=H)
                    for t2 in range(2):
                        dve.wait_ge(v_ready, 2 * (2 * n + i) + t2 + 1)
                        nc.vector.tensor_tensor(
                            sums[:, 2 * t2:2 * t2 + 2, :, 0:DH],
                            v_ps[t2][:].rearrange("p t (h d) -> p t h d", h=H),
                            c.bv[:].rearrange("p (o h d) -> p o h d", o=1, h=H).to_broadcast([P, 2, H, DH]),
                            ALU.add).then_inc(v_copied, 1)


def attend_layer0(nc, c, s, B, N):
    NQ, NCH = N // QG, N // CHUNK
    HEAD_UNITS = NQ * NCH
    BODY_UNITS = 2 * HEAD_UNITS
    PAIR_COUNT = B * PAIRS
    UNITS = BODY_UNITS * PAIR_COUNT
    GROUPS = 2 * NQ
    NT = N // P
    S_RING, P_RING, O_RING = 2, 8, 4
    AHEAD = 5
    EXP_AHEAD = 4
    MASK_AHEAD = 2
    assert BODY_UNITS % P_RING == 0 and NCH % O_RING == 0 and AHEAD < P_RING and PAIR_COUNT > 2
    with ExitStack() as ctx:
        sb, ps, sem = allocators(nc, ctx, "attend0")
        k_split = [sb(f"k_split{i}", [P, N], F16) for i in range(2)]
        q_high = [sb(f"q_high{i}", [P, N], F16) for i in range(2)]
        q_low = [sb(f"q_low{i}", [P, N], F16) for i in range(2)]
        values = [sb(f"values{i}", [P, NT, 2, DV], F16) for i in range(2)]
        whole = [sb(f"whole{i}", [P, NT, DV], F32) for i in range(2)]
        probs = [sb(f"probs{i}", [P, KT, QG], F32) for i in range(P_RING)]
        rest = [sb(f"rest{i}", [P, KT, QG], F16) for i in range(P_RING)]
        sums = [sb(f"sums{i}", [P, NCH * QT, DV], F32) for i in range(2)]
        inverse = [sb(f"inverse{i}", [P, NCH * QT], F32) for i in range(2)]
        scaled = sb("scaled", [P, NCH * QT, DH], F32)
        context = [sb(f"context{i}", [P, QT, DH], F32) for i in range(2)]
        s_ps = [ps(f"s_ps{i}", [P, KT, QG], F32) for i in range(S_RING)]
        o_ps = [ps(f"o_ps{i}", [P, QT, P], F32) for i in range(O_RING)]

        qk_loaded = [sem(f"qk_loaded{i}") for i in range(2)]
        v_loaded = [sem(f"v_loaded{i}") for i in range(2)]
        scores_ready = sem("scores_ready")
        masked = sem("masked")
        probs_ready = sem("probs_ready")
        rest_dve = sem("rest_dve")
        rest_pool = sem("rest_pool")
        probs_free = sem("probs_free")
        summed = sem("summed")
        sums_free = sem("sums_free")
        inverse_ready = sem("inverse_ready")
        group_free = sem("group_free")
        pool_step = sem("pool_step")
        context_ready = sem("context_ready")
        context_stored = [sem(f"context_stored{i}") for i in range(2)]
        sp_held = sem("sp_held")
        block = ctx.enter_context(nc.Block())
        LEVELS = NCH.bit_length() - 1
        assert NCH == 1 << LEVELS and LEVELS >= 1

        def unit(u):
            return u // HEAD_UNITS, u % HEAD_UNITS // NCH, u % NCH

        SPLIT_BY = [("DVE", "Pool", "DVE", "Pool", "DVE", "PE", "Pool", "DVE",
                     "DVE", "Pool", "DVE", "Pool", "PE", "DVE", "PE", "DVE")[u % 16] for u in range(BODY_UNITS)]

        def rest_count(it, u):
            mine = [x == SPLIT_BY[u] for x in SPLIT_BY]
            ready = {"DVE": rest_dve, "Pool": rest_pool}[SPLIT_BY[u]]
            return ready, sum(mine) * it + sum(mine[:u + 1])

        @block.sync
        def _(sp):
            def load_head(b, h):
                i = h % 2
                head = H * b + h
                bb, hh = (b, h) if h < H else (b + 1, h - H)
                rows = slice(hh % 2 * DH, hh % 2 * DH + DH)
                if not (isinstance(head, int) and head < 2):
                    hold(sp, scores_ready, HEAD_UNITS * (head - 1) + 1, sp_held)
                at = [[t[bass.ds(bb, 1), hh // 2, half, rows, :].rearrange("o d n -> (o d) n") for half in range(2)]
                      for t in (s.q, s.k)]
                for half in range(2):
                    place = slice(half * DH, half * DH + DH)
                    sp.dma_start(k_split[i][place, :], at[1][half]).then_inc(qk_loaded[i], DMA)
                    sp.dma_start(q_high[i][place, :], at[0][0]).then_inc(qk_loaded[i], DMA)
                    sp.dma_start(q_low[i][place, :], at[0][1]).then_inc(qk_loaded[i], DMA)
                if not (isinstance(head, int) and head < 2):
                    hold(sp, probs_free, P_RING + HEAD_UNITS * (head - 1), sp_held)
                v_at = s.v[bass.ds(bb, 1), hh, :, :].rearrange("o p w -> (o p) w")
                sp.dma_start(values[i][:].rearrange("p t s d -> p (t s d)"), v_at).then_inc(v_loaded[i], DMA)
                v_at = s.v32[bass.ds(bb, 1), hh, :, :].rearrange("o p w -> (o p) w")
                sp.dma_start(whole[i][:].rearrange("p t d -> p (t d)"), v_at).then_inc(v_loaded[i], DMA)

            def store_group(b, h, g):
                hold(sp, context_ready, NQ * (H * b + h) + g + 1, sp_held)
                dst = s.ctx[bass.ds(b, 1), g * QG:(g + 1) * QG, h * DH:(h + 1) * DH]
                sp.dma_start(dst.rearrange("o (t p) d -> p (o t) d", p=P), context[g % 2][:]
                             ).then_inc(context_stored[g % 2], DMA)

            def batch(b, last):
                for h in range(H):
                    for g in range(NQ):
                        if g == 0 and not (last and h == H - 1):
                            load_head(b, h + 1)
                        store_group(b, h, g)

            load_head(0, 0)
            if B > 1:
                with sp.Fori(0, B - 1) as b:
                    batch(b, last=False)
            batch(B - 1, last=True)
            for i in range(2):
                hold(sp, context_stored[i], B * H * NQ // 2 * DMA, sp_held)

        @block.tensor
        def _(pe):
            def scores(it, u):
                if u >= BODY_UNITS:
                    it, u = it + 1, u - BODY_UNITS
                hh, g, j = unit(u)
                if u % HEAD_UNITS == 0:
                    pe.wait_ge(qk_loaded[hh], 6 * DMA * (it + 1))
                if not (isinstance(it, int) and it == 0 and u < S_RING):
                    pe.wait_ge(masked, BODY_UNITS * it + u - S_RING + 1)
                for kt in range(KT):
                    key = (KT * j + kt) * P
                    for half, q in enumerate((q_high, q_low)):
                        mm = nc.tensor.matmul(s_ps[u % S_RING][:, kt, :], k_split[hh][:, key:key + P],
                                              q[hh][:, g * QG:(g + 1) * QG], start=half == 0, stop=half == 1)
                mm.then_inc(scores_ready, 1)

            def products(it, u):
                hh, g, j = unit(u)
                if u % HEAD_UNITS == 0:
                    pe.wait_ge(v_loaded[hh], 2 * DMA * (it + 1))
                in_float32 = SPLIT_BY[u] == "PE"
                if in_float32:
                    pe.wait_ge(probs_ready, BODY_UNITS * it + u + 1)
                else:
                    rest_ready, count = rest_count(it, u)
                    pe.wait_ge(rest_ready, count)
                pe.wait_ge(sums_free, BODY_UNITS * it + u + 1)
                upper = probs[u % P_RING][:].bitcast(BF16)
                for t in range(QT):
                    to = o_ps[u % O_RING][:, t, :]
                    for kt in range(KT):
                        if in_float32:
                            mm = nc.tensor.matmul(to[:, 0:DV], probs[u % P_RING][:, kt, t * P:(t + 1) * P],
                                                  whole[hh][:, KT * j + kt], start=kt == 0, stop=kt == KT - 1)
                            continue
                        w_high = upper[:, kt, 2 * t * P + 1:2 * (t + 1) * P:2]
                        w_rest = rest[u % P_RING][:, kt, t * P:(t + 1) * P]
                        v = values[hh][:, KT * j + kt]
                        last = kt == KT - 1
                        nc.tensor.matmul(to[:, 0:DV], w_high, v[:, 0, :], start=kt == 0, stop=False)
                        nc.tensor.matmul(to[:, 0:DH], w_high, v[:, 1, 0:DH], start=False, stop=False,
                                         skip_group_check=True)
                        mm = nc.tensor.matmul(to[:, 0:DV], w_rest, v[:, 0, :], start=False, stop=last)
                mm.then_inc(probs_free, 1)

            pe.sem_inc(probs_free, P_RING)
            for u in range(AHEAD):
                scores(0, u)
            with pe.Fori(0, PAIR_COUNT - 1) as it:
                for u in range(BODY_UNITS):
                    scores(it, u + AHEAD)
                    products(it, u)
            for u in range(BODY_UNITS):
                if u + AHEAD < BODY_UNITS:
                    scores(PAIR_COUNT - 1, u + AHEAD)
                products(PAIR_COUNT - 1, u)

        @block.scalar
        def _(act):
            def exponentials(it, u):
                if u >= BODY_UNITS:
                    it, u = it + 1, u - BODY_UNITS
                act.wait_ge(masked, BODY_UNITS * it + u + 1)
                nc.scalar.activation(probs[u % P_RING][:], probs[u % P_RING][:], ACT.Exp, bias=c.exp_bias[:],
                                     scale=SCALE).then_inc(probs_ready, 1)

            def copy_sums(it, u):
                g = u // NCH
                if u % NCH == 0:
                    act.wait_ge(group_free, GROUPS * it + g + 1)
                act.wait_ge(probs_free, P_RING + BODY_UNITS * it + u + 1)
                nc.scalar.copy(sums[g % 2][:, u % NCH * QT:(u % NCH + 1) * QT, :], o_ps[u % O_RING][:, :, 0:DV]
                               ).then_inc(sums_free, 1)

            act.sem_inc(sums_free, O_RING)
            for u in range(EXP_AHEAD):
                exponentials(0, u)
            with act.Fori(0, PAIR_COUNT - 1) as it:
                for u in range(BODY_UNITS):
                    exponentials(it, u + EXP_AHEAD)
                    copy_sums(it, u)
            for u in range(BODY_UNITS):
                if u + EXP_AHEAD < BODY_UNITS:
                    exponentials(PAIR_COUNT - 1, u + EXP_AHEAD)
                copy_sums(PAIR_COUNT - 1, u)

        @block.vector
        def _(dve):
            LATE = 2

            def mask(it, u):
                if u >= BODY_UNITS:
                    it, u = it + 1, u - BODY_UNITS
                hh, g, j = unit(u)
                dve.wait_ge(scores_ready, BODY_UNITS * it + u + 1)
                dve.wait_ge(probs_free, BODY_UNITS * it + u + 1)
                nc.vector.scalar_tensor_tensor(
                    out=probs[u % P_RING][:], in0=s_ps[u % S_RING][:], scalar=-RAW_CLIP,
                    in1=c.clip_mask[:, KT * j:KT * (j + 1), g * QG:(g + 1) * QG],
                    op0=ALU.max, op1=ALU.min).then_inc(masked, 1)

            def take_rest(it, u):
                if SPLIT_BY[u] != "DVE":
                    return
                dve.wait_ge(probs_ready, BODY_UNITS * it + u + 1)
                p = probs[u % P_RING]
                nc.vector.tensor_tensor(rest[u % P_RING][:], p[:], p[:].bitcast(BF16)[:, :, 1::2], ALU.subtract
                                        ).then_inc(rest_dve, 1)

            def invert(it, g):
                dve.wait_ge(sums_free, O_RING + BODY_UNITS * it + NCH * (g + 1))
                nc.vector.reciprocal(inverse[g % 2][:], sums[g % 2][:, :, DH]).then_inc(inverse_ready, 1)

            def iteration(it, last):
                for u in range(BODY_UNITS):
                    if not (last and u + MASK_AHEAD >= BODY_UNITS):
                        mask(it, u + MASK_AHEAD)
                    take_rest(it, u)
                    g = u // NCH - 1
                    if u % NCH == LATE and g >= 0:
                        invert(it, g)
                    elif u % NCH == LATE and not (isinstance(it, int) and it == 0):
                        invert(it - 1, GROUPS - 1)
                if last:
                    invert(it, GROUPS - 1)

            for u in range(MASK_AHEAD):
                mask(0, u)
            iteration(0, last=False)
            with dve.Fori(1, PAIR_COUNT - 1) as it:
                iteration(it, last=False)
            iteration(PAIR_COUNT - 1, last=True)

        @block.gpsimd
        def _(pool):
            def take_rest(it, u):
                if SPLIT_BY[u] != "Pool":
                    return
                pool.wait_ge(probs_ready, BODY_UNITS * it + u + 1)
                p = probs[u % P_RING]
                nc.gpsimd.tensor_tensor(rest[u % P_RING][:], p[:], p[:].bitcast(BF16)[:, :, 1::2], ALU.subtract
                                        ).then_inc(rest_pool, 1)

            def group_steps(it, g):
                count = GROUPS * it + g
                i = g % 2

                def scale():
                    pool.wait_ge(inverse_ready, count + 1)
                    if not (isinstance(count, int) and count == 0):
                        pool.wait_ge(context_ready, count)
                    nc.gpsimd.tensor_tensor(scaled[:], sums[i][:, :, 0:DH],
                                            inverse[i][:].unsqueeze(2).to_broadcast([P, NCH * QT, DH]), ALU.mult
                                            ).then_inc(group_free, 1)

                def halve(level):
                    width = NCH * QT >> level + 1
                    if level == 0:
                        pool.wait_ge(group_free, 2 + count + 1)
                    else:
                        pool.wait_ge(pool_step, (LEVELS - 1) * count + level)
                    if level < LEVELS - 1:
                        nc.gpsimd.tensor_tensor(scaled[:, 0:width, :], scaled[:, 0:width, :],
                                                scaled[:, width:2 * width, :], ALU.add).then_inc(pool_step, 1)
                        return
                    if not (isinstance(it, int) and it == 0 and g < 2):
                        pool.wait_ge(context_stored[i], DMA * (NQ * it + g // 2))
                    nc.gpsimd.tensor_tensor(context[i][:], scaled[:, 0:QT, :], scaled[:, QT:2 * QT, :], ALU.add
                                            ).then_inc(context_ready, 1)

                return [scale] + [lambda level=level: halve(level) for level in range(LEVELS)]

            def iteration(it, last):
                for u in range(BODY_UNITS):
                    take_rest(it, u)
                    g, place = u // NCH - 1, u % NCH - FIRST_STEP
                    if place < 0 or place > LEVELS or (g < 0 and isinstance(it, int) and it == 0):
                        continue
                    (group_steps(it, g) if g >= 0 else group_steps(it - 1, GROUPS - 1))[place]()
                if last:
                    for step in group_steps(it, GROUPS - 1):
                        step()

            FIRST_STEP = NCH - LEVELS - 1
            pool.sem_inc(group_free, 2)
            iteration(0, last=False)
            with pool.Fori(1, PAIR_COUNT - 1) as it:
                iteration(it, last=False)
            iteration(PAIR_COUNT - 1, last=True)


def finish_layer0(nc, c, s, x, B, N):
    NT = N // P
    TILES = NT // 2
    CHUNKS = TILES // 2
    V1 = F + 2 * H
    with ExitStack() as ctx:
        sb, ps, sem = allocators(nc, ctx, "finish0")
        context = [sb(f"context_in{i}", [P, TILES, F], F32) for i in range(2)]
        x_in = [sb(f"x_in{i}", [P, TILES, F], F32) for i in range(2)]
        x_res = [sb(f"x_res{i}", [P, TILES, F], F32) for i in range(2)]
        x_out = [sb(f"x_out{i}", [P, TILES, F], F32) for i in range(2)]
        contextT = [sb(f"contextT{i}", [P, FC, 2, P], F32) for i in range(2)]
        outT = [sb(f"outT{i}", [P, CHUNKS, FC, 2, P], F32) for i in range(2)]
        v1 = [sb(f"v1_{i}", [P, H, TILES, DV], F32) for i in range(2)]
        edge = [sb(f"edge{i}", [P, TILES, 2 * H], F32) for i in range(2)]
        stats = sb("stats", [P, TILES, 6], F32)
        moments = sb("moments", [P, 2, TILES, 2], F32)
        var_eps = sb("var_eps", [P, 2, TILES], F32)
        rstd = sb("rstd", [P, 2, TILES], F32)
        turn_ps = [ps(f"turn_ps{i}", [P, FC, 2, P], F32) for i in range(2)]
        o_ps = [ps(f"proj_ps{i}", [P, 2, F], F32) for i in range(CHUNKS)]
        v1_ps = [ps(f"v1_ps{i}", [P, 512], F32) for i in range(2)]

        loaded = [sem(f"loaded{i}") for i in range(2)]
        edges_loaded = sem("edges_loaded")
        turned = sem("turned")
        turned_copied = sem("turned_copied")
        projected = sem("projected")
        biased = sem("biased")
        added = sem("added")
        dve_step = sem("dve_step")
        stats_ready = sem("stats_ready")
        moments_ready = [sem(f"moments_ready{i}") for i in range(2)]
        shifted = sem("shifted")
        variance_ready = sem("variance_ready")
        held = sem("held")
        rstd_ready = [sem(f"rstd_ready{i}") for i in range(2)]
        out_ready = sem("out_ready")
        out_turned = sem("out_turned")
        out_copied = sem("out_copied")
        v1_projected = sem("v1_projected")
        v1_ready = sem("v1_ready")
        ones_ready = sem("ones_ready")
        stored = [sem(f"stored{i}") for i in range(2)]
        x1_stored = [sem(f"x1_stored{i}") for i in range(2)]
        context_loaded = [sem(f"context_loaded{i}") for i in range(2)]
        sp_held = sem("sp_held")
        block = ctx.enter_context(nc.Block())
        STORES = 2

        @block.sync
        def _(sp):
            def load(b, i):
                rows = slice(i * TILES * P, (i + 1) * TILES * P)
                if not (isinstance(b, int) and b == 0):
                    hold(sp, turned, CHUNKS * (2 * b + i - 1), sp_held)
                at = s.ctx[bass.ds(b, 1), rows, :].rearrange("o (t p) f -> p (o t) f", p=P)
                sp.dma_start(context[i][:], at).then_inc(context_loaded[i], DMA)
                if not (isinstance(b, int) and b == 0):
                    hold(sp, biased, 2 * b + i - 1, sp_held)
                    hold(sp, shifted, 2 * b + i - 1, sp_held)
                at = x[bass.ds(b, 1), rows, :].rearrange("o (t p) f -> p (o t) f", p=P)
                sp.dma_start(x_in[i][:], at).then_inc(loaded[i], DMA)

            def store_x1(b, i):
                rows = slice(i * TILES * P, (i + 1) * TILES * P)
                hold(sp, out_ready, 2 * b + i + 1, sp_held)
                at = s.x1[bass.ds(b, 1), rows, :].rearrange("o (t p) f -> p (o t) f", p=P)
                sp.dma_start(at, x_out[i][:]).then_inc(x1_stored[i], DMA)

            def store_v1(b, i):
                hold(sp, v1_ready, 2 + TILES * (2 * b + i + 1), sp_held)
                at = s.v1[bass.ds(b, 1), :, :, i * TILES * DV:(i + 1) * TILES * DV]
                sp.dma_start(at.rearrange("o h p w -> p (o h) w"), v1[i][:].rearrange("p h t d -> p h (t d)")
                             ).then_inc(stored[i], DMA)
                at = s.e[bass.ds(b, 1), :, i * TILES * 2 * H:(i + 1) * TILES * 2 * H]
                sp.dma_start(at.rearrange("o p w -> (o p) w"), edge[i][:].rearrange("p t e -> p (t e)")
                             ).then_inc(stored[i], DMA)

            for i in range(2):
                sp.sem_inc(stored[i], STORES * DMA)
                sp.sem_inc(x1_stored[i], DMA)
            load(0, 0)
            load(0, 1)
            for t in range(0, NT, 4):
                sp.dma_start(c.edge_mask[:, t:t + 4, :], s.edge_mask[:, t:t + 4, :]).then_inc(edges_loaded, DMA)
            def batch(b):
                load(b + 1, 0)
                store_x1(b, 0)
                if not isinstance(b, int):
                    store_v1(b - 1, 1)
                load(b + 1, 1)
                store_x1(b, 1)
                store_v1(b, 0)

            batch(0)
            with sp.Fori(1, B - 1) as b:
                batch(b)
            store_x1(B - 1, 0)
            store_v1(B - 2, 1)
            store_x1(B - 1, 1)
            store_v1(B - 1, 0)
            store_v1(B - 1, 1)
            for i in range(2):
                hold(sp, stored[i], STORES * DMA * (B + 1), sp_held)
                hold(sp, x1_stored[i], DMA * (B + 1), sp_held)
            hold(sp, edges_loaded, NT // 4 * DMA, sp_held)

        @block.gpsimd
        def _(pool):
            last = None
            for i in range(2):
                last = nc.gpsimd.memset(v1[i][:, :, :, DH:DV], 1.0)
            last.then_inc(ones_ready, 1)

            def add_bo(b, i):
                b, i = b + i // 2, i % 2
                pool.wait_ge(loaded[i], DMA * (b + 1))
                if not (isinstance(b, int) and b == 0):
                    pool.wait_ge(dve_step, 2 * (2 * b + i) - 2)
                nc.gpsimd.tensor_tensor(x_res[i][:], x_in[i][:],
                                        c.bo[:].unsqueeze(1).to_broadcast([P, TILES, F]), ALU.add
                                        ).then_inc(biased, 1)

            def add_beta(b, i):
                b, i = b + i // 2, i % 2
                pool.wait_ge(x1_stored[i], DMA * (b + 1))
                if not (isinstance(b, int) and b == 0 and i == 0):
                    pool.wait_ge(out_turned, CHUNKS * (2 * b + i))
                nc.gpsimd.tensor_tensor(x_out[i][:], x_in[i][:],
                                        c.beta[:].unsqueeze(1).to_broadcast([P, TILES, F]), ALU.add
                                        ).then_inc(shifted, 1)

            def take_rstd(b, i, norm):
                count = 2 * (2 * b + i) + norm + 1
                pool.wait_ge(moments_ready[norm], 2 * b + i + 1)
                nc.gpsimd.tensor_tensor(var_eps[:, norm], moments[:, norm, :, 1], c.eps[:, 0:TILES], ALU.add
                                        ).then_inc(variance_ready, 1)
                pool.wait_ge(variance_ready, count)
                nc.gpsimd.tensor_tensor(rstd[:, norm], var_eps[:, norm], c.minus_half[:, 0:TILES], ALU.pow
                                        ).then_inc(rstd_ready[norm], 1)

            def half(b, i, bo=True, beta=True):
                take_rstd(b, i, 0)
                if beta:
                    add_beta(b, i + 1)
                take_rstd(b, i, 1)
                if bo:
                    add_bo(b, i + 2)

            add_bo(0, 0)
            add_beta(0, 0)
            add_bo(0, 1)
            with pool.Fori(0, B - 1) as b:
                for i in range(2):
                    half(b, i)
            half(B - 1, 0, bo=False)
            half(B - 1, 1, bo=False, beta=False)

        @block.tensor
        def _(pe):
            def front(b, i):
                half = 2 * b + i
                pe.wait_ge(context_loaded[i], DMA * (b + 1))

                def turn(k):
                    if k >= 2:
                        pe.wait_ge(turned_copied, CHUNKS * half + k - 1)
                    for fc in range(FC):
                        for t in range(2):
                            mm = nc.tensor.transpose(turn_ps[k % 2][:, fc, t, :],
                                                     context[i][:, 2 * k + t, fc * P:(fc + 1) * P], c.ident[:])
                    mm.then_inc(turned, 1)

                def project(k):
                    pe.wait_ge(turned_copied, CHUNKS * half + k + 1)
                    if not (isinstance(half, int) and half == 0):
                        pe.wait_ge(added, CHUNKS * (half - 1) + k + 1)
                    for t in range(2):
                        for fc in range(FC):
                            mm = nc.tensor.matmul(o_ps[k][:, t, :], contextT[k % 2][:, fc, t, :],
                                                  c.woT[:, fc, :], start=fc == 0, stop=fc == FC - 1)
                    mm.then_inc(projected, 1)

                turn(0)
                for k in range(CHUNKS):
                    if k + 1 < CHUNKS:
                        turn(k + 1)
                    project(k)

            def back(b, i):
                half = 2 * b + i
                pe.wait_ge(out_ready, half + 1)
                for k in range(CHUNKS):
                    if k >= 2:
                        pe.wait_ge(out_copied, CHUNKS * half + k - 1)
                    for fc in range(FC):
                        for t in range(2):
                            mm = nc.tensor.transpose(turn_ps[k % 2][:, fc, t, :],
                                                     x_out[i][:, 2 * k + t, fc * P:(fc + 1) * P], c.ident[:])
                    mm.then_inc(out_turned, 1)
                for t in range(TILES):
                    pe.wait_ge(out_copied, CHUNKS * half + t // 2 + 1)
                    pe.wait_ge(v1_ready, TILES * half + t + 1)
                    for fc in range(FC):
                        mm = nc.tensor.matmul(v1_ps[t % 2][:, 0:V1], outT[i][:, t // 2, fc, t % 2, :],
                                              c.w1[:, fc, :], start=fc == 0, stop=fc == FC - 1)
                    mm.then_inc(v1_projected, 1)

            pe.sem_inc(out_turned, CHUNKS)
            front(0, 0)
            if B > 1:
                with pe.Fori(0, B - 1) as b:
                    front(b, 1)
                    back(b, 0)
                    front(b + 1, 0)
                    back(b, 1)
            front(B - 1, 1)
            back(B - 1, 0)
            back(B - 1, 1)

        @block.scalar
        def _(act):
            def front(b, i):
                half = 2 * b + i
                for k in range(CHUNKS):
                    count = CHUNKS * half + k
                    act.wait_ge(turned, count + 1)
                    if not (isinstance(count, int) and count < 2):
                        act.wait_ge(projected, count - 1)
                    nc.scalar.copy(contextT[k % 2][:], turn_ps[k % 2][:]).then_inc(turned_copied, 1)

            def back(b, i):
                half = 2 * b + i
                for k in range(CHUNKS):
                    act.wait_ge(out_turned, CHUNKS * (half + 1) + k + 1)
                    nc.scalar.copy(outT[i][:, k], turn_ps[k % 2][:]).then_inc(out_copied, 1)
                act.wait_ge(stored[i], STORES * DMA * (b + 1))
                for t in range(TILES):
                    act.wait_ge(v1_projected, TILES * half + t + 1)
                    nc.scalar.copy(edge[i][:, t, :], v1_ps[t % 2][:, F:V1])
                    nc.scalar.copy(v1[i][:, :, t, 0:DH], v1_ps[t % 2][:, 0:F].rearrange("p (h d) -> p h d", h=H)
                                   ).then_inc(v1_ready, 1)

            act.wait_ge(ones_ready, 1)
            act.sem_inc(v1_ready, 2)
            front(0, 0)
            if B > 1:
                with act.Fori(0, B - 1) as b:
                    front(b, 1)
                    back(b, 0)
                    front(b + 1, 0)
                    back(b, 1)
            front(B - 1, 1)
            back(B - 1, 0)
            back(B - 1, 1)

        @block.vector
        def _(dve):
            def take_moments(half, norm, source):
                if norm == 0 and not (isinstance(half, int) and half == 0):
                    dve.wait_ge(moments_ready[1], half)
                for t in range(TILES):
                    last = nc.vector.bn_stats(stats[:, t, :], source[:, t, :])
                last.then_inc(stats_ready, 1)
                hold(dve, stats_ready, 2 * half + 1 + norm, held)
                for t in range(TILES):
                    last = nc.vector.bn_aggr(moments[:, norm, t, :], stats[:, t, :])
                last.then_inc(moments_ready[norm], 1)

            def residual(b, i):
                b, i = b + i // 2, i % 2
                half = 2 * b + i
                X = x_res[i]
                dve.wait_ge(biased, half + 1)
                for k in range(CHUNKS):
                    dve.wait_ge(projected, CHUNKS * half + k + 1)
                    nc.vector.tensor_tensor(X[:, 2 * k:2 * k + 2, :], o_ps[k][:], X[:, 2 * k:2 * k + 2, :],
                                            ALU.add).then_inc(added, 1)
                dve.wait_ge(added, CHUNKS * (half + 1))
                take_moments(half, 0, X)

            def first_norm(b, i):
                half = 2 * b + i
                X, G = x_res[i], x_out[i]
                dve.wait_ge(moments_ready[0], half + 1)
                for t in range(TILES):
                    last = nc.vector.scalar_tensor_tensor(
                        out=X[:, t, :], in0=X[:, t, :], scalar=moments[:, 0, t, 0:1], in1=c.gamma[:],
                        op0=ALU.subtract, op1=ALU.mult)
                last.then_inc(dve_step, 1)
                dve.wait_ge(dve_step, 2 * half + 1)
                dve.wait_ge(rstd_ready[0], half + 1)
                dve.wait_ge(shifted, half + 1)
                for t in range(TILES):
                    last = nc.vector.scalar_tensor_tensor(
                        out=G[:, t, :], in0=X[:, t, :], scalar=rstd[:, 0, t:t + 1], in1=G[:, t, :],
                        op0=ALU.mult, op1=ALU.add)
                last.then_inc(dve_step, 1)
                dve.wait_ge(dve_step, 2 * half + 2)
                take_moments(half, 1, G)

            def second_norm(b, i):
                half = 2 * b + i
                G = x_out[i]
                dve.wait_ge(moments_ready[1], half + 1)
                dve.wait_ge(rstd_ready[1], half + 1)
                for t in range(TILES):
                    last = nc.vector.tensor_scalar(G[:, t, :], G[:, t, :], moments[:, 1, t, 0:1],
                                                   rstd[:, 1, t:t + 1], ALU.subtract, ALU.mult)
                last.then_inc(out_ready, 1)

            residual(0, 0)
            with dve.Fori(0, B - 1) as b:
                for i in range(2):
                    first_norm(b, i)
                    second_norm(b, i)
                    residual(b, i + 1)
            first_norm(B - 1, 0)
            second_norm(B - 1, 0)
            residual(B - 1, 1)
            first_norm(B - 1, 1)
            second_norm(B - 1, 1)


def prepare_layer1(nc, c, s, B, N):
    NT = N // P
    COLS = B * H * NT
    BLOCKS = COLS // P
    MM = 512
    with ExitStack() as ctx:
        sb, ps, sem = allocators(nc, ctx, "prepare1")
        edge = sb("edge_all", [P, B, NT, 2 * H], F32)
        highest = sb("highest", [P, B, H], F32)
        top = sb("top", [P, B, H], F32)
        src = sb("src", [P, B, H, NT], F32)
        d = sb("d", [P, B, H, NT], F32)
        total = sb("s_plus", [P, B, H, NT], F32)
        small = sb("s_small", [P, B, H, NT], F32)
        largest = sb("m", [P, B, H, NT], F32)
        exponents = sb("exponents", [P, 2, B, H, NT], F32)
        factors = sb("factors", [P, B, H, FACTORS, NT], F32)
        rows = sb("src_rows_sb", [P, BLOCKS, P], F32)
        ones = sb("ones16", [P, P], BF16)
        rows_ps = ps("rows_ps", [P, BLOCKS, P], F32)
        degree = ps("degree", [P, N], F32)
        loaded = sem("edge_loaded")
        highest_ready = sem("highest_ready")
        top_ready = sem("top_ready")
        src_ready = sem("src_ready")
        dve_step = sem("dve_step")
        exponents_ready = sem("exponents_ready")
        exp_ready = sem("exp_ready")
        negated = sem("negated")
        ones_ready = sem("ones_ready")
        degree_ready = sem("degree_ready")
        rows_ready = sem("rows_ready")
        rows_copied = sem("rows_copied")
        no_edge_ready = sem("no_edge_ready")
        stored = sem("stored")
        sp_held = sem("sp_held")
        block = ctx.enter_context(nc.Block())

        @block.sync
        def _(sp):
            sp.dma_start(edge[:].rearrange("p b t e -> p b (t e)"), s.e[:, :, :].rearrange("b p w -> p b w")
                         ).then_inc(loaded, DMA)
            hold(sp, rows_copied, 1, sp_held)
            width = min(P, COLS)
            sp.dma_start(s.src[:, :].rearrange("(k p) w -> p k w", p=width), rows[0:width]).then_inc(stored, DMA)
            hold(sp, negated, 1, sp_held)
            for b in range(B):
                sp.dma_start(s.factors[b].rearrange("h p w -> p h w"),
                             factors[:, b].rearrange("p h k t -> p h (k t)")).then_inc(stored, DMA)
            hold(sp, stored, (B + 1) * DMA, sp_held)

        @block.gpsimd
        def _(pool):
            nc.gpsimd.memset(ones[:], 1.0).then_inc(ones_ready, 1)
            pool.wait_ge(highest_ready, 1)
            nc.gpsimd.partition_all_reduce(top[:].rearrange("p b h -> p (b h)"),
                                           highest[:].rearrange("p b h -> p (b h)"), P, REDUCE_MAX
                                           ).then_inc(top_ready, 1)

        @block.tensor
        def _(pe):
            pe.wait_ge(ones_ready, 1)
            for j in range(NT):
                for q in range(N // MM):
                    mm = nc.tensor.matmul(degree[:, q * MM:(q + 1) * MM], ones[:],
                                          c.edge_mask[:, j, q * MM:(q + 1) * MM], start=j == 0, stop=j == NT - 1)
            mm.then_inc(degree_ready, 1)
            pe.wait_ge(src_ready, 1)
            for k in range(BLOCKS):
                mm = nc.tensor.transpose(rows_ps[:, k, :],
                                         src[:].rearrange("p b h t -> p (b h t)")[:, k * P:(k + 1) * P], c.ident[:])
            mm.then_inc(rows_ready, 1)

        @block.scalar
        def _(act):
            act.wait_ge(rows_ready, 1)
            nc.scalar.copy(rows[:], rows_ps[:]).then_inc(rows_copied, 1)
            act.wait_ge(exponents_ready, 1)
            for k, source, scale, bias in ((0, d[:], 1.0, c.source_bias[:]), (2, d[:], SLOPE, c.source_bias[:]),
                                           (TARGET, exponents[:, 0], 1.0, 0.0),
                                           (TARGET + 1, exponents[:, 1], 1.0, 0.0)):
                nc.scalar.activation(factors[:, :, :, k, :].rearrange("p b h t -> p (b h) t"),
                                     source.rearrange("p b h t -> p (b h) t"), ACT.Exp, bias=bias, scale=scale
                                     ).then_inc(exp_ready, 1)

        @block.vector
        def _(dve):
            dve.wait_ge(loaded, DMA)
            dst = edge[:, :, :, H:2 * H].rearrange("p b t h -> p b h t")
            for b in range(B):
                last = nc.vector.tensor_reduce(highest[:, b], dst[:, b], AXIS_FREE, ALU.max)
            last.then_inc(highest_ready, 1)
            for b in range(B):
                last = nc.vector.tensor_copy(src[:, b], edge[:, b, :, 0:H].rearrange("p t h -> p h t"))
            last.then_inc(src_ready, 1)
            for b in range(B):
                last = nc.vector.tensor_scalar(factors[:, b, :, STEEP_DST, :], dst[:, b], STEEP, None, ALU.mult)
            dve.wait_ge(top_ready, 1)
            dve.wait_ge(src_ready, 1)
            for b in range(B):
                at = top[:, b].unsqueeze(2).to_broadcast([P, H, NT])
                nc.vector.tensor_tensor(d[:, b], dst[:, b], at, ALU.subtract)
                last = nc.vector.tensor_tensor(total[:, b], src[:, b], at, ALU.add)
            last.then_inc(dve_step, 1)
            dve.wait_ge(dve_step, 1)
            nc.vector.tensor_scalar(small[:], total[:], SLOPE, None, ALU.mult).then_inc(dve_step, 1)
            dve.wait_ge(dve_step, 2)
            nc.vector.tensor_tensor(largest[:], total[:], small[:], ALU.max).then_inc(dve_step, 1)
            dve.wait_ge(dve_step, 3)
            nc.vector.tensor_tensor(exponents[:, 0], total[:], largest[:], ALU.subtract)
            nc.vector.tensor_tensor(exponents[:, 1], small[:], largest[:], ALU.subtract).then_inc(exponents_ready, 1)
            dve.wait_ge(exp_ready, 4)
            nc.vector.tensor_scalar(factors[:, :, :, 1, :].rearrange("p b h t -> p (b h) t"),
                                    factors[:, :, :, 2, :].rearrange("p b h t -> p (b h) t"), -1.0, None, ALU.mult
                                    ).then_inc(negated, 1)
            dve.wait_ge(degree_ready, 1)
            nc.vector.tensor_scalar(c.no_edge[:], degree[:], 0.0, None, ALU.is_equal).then_inc(no_edge_ready, 1)
            dve.wait_ge(no_edge_ready, 1)


def attend_layer1(nc, c, s, out, B, N):
    NT = N // P
    TH = NT // 2
    W = N // 2
    GROUPS = 2 * H
    BODY_UNITS = GROUPS * NT
    R_RING, G_RING = 4, 8
    R_AHEAD = 2
    BANK_T = 3
    BANKS = -(-TH // BANK_T)
    FORMED = [u % NT % 2 == 0 for u in range(BODY_UNITS)]
    N_RING = sum(FORMED[:G_RING])
    SCALE_AT, ADD_AT, INVERT_AT, DIVIDE_AT = 5, 6, 7, 8
    assert BODY_UNITS % G_RING == 0 and NT % 8 == 0 and B > 2
    with ExitStack() as ctx:
        sb, ps, sem = allocators(nc, ctx, "attend1")
        src_row = [sb(f"src_row{i}", [P, N], F32) for i in range(2)]
        factors = [sb(f"factors{i}", [P, FACTORS, NT], F32) for i in range(2)]
        values = [sb(f"values{i}", [P, NT, DV], F32) for i in range(2)]
        product = sb("product", [P, NT, DV], F32)
        high = [sb(f"high{i}", [P, NT, 3, DV], BF16) for i in range(2)]
        low = [sb(f"low{i}", [P, NT, 3, DV], F16) for i in range(2)]
        total = sb("total", [P, NT // 2, DV], F32)
        total_high = [sb(f"total_high{i}", [P, DV], BF16) for i in range(2)]
        total_low = [sb(f"total_low{i}", [P, DV], F16) for i in range(2)]
        steep = [sb(f"steep{i}", [P, W], BF16) for i in range(R_RING)]
        positive = [sb(f"positive{i}", [P, W], BF16) for i in range(G_RING)]
        negative = [sb(f"negative{i}", [P, W], BF16) for i in range(N_RING)]
        scaled = [sb(f"scaled{i}", [P, TH, 2, DV], F32) for i in range(2)]
        inverse = sb("inverse", [P, TH], F32)
        hidden = sb("hidden", [P, NT, F], F32)
        x1 = sb("x1", [P, TH, F], F32)
        work = sb("work", [P, TH, F], F32)
        stats = sb("stats", [P, TH, 6], F32)
        moments = sb("moments", [P, TH, 2], F32)
        var_eps = sb("var_eps", [P, TH], F32)
        rstd = sb("rstd", [P, TH], F32)
        shift = sb("shift", [P, TH], F32)
        acc = [[ps(f"acc{i}_{k}", [P, BANK_T, 2, DV], F32) for k in range(BANKS)] for i in range(2)]

        loaded = [sem(f"head_loaded{i}") for i in range(2)]
        x1_loaded = sem("x1_loaded")
        pool_step = sem("pool_step")
        total_part = sem("total_part")
        split_ready = sem("split_ready")
        steep_ready = sem("steep_ready")
        positive_ready = sem("positive_ready")
        negative_ready = sem("negative_ready")
        matrices_free = sem("matrices_free")
        group_summed = sem("group_summed")
        sums_scaled = sem("sums_scaled")
        group_added = sem("group_added")
        inverse_ready = sem("inverse_ready")
        group_ready = sem("group_ready")
        shifted = sem("shifted")
        exp_ready = sem("exp_ready")
        dve_step = sem("dve_step")
        moments_ready = sem("moments_ready")
        variance_ready = sem("variance_ready")
        held = sem("held")
        rstd_ready = sem("rstd_ready")
        shift_ready = sem("shift_ready")
        normed = sem("normed")
        stored = sem("out_stored")
        sp_held = sem("sp_held")
        block = ctx.enter_context(nc.Block())

        def wrapped(b, u):
            return (b + 1, u - BODY_UNITS) if u >= BODY_UNITS else (b, u)

        def place(u):
            return u // (2 * NT), u // NT % 2, u % NT

        def formed_before(u):
            return sum(FORMED[:u])

        def bank_tiles(k):
            return slice(k * BANK_T, min((k + 1) * BANK_T, TH))

        @block.sync
        def _(sp):
            def load_head(b, h):
                i = h % 2
                head = H * b + h
                bb, hh = (b, h) if h < H else (b + 1, h - H)
                if not (isinstance(head, int) and head < 2):
                    hold(sp, steep_ready, 2 * NT * (head - 1), sp_held)
                    hold(sp, split_ready, head - 1, sp_held)
                    hold(sp, sums_scaled, 2 + 2 * (head - 1), sp_held)
                at = s.src[bass.ds(head * NT, NT), :].rearrange("t p -> (t p)").partition_broadcast(P)
                sp.dma_start(src_row[i][:], at).then_inc(loaded[i], DMA)
                at = s.factors[bass.ds(bb, 1), hh].rearrange("o p w -> (o p) w")
                sp.dma_start(factors[i][:].rearrange("p k t -> p (k t)"), at).then_inc(loaded[i], DMA)
                at = s.v1[bass.ds(bb, 1), hh].rearrange("o p w -> (o p) w")
                sp.dma_start(values[i][:].rearrange("p t d -> p (t d)"), at).then_inc(loaded[i], DMA)

            def half_of(t, b, k):
                return t[bass.ds(b, 1), k * TH * P:(k + 1) * TH * P, :].rearrange("o (t p) f -> p (o t) f", p=P)

            def load_x1(b, k):
                sp.dma_start(x1[:], half_of(s.x1, b, k)).then_inc(x1_loaded, DMA)

            def finish_batch(b, last):
                for k in range(2):
                    hold(sp, moments_ready, 2 * b + k + 1, sp_held)
                    if k == 0:
                        load_x1(b, 1)
                    elif not last:
                        load_x1(b + 1, 0)
                    hold(sp, normed, 2 * b + k + 1, sp_held)
                    sp.dma_start(half_of(out, b, k), work[:]).then_inc(stored, DMA)

            sp.sem_inc(stored, DMA)
            load_head(0, 0)
            load_x1(0, 0)
            for h in range(H):
                load_head(0, h + 1)
            with sp.Fori(1, B - 1) as b:
                load_head(b, 1)
                finish_batch(b - 1, last=False)
                for h in range(1, H):
                    load_head(b, h + 1)
            load_head(B - 1, 1)
            finish_batch(B - 2, last=False)
            for h in range(1, H - 1):
                load_head(B - 1, h + 1)
            finish_batch(B - 1, last=True)
            hold(sp, stored, DMA * (2 * B + 1), sp_held)

        @block.gpsimd
        def _(pool):
            LEVELS = (NT // 2).bit_length()
            STEPS = 9 + LEVELS

            def head_steps(b, h):
                i = h % 2
                head = H * b + h
                v = values[i]

                def split_one(k):
                    step = STEPS * head + 3 * k
                    if k == 0:
                        pool.wait_ge(loaded[i], 3 * DMA * (H // 2 * b + h // 2 + 1))
                        if not (isinstance(head, int) and head < 2):
                            pool.wait_ge(sums_scaled, 2 + 2 * (head - 1))
                    factor = factors[i][:, k, :].unsqueeze(2).to_broadcast([P, NT, DV])
                    nc.gpsimd.tensor_tensor(high[i][:, :, k], v[:], factor, ALU.mult).then_inc(pool_step, 1)
                    if not (isinstance(step, int) and step == 0):
                        pool.wait_ge(pool_step, step)
                    nc.gpsimd.tensor_tensor(product[:], v[:], factor, ALU.mult).then_inc(pool_step, 1)
                    pool.wait_ge(pool_step, step + 2)
                    nc.gpsimd.tensor_tensor(low[i][:, :, k], product[:], high[i][:, :, k], ALU.subtract
                                            ).then_inc(pool_step, 1)

                def add_all():
                    width = NT // 2
                    nc.gpsimd.tensor_tensor(total[:, 0:width], v[:, 0:width, :], v[:, width:2 * width, :],
                                            ALU.add).then_inc(pool_step, 1)
                    for level in range(1, LEVELS):
                        width //= 2
                        pool.wait_ge(pool_step, STEPS * head + 9 + level)
                        nc.gpsimd.tensor_tensor(total[:, 0:width], total[:, 0:width], total[:, width:2 * width],
                                                ALU.add).then_inc(pool_step, 1)
                    hold(pool, pool_step, STEPS * (head + 1), held)
                    nc.gpsimd.tensor_copy(total_high[i][:], total[:, 0]).then_inc(total_part, 1)
                    pool.wait_ge(total_part, head + 1)
                    nc.gpsimd.tensor_tensor(total_low[i][:], total[:, 0], total_high[i][:], ALU.subtract
                                            ).then_inc(split_ready, 1)

                return [lambda k=k: split_one(k) for k in range(3)] + [add_all]

            def take_rstd(b, k):
                pool.wait_ge(moments_ready, 2 * b + k + 1)
                nc.gpsimd.tensor_tensor(var_eps[:], moments[:, :, 1], c.eps[:, 0:TH], ALU.add
                                        ).then_inc(variance_ready, 1)
                pool.wait_ge(variance_ready, 2 * b + k + 1)
                nc.gpsimd.tensor_tensor(rstd[:], var_eps[:], c.minus_half[:, 0:TH], ALU.pow).then_inc(rstd_ready, 1)

            def shift_x1(b, k):
                pool.wait_ge(x1_loaded, DMA * (2 * b + k + 1))
                nc.gpsimd.tensor_tensor(x1[:], x1[:], c.minus_one[:].unsqueeze(2).to_broadcast([P, TH, F]), ALU.add
                                        ).then_inc(shifted, 1)

            shift_x1(0, 0)
            for h in range(H):
                for step in head_steps(0, h):
                    step()
            with pool.Fori(1, B) as b:
                for h in range(H):
                    steps = head_steps(b, h)
                    for step in steps[:2]:
                        step()
                    if h == 1:
                        take_rstd(b - 1, 0)
                    for step in steps[2:]:
                        step()
                    if h == 1:
                        shift_x1(b - 1, 1)
                        take_rstd(b - 1, 1)
                        shift_x1(b, 0)
            take_rstd(B - 1, 0)
            shift_x1(B - 1, 1)
            take_rstd(B - 1, 1)

        @block.tensor
        def _(pe):
            def unit(b, u):
                h, half, j = place(u)
                if j == 0:
                    if half == 0:
                        pe.wait_ge(split_ready, H * b + h + 1)
                    pe.wait_ge(sums_scaled, GROUPS * b + 2 * h + half + 1)
                if FORMED[u]:
                    pe.wait_ge(negative_ready, formed_before(BODY_UNITS) * b + formed_before(u + 1))
                else:
                    pe.wait_ge(positive_ready, BODY_UNITS * b + u + 1)
                parts = (high[h % 2], low[h % 2])
                for t in range(TH):
                    to = acc[half][t // BANK_T][:, t % BANK_T].rearrange("p s d -> p (s d)")
                    cols = slice(t * P, (t + 1) * P)
                    edges = c.edge_mask[:, j, half * W + t * P:half * W + (t + 1) * P]
                    first = j == 0 and t % BANK_T == 0
                    if FORMED[u]:
                        products = [(to[:, 0:DV], positive[u % G_RING][:, cols], 0, 1),
                                    (to[:, DV:2 * DV], negative[formed_before(u) % N_RING][:, cols], 2, 3)]
                    else:
                        products = [(to[:, 0:2 * DV], positive[u % G_RING][:, cols], 0, 2),
                                    (to[:, DV:2 * DV], edges, 2, 3)]
                    for dst, matrix, start, stop in products:
                        for part in parts:
                            mm = nc.tensor.matmul(dst, matrix,
                                                  part[:, j, start:stop, :].rearrange("p k d -> p (k d)"),
                                                  start=first, stop=False, skip_group_check=True)
                            first = False
                mm.then_inc(matrices_free, 1)
                if j == NT - 1:
                    for t in range(TH):
                        tile = (half * TH + t) * P
                        for sign in range(2):
                            to = acc[half][t // BANK_T][:, t % BANK_T, sign]
                            for part, total_part in enumerate((total_high, total_low)):
                                mm = nc.tensor.matmul(to, c.no_edge[:, tile:tile + P], total_part[h % 2][:],
                                                      start=False, skip_group_check=True,
                                                      stop=part == 1 and sign == 1 and (t + 1) % BANK_T == 0)
                    mm.then_inc(group_summed, 1)

            pe.sem_inc(matrices_free, G_RING)
            with pe.Fori(0, B) as b:
                for u in range(BODY_UNITS):
                    unit(b, u)

        EXP_AT = (DIVIDE_AT + 1, NT + DIVIDE_AT + 2)
        RESIDUAL_AT = tuple(u + 3 for u in EXP_AT)
        NORM_AT = tuple(u + 13 for u in EXP_AT)

        @block.scalar
        def _(act):
            def unit(b, u):
                h, half, j = place(u)
                if half == 0 and j == 0:
                    act.wait_ge(loaded[h % 2], 3 * DMA * (H // 2 * b + h // 2 + 1))
                if not (isinstance(b, int) and b == 0 and u < R_RING):
                    act.wait_ge(positive_ready, BODY_UNITS * b + u - R_RING + 1)
                nc.scalar.activation(steep[u % R_RING][:], src_row[h % 2][:, half * W:(half + 1) * W], ACT.Relu,
                                     bias=factors[h % 2][:, STEEP_DST, j:j + 1], scale=STEEP
                                     ).then_inc(steep_ready, 1)

            def exponential(b, k):
                act.wait_ge(group_ready, GROUPS * (b + 1) - 1 + k)
                act.wait_ge(stored, DMA * (2 * b + k + 1))
                nc.scalar.activation(work[:], hidden[:, k * TH:(k + 1) * TH], ACT.Exp).then_inc(exp_ready, 1)

            def norm(b, k):
                act.wait_ge(shift_ready, 2 * b + k + 1)
                for t in range(TH):
                    last = nc.scalar.activation(work[:, t, :], hidden[:, k * TH + t, :], ACT.Identity,
                                                bias=shift[:, t:t + 1], scale=rstd[:, t:t + 1])
                last.then_inc(normed, 1)

            def batch(b, first=False):
                for u in range(BODY_UNITS):
                    unit(b, u)
                    if u in EXP_AT and not first:
                        exponential(b - 1, EXP_AT.index(u))
                    if u in NORM_AT and not first:
                        norm(b - 1, NORM_AT.index(u))

            batch(0, first=True)
            with act.Fori(1, B) as b:
                batch(b)
            for k in range(2):
                exponential(B - 1, k)
                norm(B - 1, k)

        @block.vector
        def _(dve):
            def take_positive(b, u):
                h, half, j = place(u)
                dve.wait_ge(steep_ready, BODY_UNITS * b + u + 1)
                dve.wait_ge(matrices_free, BODY_UNITS * b + u + 1)
                edges = c.edge_mask[:, j, half * W:(half + 1) * W]
                nc.vector.tensor_tensor(positive[u % G_RING][:], steep[u % R_RING][:], edges, ALU.min
                                        ).then_inc(positive_ready, 1)

            def take_negative(b, u):
                if not FORMED[u]:
                    return
                h, half, j = place(u)
                edges = c.edge_mask[:, j, half * W:(half + 1) * W]
                dve.wait_ge(positive_ready, BODY_UNITS * b + u + 1)
                nc.vector.tensor_tensor(negative[formed_before(u) % N_RING][:], edges, positive[u % G_RING][:],
                                        ALU.subtract).then_inc(negative_ready, 1)

            def scale_sums(b, g):
                h, i = g // 2, g % 2
                count = GROUPS * b + g
                dve.wait_ge(group_summed, count + 1)
                if not (isinstance(count, int) and count < 2):
                    dve.wait_ge(group_ready, count - 1)
                factor = factors[h % 2][:, TARGET:TARGET + 2, i * TH:(i + 1) * TH].rearrange("p s t -> p t s")
                for k in range(BANKS):
                    tiles = bank_tiles(k)
                    count = tiles.stop - tiles.start
                    last = nc.vector.tensor_tensor(
                        scaled[i][:, tiles], acc[i][k][:, 0:count],
                        factor[:, tiles].unsqueeze(3).to_broadcast([P, count, 2, DV]), ALU.mult)
                last.then_inc(sums_scaled, 1)

            def add_sums(b, g):
                i = g % 2
                dve.wait_ge(sums_scaled, 2 + GROUPS * b + g + 1)
                nc.vector.tensor_tensor(scaled[i][:, :, 0], scaled[i][:, :, 0], scaled[i][:, :, 1], ALU.add
                                        ).then_inc(group_added, 1)

            def invert(b, g):
                count = GROUPS * b + g
                dve.wait_ge(group_added, count + 1)
                if not (isinstance(count, int) and count == 0):
                    dve.wait_ge(group_ready, count)
                nc.vector.reciprocal(inverse[:], scaled[g % 2][:, :, 0, DH]).then_inc(inverse_ready, 1)

            def divide_sums(b, g):
                h, i = g // 2, g % 2
                if h == 0 and not (isinstance(b, int) and b == 0):
                    dve.wait_ge(normed, 2 * b - 1 + i)
                dve.wait_ge(inverse_ready, GROUPS * b + g + 1)
                nc.vector.tensor_tensor(hidden[:, i * TH:(i + 1) * TH, h * DH:(h + 1) * DH], scaled[i][:, :, 0, 0:DH],
                                        inverse[:].unsqueeze(2).to_broadcast([P, TH, DH]), ALU.mult
                                        ).then_inc(group_ready, 1)

            GROUP_STEPS = {SCALE_AT: scale_sums, ADD_AT: add_sums, INVERT_AT: invert, DIVIDE_AT: divide_sums}

            def residual_steps(b, k):
                step = 3 * (2 * b + k)
                part = hidden[:, k * TH:(k + 1) * TH]

                def add_x1():
                    dve.wait_ge(exp_ready, 2 * b + k + 1)
                    dve.wait_ge(shifted, 2 * b + k + 1)
                    nc.vector.scalar_tensor_tensor(out=work[:], in0=work[:], scalar=1.0, in1=x1[:], op0=ALU.min,
                                                   op1=ALU.add).then_inc(dve_step, 1)

                def add_positive():
                    dve.wait_ge(dve_step, step + 1)
                    nc.vector.scalar_tensor_tensor(out=part, in0=part, scalar=0.0, in1=work[:], op0=ALU.max,
                                                   op1=ALU.add).then_inc(dve_step, 1)

                def take_stats():
                    dve.wait_ge(dve_step, step + 2)
                    for t in range(TH):
                        last = nc.vector.bn_stats(stats[:, t, :], hidden[:, k * TH + t, :])
                    last.then_inc(dve_step, 1)

                def take_moments():
                    hold(dve, dve_step, step + 3, held)
                    for t in range(TH):
                        last = nc.vector.bn_aggr(moments[:, t, :], stats[:, t, :])
                    last.then_inc(moments_ready, 1)

                def take_shift():
                    dve.wait_ge(rstd_ready, 2 * b + k + 1)
                    nc.vector.scalar_tensor_tensor(out=shift[:], in0=moments[:, :, 0], scalar=-1.0, in1=rstd[:],
                                                   op0=ALU.mult, op1=ALU.mult).then_inc(shift_ready, 1)

                return [add_x1, add_positive, take_stats, take_moments, take_shift]

            RESIDUAL_STEP = {at + offset: (k, n) for k, at in enumerate(RESIDUAL_AT)
                             for n, offset in enumerate((0, 2, 4, 5, 7))}

            def batch(b, first=False, last=False):
                for u in range(BODY_UNITS):
                    if not (last and u + R_AHEAD >= BODY_UNITS):
                        take_positive(*wrapped(b, u + R_AHEAD))
                    take_negative(b, u)
                    j = u % NT
                    g = u // NT - 1
                    if g >= 0 or not first:
                        at = (b, g) if g >= 0 else (b - 1, GROUPS - 1)
                        if j in GROUP_STEPS:
                            GROUP_STEPS[j](*at)
                    if u in RESIDUAL_STEP and not first:
                        k, n = RESIDUAL_STEP[u]
                        residual_steps(b - 1, k)[n]()

            dve.sem_inc(sums_scaled, 2)
            for u in range(R_AHEAD):
                take_positive(0, u)
            batch(0, first=True)
            with dve.Fori(1, B - 1) as b:
                batch(b)
            batch(B - 1, last=True)
            for step in GROUP_STEPS.values():
                step(B - 1, GROUPS - 1)
            for k in range(2):
                for step in residual_steps(B - 1, k):
                    step()


def program(nc, x, adj, weights, out):
    B, N, _ = x.shape
    s = Scratch(nc, B, N)
    with ExitStack() as ctx:
        c = Constants(nc, ctx)
        with ExitStack() as layer0:
            c.for_layer0(nc, layer0, N)
            prepare_weights(nc, c, weights)
            project_layer0(nc, c, s, x, adj, B, N)
            attend_layer0(nc, c, s, B, N)
        c.for_layer1(nc, ctx, N)
        finish_layer0(nc, c, s, x, B, N)
        prepare_layer1(nc, c, s, B, N)
        attend_layer1(nc, c, s, out, B, N)


_WEIGHTS = {"Wq": "L0_gnn_Wq", "bq": "L0_gnn_bq", "Wk": "L0_gnn_Wk", "bk": "L0_gnn_bk", "Wv": "L0_gnn_Wv",
            "bv": "L0_gnn_bv", "Wo": "L0_gnn_Wo", "bo": "L0_gnn_bo", "gamma": "L0_gnn_gamma",
            "beta": "L0_gnn_beta", "W": "L1_gnn_W", "a": "L1_gnn_a"}


def kernel(**inputs):
    import numpy as np
    from concourse import bacc
    from concourse.bass_utils import run_bass_kernel_spmd

    nc = bacc.Bacc("TRN2", target_bir_lowering=False, num_devices=1)
    arrays, aps = {}, {}
    for name in ("x", "adj", *_WEIGHTS.values()):
        a = np.ascontiguousarray(inputs[name])
        arrays[f"in_{name}"] = a
        aps[name] = nc.dram_tensor(f"in_{name}", a.shape, mybir.dt.from_np(a.dtype), kind="ExternalInput").ap()
    out = nc.dram_tensor("out", aps["x"].shape, F32, kind="ExternalOutput").ap()
    program(nc, aps["x"], aps["adj"], {short: aps[name] for short, name in _WEIGHTS.items()}, out)
    r = run_bass_kernel_spmd(nc, [arrays], core_ids=[0])
    return r.results[0]["out"]
```
